# Optimizing a Trainium2 kernel written in Bass

```python
import numpy as np
import jax
import jax.numpy as jnp

def _softmax(x, axis=-1):
    return jax.nn.softmax(x, axis=axis)

def _gelu(x):
    return jax.nn.gelu(x, approximate=True)

def _silu(x):
    return jax.nn.silu(x)

def _sigmoid(x):
    return jax.nn.sigmoid(x)

def _layernorm(x, axis=-1, eps=1e-05):
    m = jnp.mean(x, axis=axis, keepdims=True)
    v = jnp.var(x, axis=axis, keepdims=True)
    return (x - m) / jnp.sqrt(v + eps)

def _scatter_add(tgt, idx, src, axis=0):
    return tgt.at[idx].add(src)

def _segment_sum(src, seg, n):
    return jax.ops.segment_sum(src, seg, n)
kernel_name = 'mk_perceiver_d2_seqx_r8_c26188'

def setup_inputs(seed: int=0):
    np.random.seed(seed)
    _w = jnp.asarray

    def _rec_inputs():
        import jax
        import jax.numpy as jnp
        _rk = jax.random.key(seed)
        x = -0.0003929 + 0.9999 * jax.random.normal(jax.random.fold_in(_rk, 1), (1, 64, 128), jnp.float32)
        _lenS = 64 - jax.random.randint(jax.random.fold_in(_rk, 7), (1,), 0, max(1, 64 // 4) + 1, jnp.int32)
        _lenS2 = 6272 - jax.random.randint(jax.random.fold_in(_rk, 8), (1,), 0, max(1, 6272 // 4) + 1, jnp.int32)
        _ctx_1024P = jax.random.normal(jax.random.fold_in(_rk, 11), (1, 16, 128), jnp.float32)
        _ctx_1024c = jax.random.dirichlet(jax.random.fold_in(_rk, 511), 0.3 * jnp.ones((16,), jnp.float32), (1, 6272))
        _ctx_1024t = jnp.einsum('bsk,bkd->bsd', _ctx_1024c, _ctx_1024P)
        _ctx_1024t = _ctx_1024t * jax.lax.rsqrt(jnp.mean(jnp.square(_ctx_1024t)) + 1e-12) * 0.953939
        ctx_1024 = 0.00208318 + 0.999174 * (_ctx_1024t + 0.3 * jax.random.normal(jax.random.fold_in(_rk, 611), (1, 6272, 128), jnp.float32))
        _validS = jnp.arange(64)[None, :] < _lenS[:, None]
        _validS2 = jnp.arange(6272)[None, :] < _lenS2[:, None]
        _causal = jnp.tril(jnp.ones((64, 64), dtype=bool))
        mask_BxSxS2_ff0 = jnp.where(jnp.ones((1, 64, 6272), dtype=bool), 0.0, -1000000000.0).astype(jnp.float32)
        mask_SxS2_bk1 = jnp.broadcast_to(_validS2[0:1, :], (64, 6272))
        return (x, ctx_1024, mask_BxSxS2_ff0, mask_SxS2_bk1)
    x, ctx_1024, mask_BxSxS2_ff0, mask_SxS2_bk1 = _rec_inputs()

    def _L0_xattn_setup():
        import jax, jax.numpy as jnp
        import numpy as np
        NUM_HEADS = 16
        DIM = 128
        key = jax.random.key(seed)
        ks = jax.random.split(key, 12)
        B, N, T, C = (4, 512, 77, DIM)
        s = 1.0 / np.sqrt(C)
        return {'hidden_states': jax.random.normal(ks[0], (B, N, C), jnp.float32), 'encoder_hidden_states': jax.random.normal(ks[1], (B, T, C), jnp.float32), 'attention_mask': jnp.zeros((B, N, T), jnp.float32), 'Wq': jax.random.normal(ks[2], (C, C), jnp.float32) * s, 'bq': jnp.zeros((C,), jnp.float32), 'Wk': jax.random.normal(ks[3], (C, C), jnp.float32) * s, 'bk': jnp.zeros((C,), jnp.float32), 'Wv': jax.random.normal(ks[4], (C, C), jnp.float32) * s, 'bv': jnp.zeros((C,), jnp.float32), 'Wo': jax.random.normal(ks[5], (C, C), jnp.float32) * s, 'bo': jnp.zeros((C,), jnp.float32)}
    _L0_xattn_all = _L0_xattn_setup()
    _L0_xattn_in = {k: v for k, v in _L0_xattn_all.items() if k in ('Wq', 'bq', 'Wk', 'bk', 'Wv', 'bv', 'Wo', 'bo')}
    del _L0_xattn_all

    def _L0_attn_setup():
        import jax, jax.numpy as jnp
        import numpy as np
        import math
        B, T, D = (2, 256, 128)
        N_HEADS = 16
        D_HEAD = D // N_HEADS

        def _rope_tables(t, d_head, dtype=jnp.float32):
            theta = 1.0 / 10000.0 ** (jnp.arange(0, d_head, 2, dtype=jnp.float32) / d_head)
            angles = jnp.outer(jnp.arange(t, dtype=jnp.float32), theta)
            angles = jnp.concatenate([angles, angles], axis=-1)
            return (jnp.cos(angles).astype(dtype), jnp.sin(angles).astype(dtype))

        def _rotate_half(x):
            half = x.shape[-1] // 2
            return jnp.concatenate([-x[..., half:], x[..., :half]], axis=-1)

        def _apply_rope(x, cos, sin):
            return x * cos[None, None] + _rotate_half(x) * sin[None, None]
        key = jax.random.key(seed)
        k1, k2, k3, k4 = jax.random.split(key, 4)
        s_in = 1.0 / math.sqrt(D)
        return {'x': jax.random.normal(k1, (B, T, D), dtype=jnp.float32), 'w_qkv': jax.random.normal(k2, (D, 3 * D), dtype=jnp.float32) * s_in, 'w_out': jax.random.normal(k3, (D, D), dtype=jnp.float32) * s_in, 'b_out': jax.random.normal(k4, (D,), dtype=jnp.float32) * 0.01}
    _L0_attn_all = _L0_attn_setup()
    _L0_attn_in = {k: v for k, v in _L0_attn_all.items() if k in ('w_qkv', 'w_out', 'b_out')}
    del _L0_attn_all

    def _L0_ffn_setup():
        import jax, jax.numpy as jnp
        import numpy as np
        IN_F, OUT_F, BLOCK, NBLK = (128, 512, 32, 16)
        TOPK = NBLK // 4
        key = jax.random.key(seed)
        ks = jax.random.split(key, 7)
        s = 1.0 / np.sqrt(IN_F)
        s2 = 1.0 / np.sqrt(OUT_F)
        return {'x': jax.random.normal(ks[0], (4, 512, IN_F), jnp.float32), 'router_w': jax.random.uniform(ks[1], (NBLK, IN_F), jnp.float32, -s, s), 'router_b': jax.random.uniform(ks[2], (NBLK,), jnp.float32, -s, s), 'w1': jax.random.uniform(ks[3], (OUT_F, IN_F), jnp.float32, -s, s), 'b1': jax.random.uniform(ks[4], (OUT_F,), jnp.float32, -s, s), 'w2': jax.random.uniform(ks[5], (IN_F, OUT_F), jnp.float32, -s2, s2), 'b2': jax.random.uniform(ks[6], (IN_F,), jnp.float32, -s2, s2)}
    _L0_ffn_all = _L0_ffn_setup()
    _L0_ffn_in = {k: v for k, v in _L0_ffn_all.items() if k in ('router_w', 'router_b', 'w1', 'b1', 'w2', 'b2')}
    del _L0_ffn_all

    def _L1_xattn_setup():
        import jax, jax.numpy as jnp
        import numpy as np
        D_MODEL = 128
        NHEAD = 16
        HEAD_DIM = D_MODEL // NHEAD
        B, SQ, SK = (2, 256, 256)
        key = jax.random.key(seed)
        ks = jax.random.split(key, 12)
        s = 0.02
        inp = {'q': jax.random.normal(ks[0], (B, SQ, D_MODEL), jnp.float32), 'k': jax.random.normal(ks[1], (B, SK, D_MODEL), jnp.float32), 'v': jax.random.normal(ks[2], (B, SK, D_MODEL), jnp.float32), 'causal_mask': jnp.triu(jnp.ones((SQ, SK), jnp.bool_), k=1), 'Wq': jax.random.normal(ks[3], (D_MODEL, D_MODEL), jnp.float32) * s, 'bq': jnp.zeros((D_MODEL,), jnp.float32), 'Wk': jax.random.normal(ks[4], (D_MODEL, D_MODEL), jnp.float32) * s, 'bk': jnp.zeros((D_MODEL,), jnp.float32), 'Wv': jax.random.normal(ks[5], (D_MODEL, D_MODEL), jnp.float32) * s, 'bv': jnp.zeros((D_MODEL,), jnp.float32), 'Wo': jax.random.normal(ks[6], (D_MODEL, D_MODEL), jnp.float32) * s, 'bo': jnp.zeros((D_MODEL,), jnp.float32)}
        return inp
    _L1_xattn_all = _L1_xattn_setup()
    _L1_xattn_in = {k: v for k, v in _L1_xattn_all.items() if k in ('Wq', 'bq', 'Wk', 'bk', 'Wv', 'bv', 'Wo', 'bo')}
    del _L1_xattn_all

    def _L1_attn_setup():
        import jax, jax.numpy as jnp
        import numpy as np
        B, T, C, H = (2, 256, 128, 16)
        D = C // H
        RW, RA, RG = (64, 64, 128)
        EPS = 1e-05

        def _rwkv7_scan(r, log_w, k, v, a, b):
            Bn, Tn, Hn, Dn = r.shape

            def step(S, xs):
                r_t, w_t, k_t, v_t, a_t, b_t = xs
                sa = jnp.einsum('bhij,bhj->bhi', S, a_t)
                S = S * jnp.exp(w_t)[:, :, None, :] + sa[..., None] * b_t[:, :, None, :] + v_t[..., None] * k_t[:, :, None, :]
                o_t = jnp.einsum('bhij,bhj->bhi', S, r_t)
                return (S, o_t)
            S0 = jnp.zeros((Bn, Hn, Dn, Dn), r.dtype)
            xs = tuple((jnp.swapaxes(x, 0, 1) for x in (r, log_w, k, v, a, b)))
            _, o = jax.lax.scan(step, S0, xs)
            return jnp.swapaxes(o, 0, 1)
        key = jax.random.key(seed)
        ks = iter(jax.random.split(key, 40))
        n = lambda s, sc=0.02: jax.random.normal(next(ks), s, jnp.float32) * sc
        u = lambda s: jax.random.uniform(next(ks), s, jnp.float32)
        return dict(hidden_states=jax.random.normal(next(ks), (B, T, C), jnp.float32), x_r=u((C,)), x_w=u((C,)), x_k=u((C,)), x_v=u((C,)), x_a=u((C,)), x_g=u((C,)), k_k=u((C,)), k_a=u((C,)), r_k=n((H, D), 0.1), W_r=n((C, C)), W_k=n((C, C)), W_v=n((C, C)), W_o=n((C, C)), w_lora_a=n((C, RW)), w_lora_b=n((RW, C)), w_lora_bias=n((C,), 0.1), a_lora_a=n((C, RA)), a_lora_b=n((RA, C)), a_lora_bias=jnp.zeros((C,), jnp.float32), g_lora_a=n((C, RG)), g_lora_b=n((RG, C)), g_lora_bias=jnp.zeros((C,), jnp.float32), gn_weight=jnp.ones((C,), jnp.float32), gn_bias=jnp.zeros((C,), jnp.float32))
    _L1_attn_all = _L1_attn_setup()
    _L1_attn_in = {k: v for k, v in _L1_attn_all.items() if k in ('x_r', 'x_w', 'x_k', 'x_v', 'x_a', 'x_g', 'k_k', 'k_a', 'r_k', 'W_r', 'W_k', 'W_v', 'W_o', 'w_lora_a', 'w_lora_b', 'w_lora_bias', 'a_lora_a', 'a_lora_b', 'a_lora_bias', 'g_lora_a', 'g_lora_b', 'g_lora_bias', 'gn_weight', 'gn_bias')}
    del _L1_attn_all

    def _L1_ffn_setup():
        import jax, jax.numpy as jnp
        import numpy as np
        HIDDEN = 128
        INNER = 512

        def _weight_quant(w):
            scale = 1.0 / jnp.clip(jnp.mean(jnp.abs(w)), 1e-05)
            wq = jnp.clip(jnp.round(w * scale), -1.0, 1.0) / scale
            return w + jax.lax.stop_gradient(wq - w)

        def _act_quant(x):
            scale = 127.0 / jnp.clip(jnp.max(jnp.abs(x), axis=-1, keepdims=True), 1e-05)
            xq = jnp.clip(jnp.round(x * scale), -128.0, 127.0) / scale
            return x + jax.lax.stop_gradient(xq - x)

        def _bitlinear(x, w):
            return jnp.einsum('bsi,oi->bso', _act_quant(x), _weight_quant(w))
        key = jax.random.key(seed)
        k0, k1, k2, k3 = jax.random.split(key, 4)
        x = jax.random.normal(k0, (4, 256, HIDDEN), dtype=jnp.float32)
        w_gate = jax.random.normal(k1, (INNER, HIDDEN), dtype=jnp.float32) / np.sqrt(HIDDEN)
        w_up = jax.random.normal(k2, (INNER, HIDDEN), dtype=jnp.float32) / np.sqrt(HIDDEN)
        w_down = jax.random.normal(k3, (HIDDEN, INNER), dtype=jnp.float32) / np.sqrt(INNER)
        return {'x': x, 'w_gate': w_gate, 'w_up': w_up, 'w_down': w_down}
    _L1_ffn_all = _L1_ffn_setup()
    _L1_ffn_in = {k: v for k, v in _L1_ffn_all.items() if k in ('w_gate', 'w_up', 'w_down')}
    del _L1_ffn_all
    return {'x': x, 'ctx_1024': ctx_1024, 'mask_BxSxS2_ff0': mask_BxSxS2_ff0, 'mask_SxS2_bk1': mask_SxS2_bk1, 'L0_xattn_Wq': _L0_xattn_in['Wq'], 'L0_xattn_bq': _L0_xattn_in['bq'], 'L0_xattn_Wk': _L0_xattn_in['Wk'], 'L0_xattn_bk': _L0_xattn_in['bk'], 'L0_xattn_Wv': _L0_xattn_in['Wv'], 'L0_xattn_bv': _L0_xattn_in['bv'], 'L0_xattn_Wo': _L0_xattn_in['Wo'], 'L0_xattn_bo': _L0_xattn_in['bo'], 'L0_attn_w_qkv': _L0_attn_in['w_qkv'], 'L0_attn_w_out': _L0_attn_in['w_out'], 'L0_attn_b_out': _L0_attn_in['b_out'], 'L0_ffn_router_w': _L0_ffn_in['router_w'], 'L0_ffn_router_b': _L0_ffn_in['router_b'], 'L0_ffn_w1': _L0_ffn_in['w1'], 'L0_ffn_b1': _L0_ffn_in['b1'], 'L0_ffn_w2': _L0_ffn_in['w2'], 'L0_ffn_b2': _L0_ffn_in['b2'], 'L1_xattn_Wq': _L1_xattn_in['Wq'], 'L1_xattn_bq': _L1_xattn_in['bq'], 'L1_xattn_Wk': _L1_xattn_in['Wk'], 'L1_xattn_bk': _L1_xattn_in['bk'], 'L1_xattn_Wv': _L1_xattn_in['Wv'], 'L1_xattn_bv': _L1_xattn_in['bv'], 'L1_xattn_Wo': _L1_xattn_in['Wo'], 'L1_xattn_bo': _L1_xattn_in['bo'], 'L1_attn_x_r': _L1_attn_in['x_r'], 'L1_attn_x_w': _L1_attn_in['x_w'], 'L1_attn_x_k': _L1_attn_in['x_k'], 'L1_attn_x_v': _L1_attn_in['x_v'], 'L1_attn_x_a': _L1_attn_in['x_a'], 'L1_attn_x_g': _L1_attn_in['x_g'], 'L1_attn_k_k': _L1_attn_in['k_k'], 'L1_attn_k_a': _L1_attn_in['k_a'], 'L1_attn_r_k': _L1_attn_in['r_k'], 'L1_attn_W_r': _L1_attn_in['W_r'], 'L1_attn_W_k': _L1_attn_in['W_k'], 'L1_attn_W_v': _L1_attn_in['W_v'], 'L1_attn_W_o': _L1_attn_in['W_o'], 'L1_attn_w_lora_a': _L1_attn_in['w_lora_a'], 'L1_attn_w_lora_b': _L1_attn_in['w_lora_b'], 'L1_attn_w_lora_bias': _L1_attn_in['w_lora_bias'], 'L1_attn_a_lora_a': _L1_attn_in['a_lora_a'], 'L1_attn_a_lora_b': _L1_attn_in['a_lora_b'], 'L1_attn_a_lora_bias': _L1_attn_in['a_lora_bias'], 'L1_attn_g_lora_a': _L1_attn_in['g_lora_a'], 'L1_attn_g_lora_b': _L1_attn_in['g_lora_b'], 'L1_attn_g_lora_bias': _L1_attn_in['g_lora_bias'], 'L1_attn_gn_weight': _L1_attn_in['gn_weight'], 'L1_attn_gn_bias': _L1_attn_in['gn_bias'], 'L1_ffn_w_gate': _L1_ffn_in['w_gate'], 'L1_ffn_w_up': _L1_ffn_in['w_up'], 'L1_ffn_w_down': _L1_ffn_in['w_down']}

def reference(x, ctx_1024, mask_BxSxS2_ff0, mask_SxS2_bk1, L0_xattn_Wq, L0_xattn_bq, L0_xattn_Wk, L0_xattn_bk, L0_xattn_Wv, L0_xattn_bv, L0_xattn_Wo, L0_xattn_bo, L0_attn_w_qkv, L0_attn_w_out, L0_attn_b_out, L0_ffn_router_w, L0_ffn_router_b, L0_ffn_w1, L0_ffn_b1, L0_ffn_w2, L0_ffn_b2, L1_xattn_Wq, L1_xattn_bq, L1_xattn_Wk, L1_xattn_bk, L1_xattn_Wv, L1_xattn_bv, L1_xattn_Wo, L1_xattn_bo, L1_attn_x_r, L1_attn_x_w, L1_attn_x_k, L1_attn_x_v, L1_attn_x_a, L1_attn_x_g, L1_attn_k_k, L1_attn_k_a, L1_attn_r_k, L1_attn_W_r, L1_attn_W_k, L1_attn_W_v, L1_attn_W_o, L1_attn_w_lora_a, L1_attn_w_lora_b, L1_attn_w_lora_bias, L1_attn_a_lora_a, L1_attn_a_lora_b, L1_attn_a_lora_bias, L1_attn_g_lora_a, L1_attn_g_lora_b, L1_attn_g_lora_bias, L1_attn_gn_weight, L1_attn_gn_bias, L1_ffn_w_gate, L1_ffn_w_up, L1_ffn_w_down):
    import jax
    import jax.numpy as jnp

    def _L0_xattn_ref(hidden_states, encoder_hidden_states, attention_mask, Wq, bq, Wk, bk, Wv, bv, Wo, bo):
        import jax, jax.numpy as jnp
        import numpy as np
        NUM_HEADS = 16
        DIM = 128
        B, N, C = hidden_states.shape
        T = encoder_hidden_states.shape[1]
        H = NUM_HEADS
        D = C // H
        q = (hidden_states @ Wq.T + bq).reshape(B, N, H, D).transpose(0, 2, 1, 3)
        k = (encoder_hidden_states @ Wk.T + bk).reshape(B, T, H, D).transpose(0, 2, 1, 3)
        v = (encoder_hidden_states @ Wv.T + bv).reshape(B, T, H, D).transpose(0, 2, 1, 3)
        scale = 1.0 / jnp.sqrt(jnp.asarray(D, q.dtype))
        scores = jnp.einsum('bhnd,bhtd->bhnt', q, k) * scale + attention_mask[:, None, :, :]
        attn = jax.nn.softmax(scores, axis=-1)
        out = jnp.einsum('bhnt,bhtd->bhnd', attn, v)
        out = out.transpose(0, 2, 1, 3).reshape(B, N, C)
        return out @ Wo.T + bo

    def _L0_attn_ref(x, w_qkv, w_out, b_out):
        import jax, jax.numpy as jnp
        import numpy as np
        import math
        B, T, D = (2, 256, 128)
        N_HEADS = 16
        D_HEAD = D // N_HEADS

        def _rope_tables(t, d_head, dtype=jnp.float32):
            theta = 1.0 / 10000.0 ** (jnp.arange(0, d_head, 2, dtype=jnp.float32) / d_head)
            angles = jnp.outer(jnp.arange(t, dtype=jnp.float32), theta)
            angles = jnp.concatenate([angles, angles], axis=-1)
            return (jnp.cos(angles).astype(dtype), jnp.sin(angles).astype(dtype))

        def _rotate_half(x):
            half = x.shape[-1] // 2
            return jnp.concatenate([-x[..., half:], x[..., :half]], axis=-1)

        def _apply_rope(x, cos, sin):
            return x * cos[None, None] + _rotate_half(x) * sin[None, None]
        b, t, d = x.shape
        qkv = x @ w_qkv
        qkv = qkv.reshape(b, t, 3, N_HEADS, D_HEAD)
        q = jnp.transpose(qkv[:, :, 0], (0, 2, 1, 3))
        k = jnp.transpose(qkv[:, :, 1], (0, 2, 1, 3))
        v = jnp.transpose(qkv[:, :, 2], (0, 2, 1, 3))
        cos, sin = _rope_tables(t, D_HEAD, x.dtype)
        q = _apply_rope(q, cos, sin)
        k = _apply_rope(k, cos, sin)
        scores = jnp.einsum('bhqd,bhkd->bhqk', q, k) / math.sqrt(D_HEAD)
        probs = jax.nn.softmax(scores, axis=-1)
        out = jnp.einsum('bhqk,bhkd->bhqd', probs, v)
        out = jnp.transpose(out, (0, 2, 1, 3)).reshape(b, t, d)
        return out @ w_out + b_out

    def _L0_ffn_ref(x, router_w, router_b, w1, b1, w2, b2):
        import jax, jax.numpy as jnp
        import numpy as np
        IN_F, OUT_F, BLOCK, NBLK = (128, 512, 32, 16)
        TOPK = NBLK // 4
        x_shape = x.shape
        xf = x.reshape(-1, IN_F)
        n = xf.shape[0]
        prob = jax.nn.softmax(xf @ router_w.T + router_b, axis=-1)
        _, idx = jax.lax.top_k(prob, TOPK)
        mask = jnp.zeros((n, NBLK), bool).at[jnp.arange(n)[:, None], idx].set(True)
        w1b = w1.reshape(NBLK, BLOCK, IN_F)
        b1b = b1.reshape(NBLK, BLOCK)
        h = jnp.einsum('nd,ibd->nib', xf, w1b) + b1b
        h = jnp.where(mask[:, :, None], h, jnp.zeros((), h.dtype))
        h = jax.nn.relu(h)
        w2b = w2.reshape(IN_F, NBLK, BLOCK)
        y = jnp.einsum('nib,dib->nd', jnp.where(mask[:, :, None], h, 0.0), w2b) + b2
        return y.reshape(x_shape)

    def _L1_xattn_ref(q, k, v, causal_mask, Wq, bq, Wk, bk, Wv, bv, Wo, bo):
        import jax, jax.numpy as jnp
        import numpy as np
        D_MODEL = 128
        NHEAD = 16
        HEAD_DIM = D_MODEL // NHEAD
        B, SQ, SK = (2, 256, 256)
        Bq, Sq, D = q.shape
        Sk = k.shape[1]
        H, Dh = (NHEAD, HEAD_DIM)
        scale = Dh ** (-0.5)
        qh = (q @ Wq.T + bq).reshape(Bq, Sq, H, Dh).transpose(0, 2, 1, 3)
        kh = (k @ Wk.T + bk).reshape(Bq, Sk, H, Dh).transpose(0, 2, 1, 3)
        vh = (v @ Wv.T + bv).reshape(Bq, Sk, H, Dh).transpose(0, 2, 1, 3)
        attn = jnp.einsum('bhqd,bhkd->bhqk', qh, kh) * scale
        attn = jnp.where(causal_mask[None, None, :, :], -jnp.inf, attn)
        attn = jax.nn.softmax(attn, axis=-1)
        out = jnp.einsum('bhqk,bhkd->bhqd', attn, vh)
        out = out.transpose(0, 2, 1, 3).reshape(Bq, Sq, D)
        return out @ Wo.T + bo

    def _L1_attn_ref(hidden_states, x_r, x_w, x_k, x_v, x_a, x_g, k_k, k_a, r_k, W_r, W_k, W_v, W_o, w_lora_a, w_lora_b, w_lora_bias, a_lora_a, a_lora_b, a_lora_bias, g_lora_a, g_lora_b, g_lora_bias, gn_weight, gn_bias):
        import jax, jax.numpy as jnp
        import numpy as np
        B, T, C, H = (2, 256, 128, 16)
        D = C // H
        RW, RA, RG = (64, 64, 128)
        EPS = 1e-05

        def _rwkv7_scan(r, log_w, k, v, a, b):
            Bn, Tn, Hn, Dn = r.shape

            def step(S, xs):
                r_t, w_t, k_t, v_t, a_t, b_t = xs
                sa = jnp.einsum('bhij,bhj->bhi', S, a_t)
                S = S * jnp.exp(w_t)[:, :, None, :] + sa[..., None] * b_t[:, :, None, :] + v_t[..., None] * k_t[:, :, None, :]
                o_t = jnp.einsum('bhij,bhj->bhi', S, r_t)
                return (S, o_t)
            S0 = jnp.zeros((Bn, Hn, Dn, Dn), r.dtype)
            xs = tuple((jnp.swapaxes(x, 0, 1) for x in (r, log_w, k, v, a, b)))
            _, o = jax.lax.scan(step, S0, xs)
            return jnp.swapaxes(o, 0, 1)
        Bn, Tn, Cn = hidden_states.shape
        shifted = jnp.concatenate([jnp.zeros_like(hidden_states[:, :1]), hidden_states[:, :-1]], axis=1)
        delta = shifted - hidden_states
        xr = hidden_states + delta * x_r
        xw = hidden_states + delta * x_w
        xk = hidden_states + delta * x_k
        xv = hidden_states + delta * x_v
        xa = hidden_states + delta * x_a
        r = xr @ W_r
        log_w = -jax.nn.softplus(-(jnp.tanh(xw @ w_lora_a) @ w_lora_b + w_lora_bias)) - 0.5
        k = xk @ W_k
        v = xv @ W_v
        a = jax.nn.sigmoid(xa @ a_lora_a @ a_lora_b + a_lora_bias)
        g = jax.nn.sigmoid(r @ g_lora_a) @ g_lora_b + g_lora_bias
        kk = (k * k_k).reshape(Bn, Tn, H, D)
        kk = kk / jnp.maximum(jnp.linalg.norm(kk, axis=-1, keepdims=True), 1e-12)
        k = k * (1.0 + (a - 1.0) * k_a)
        rh = r.reshape(Bn, Tn, H, D)
        wh = log_w.reshape(Bn, Tn, H, D)
        kh = k.reshape(Bn, Tn, H, D)
        vh = v.reshape(Bn, Tn, H, D)
        ah = a.reshape(Bn, Tn, H, D)
        o = _rwkv7_scan(rh, wh, kh, vh, -kk, kk * ah)
        mu = o.mean(-1, keepdims=True)
        var = ((o - mu) ** 2).mean(-1, keepdims=True)
        o_flat = ((o - mu) * jax.lax.rsqrt(var + EPS)).reshape(Bn, Tn, C) * gn_weight + gn_bias
        bonus = ((rh * kh * r_k).sum(-1, keepdims=True) * vh).reshape(Bn, Tn, C)
        o_flat = o_flat + bonus
        return o_flat * g @ W_o

    def _L1_ffn_ref(x, w_gate, w_up, w_down):
        import jax, jax.numpy as jnp
        import numpy as np
        HIDDEN = 128
        INNER = 512

        def _weight_quant(w):
            scale = 1.0 / jnp.clip(jnp.mean(jnp.abs(w)), 1e-05)
            wq = jnp.clip(jnp.round(w * scale), -1.0, 1.0) / scale
            return w + jax.lax.stop_gradient(wq - w)

        def _act_quant(x):
            scale = 127.0 / jnp.clip(jnp.max(jnp.abs(x), axis=-1, keepdims=True), 1e-05)
            xq = jnp.clip(jnp.round(x * scale), -128.0, 127.0) / scale
            return x + jax.lax.stop_gradient(xq - x)

        def _bitlinear(x, w):
            return jnp.einsum('bsi,oi->bso', _act_quant(x), _weight_quant(w))
        gate = jax.nn.silu(_bitlinear(x, w_gate))
        up = _bitlinear(x, w_up)
        return _bitlinear(gate * up, w_down)
    x = x + _L0_xattn_ref(_layernorm(x, axis=-1), ctx_1024, mask_BxSxS2_ff0, L0_xattn_Wq, L0_xattn_bq, L0_xattn_Wk, L0_xattn_bk, L0_xattn_Wv, L0_xattn_bv, L0_xattn_Wo, L0_xattn_bo)
    x = x + _L0_attn_ref(_layernorm(x, axis=-1), L0_attn_w_qkv, L0_attn_w_out, L0_attn_b_out)
    x = x + _L0_ffn_ref(_layernorm(x, axis=-1), L0_ffn_router_w, L0_ffn_router_b, L0_ffn_w1, L0_ffn_b1, L0_ffn_w2, L0_ffn_b2)
    x = x + _L1_xattn_ref(_layernorm(x, axis=-1), ctx_1024, ctx_1024, mask_SxS2_bk1, L1_xattn_Wq, L1_xattn_bq, L1_xattn_Wk, L1_xattn_bk, L1_xattn_Wv, L1_xattn_bv, L1_xattn_Wo, L1_xattn_bo)
    x = x + _L1_attn_ref(_layernorm(x, axis=-1), L1_attn_x_r, L1_attn_x_w, L1_attn_x_k, L1_attn_x_v, L1_attn_x_a, L1_attn_x_g, L1_attn_k_k, L1_attn_k_a, L1_attn_r_k, L1_attn_W_r, L1_attn_W_k, L1_attn_W_v, L1_attn_W_o, L1_attn_w_lora_a, L1_attn_w_lora_b, L1_attn_w_lora_bias, L1_attn_a_lora_a, L1_attn_a_lora_b, L1_attn_a_lora_bias, L1_attn_g_lora_a, L1_attn_g_lora_b, L1_attn_g_lora_bias, L1_attn_gn_weight, L1_attn_gn_bias)
    x = x + _L1_ffn_ref(_layernorm(x, axis=-1), L1_ffn_w_gate, L1_ffn_w_up, L1_ffn_w_down)
    return x

_drawn_inputs = setup_inputs


def setup_inputs(seed=0):
    import zlib

    import numpy as np

    out = dict(_drawn_inputs(seed))
    spreads = {'L0_xattn_bq': (0.0, 0.281),
     'L0_xattn_bk': (0.0, 2.0),
     'L0_xattn_bv': (0.0, 0.1),
     'L0_xattn_bo': (0.0, 0.1),
     'L1_xattn_bq': (0.0, 2.0),
     'L1_xattn_bk': (0.0, 2.0),
     'L1_xattn_bv': (0.0, 0.522),
     'L1_xattn_bo': (0.0, 0.1),
     'L1_attn_a_lora_bias': (0.0, 0.8),
     'L1_attn_g_lora_bias': (0.0, 0.48),
     'L1_attn_gn_weight': (1.0, 0.6),
     'L1_attn_gn_bias': (0.0, 0.8)}
    factors = {'L0_attn_b_out': 5.794,
     'L0_ffn_b1': 6.158,
     'L1_xattn_Wq': 8.0,
     'L1_xattn_Wk': 8.0,
     'L1_attn_x_r': 4.234,
     'L1_attn_x_w': 8.0,
     'L1_attn_x_k': 4.437,
     'L1_attn_x_v': 4.495,
     'L1_attn_x_a': 8.0,
     'L1_attn_k_k': 7.939,
     'L1_attn_k_a': 7.662,
     'L1_attn_r_k': 8.0,
     'L1_attn_w_lora_a': 8.0,
     'L1_attn_w_lora_b': 8.0,
     'L1_attn_w_lora_bias': 8.0,
     'L1_attn_a_lora_a': 8.0,
     'L1_attn_a_lora_b': 8.0,
     'L1_attn_g_lora_a': 8.0,
     'L1_attn_g_lora_b': 3.015}
    for name, (base, spread) in spreads.items():
        noise = np.random.default_rng([zlib.crc32(name.encode()), seed]).standard_normal(out[name].shape)
        drawn = base * np.exp(spread * noise) if base else spread * noise
        out[name] = jnp.asarray(drawn.astype(out[name].dtype))
    for name, factor in factors.items():
        out[name] = (out[name] * factor).astype(out[name].dtype)
    return out
```

```python
import numpy as np
import concourse.bass as bass
from concourse import mybir
from contextlib import ExitStack

N, C, T = 64, 128, 6272
H, D = 16, 8
PAIRS = H // 2
TILES = T // 128
BCH, BT = 7, TILES // 7
BW = BT * 128
ACH = 14
AW = T // ACH
CUT = 6 * AW
VG = (TILES + 3) // 4
INNER = 512
FT = INNER // 128
STEPS, SEGS = 8, N // 8
BIG = 1e30
SCALE = float(1.0 / np.sqrt(np.float32(D)))
Q_PART = [0, 1, 2, 0, 1, 0]
K_PART = [0, 0, 0, 1, 1, 2]
QK = len(Q_PART) * 2 * D
QKM = QK + 3

WCOLS = {}
def _lay(names, into, start=0):
    for n, w in names:
        into[n] = slice(start, start + w)
        start += w
    return start

W_EARLY = _lay([("Wk0", C), ("Wv0", C), ("Wq0", C), ("Wo0", C)], WCOLS)
W_ALL = _lay([("Wk1", C), ("Wv1", C), ("Wq1", C), ("Wo1", C), ("aq", C), ("aqr", C), ("ak", C), ("akr", C),
              ("av", C), ("aout", C), ("router", H), ("w1", INNER), ("w2", INNER), ("W_r", C), ("W_k", C),
              ("W_v", C), ("W_o", C), ("wla", 64), ("wlb", C), ("ala", 64), ("alb", C), ("gla", C),
              ("glb", C), ("gate", INNER), ("up", INNER), ("down", INNER)], WCOLS, W_EARLY)
COLS = {}
N_COLS = _lay([("bk0", 1), ("bq0", 1), ("bk1", 1), ("bq1", 1), ("b1", FT), ("x_r", 1), ("x_w", 1), ("x_k", 1),
               ("x_v", 1), ("x_a", 1), ("k_k", 1), ("k_a", 1), ("r_k", 1), ("w_bias", 1), ("a_bias", 1),
               ("g_bias", 1), ("gn_w", 1), ("gn_b", 1)], COLS)
ROWS = {}
N_ROWS = _lay([("bv0", C), ("bo0", C), ("bv1", C), ("bo1", C), ("b_out", C), ("b2", C), ("router_b", H)], ROWS)
CF = {}
N_CF = _lay([("ident", 128), ("group", 128), ("hmask", 128), ("comb", 18), ("head", H), ("vmask", 128),
             ("cos", N), ("sin", N), ("before", H * H), ("eye8", D)], CF)
CB = {}
N_CB = _lay([("ident", 128), ("rep", 128), ("half", 128), ("spread", 3 * PAIRS * QK)], CB)


def program(nc, x_d, ctx_d, mask0_d, mask1_d, w_d, cols_d, rows_d, cf_d, cb_d, out_d):
    fp32, bf16, u8, i32 = mybir.dt.float32, mybir.dt.bfloat16, mybir.dt.uint8, mybir.dt.int32
    ALU, ACT, AX = mybir.AluOpType, mybir.ActivationFunctionType, mybir.AxisListType

    ctx = ExitStack()
    with ctx:
        def sb(name, shape, dt=fp32):
            return ctx.enter_context(nc.sbuf_tensor(name, shape, dt))

        bank = [ctx.enter_context(nc.psum_tensor(f"bank{i}", [128, 512], fp32)) for i in range(2)]
        wide = [ctx.enter_context(nc.psum_tensor(f"wide{i}", [128, 1024], fp32)) for i in range(2)]
        outb = [ctx.enter_context(nc.psum_tensor(f"outb{i}", [128, 512], fp32)) for i in range(2)]

        w = sb("w", [128, W_ALL])
        cols = sb("cols", [128, N_COLS])
        rows = sb("rows", [N, N_ROWS])
        cf = sb("cf", [128, N_CF])
        cb = sb("cb", [128, N_CB], bf16)
        ctxT = sb("ctxT", [128, T])
        keys = [sb(f"keys{i}", [128, T], bf16) for i in range(2)]
        mask = sb("mask", [128, T])
        mask_hm = sb("mask_hm", [128, T], bf16)
        mask_lo = sb("mask_lo", [128, T], bf16)
        values = sb("values", [128, TILES, C])
        vpair = [sb(f"vpair{i}", [128, TILES, 32]) for i in range(2)]
        probs = [sb(f"probs{i}", [128, BW]) for i in range(2)]
        kfull = [sb(f"kfull{i}", [128, AW]) for i in range(2)]
        kparts = [sb(f"kparts{i}", [128, 3, AW], bf16) for i in range(2)]
        mrest = [sb(f"mrest{i}", [128, BW]) for i in range(2)]
        qstack = sb("qstack", [128, PAIRS, 128], bf16)
        qparts = sb("qparts", [128, 3, 2, N], bf16)
        outs = sb("outs", [128, PAIRS, 128])
        junk = sb("junk", [128, 2, AW], bf16)
        cmax = [sb(f"cmax{i}", [128, ACH]) for i in range(2)]
        pmax = sb("pmax", [128, PAIRS])
        mcol = [sb(f"mcol{i}", [128, QKM], bf16) for i in range(2)]
        mres = sb("mres", [128, 2])
        xs = sb("xs", [N, 7, C])
        xb = sb("xb", [N, C])
        xn = sb("xn", [N, C])
        xnT = sb("xnT", [C, 2, N])
        qT = sb("qT", [C, N])
        qres = sb("qres", [C, N])
        stat = sb("stat", [N, 16])
        mhalf = sb("mhalf", [128, N])
        o = sb("o", [N, C])
        oT = sb("oT", [C, N])
        rsum = sb("rsum", [N, H])
        place = {"mask": 0, "ctxT": 0, "values": 0}
        home = {"mask": mask[:, :], "ctxT": ctxT[:, :], "values": values[:, :, :].rearrange("p t c -> p (t c)")}

        def take(where, n, parts=128):
            a = place[where]
            place[where] = a + n
            return home[where][0:parts, a:a + n]

        wq = take("mask", 3 * INNER // 2).bitcast(bf16).rearrange("p (m f) -> p m f", m=3)
        wabs, wmean, winv, ones = take("mask", 3), take("mask", 3), take("mask", 3), take("mask", 128)
        wtmp = take("mask", 2 * INNER).rearrange("p (a f) -> p a f", a=2)
        begin = place["mask"]
        qkrot = take("mask", 128).rearrange("p (a n) -> p a n", a=2)
        qksin = take("mask", 128).rearrange("p (a n) -> p a n", a=2)
        qrot = qkrot[:, 0, :]
        kbd = take("mask", H * N)
        prob = take("mask", H * N, N)
        smax = take("mask", H, N)
        probT = take("mask", PAIRS * N).rearrange("p (h n) -> p h n", h=PAIRS)
        v2 = take("mask", C)
        place["mask"] = begin
        logit, rank = take("mask", H, N), take("mask", H, N)
        over, even = take("mask", H * H, N), take("mask", H * H, N)
        fmask = take("mask", INNER // 2, N).bitcast(bf16)
        hpre, hT_ = take("mask", FT * N), take("mask", FT * N)
        hT = hT_.rearrange("p (f n) -> p f n", f=FT)
        place["mask"] = begin
        delta = take("mask", N)
        mix = take("mask", 5 * N).rearrange("p (m n) -> p m n", m=5)
        lmid = take("mask", 2 * N, 64).rearrange("p (m n) -> p m n", m=2)
        rkv = take("mask", 3 * N).rearrange("p (m n) -> p m n", m=3)
        sig = take("mask", 2 * N).rearrange("p (m n) -> p m n", m=2)
        expo = take("mask", 2 * N).rearrange("p (m n) -> p m n", m=2)
        nbias = take("mask", 2)
        gexp, gsig, kk, kk_ss, kk_inv, nkk, bvec, kmix, tmpA, tmpB = [take("mask", N) for _ in range(10)]
        oseq, gn_v, gn_rstd, gated, onrm, bonus = [take("mask", N) for _ in range(6)]
        sa = take("mask", SEGS * 2).rearrange("p (c y) -> p c y", c=SEGS)
        prod = take("mask", SEGS * 2 * D).rearrange("p (c y j) -> p c y j", c=SEGS, y=2)
        prod2 = take("mask", SEGS * 2 * D).rearrange("p (c y j) -> p c y j", c=SEGS, y=2)
        first = take("mask", SEGS * 2 * D).rearrange("p (c y j) -> p c y j", c=SEGS, y=2)
        diag = take("ctxT", 5 * N * D).rearrange("p (v n) -> p v n", v=5)
        bdU = take("ctxT", (SEGS - 1) * 128).rearrange("p (c n) -> p c n", n=128)
        bdP = take("ctxT", (SEGS - 2) * 128).rearrange("p (c n) -> p c n", n=128)
        carryT = take("ctxT", (SEGS - 1) * 128).rearrange("p (c n) -> p c n", n=128)
        along = take("values", 5 * N * D).rearrange("p (v n) -> p v n", v=5)
        vk = take("values", N * D)
        states = take("values", STEPS * SEGS * 2 * D).rearrange("p (s c y j) -> p s c y j", s=STEPS, c=SEGS, y=2)
        rd = take("values", 2 * N * D).rearrange("p (y n) -> p y n", y=2)
        pread = take("values", 2 * N).rearrange("p (y s c) -> p y s c", y=2, s=STEPS)
        absx, xint = take("values", C, N), take("values", C, N)
        xiT = take("values", N // 2).bitcast(bf16)
        am = take("values", 8, N)
        place["ctxT"] = 0
        gate_, up_, den_, hint = [take("ctxT", INNER, N) for _ in range(4)]
        hiT = take("values", FT * N // 2).bitcast(bf16).rearrange("p (f n) -> p f n", f=FT)
        kscr = [nc.dram_tensor(f"key_parts{i}", [3, 128, T], bf16, kind="Internal").ap() for i in range(2)]

        def W(name):
            return w[:, WCOLS[name]]

        def col(name):
            return cols[:, COLS[name]]

        def row(name):
            return rows[:, ROWS[name]]

        def const(name, n=128):
            return cf[0:n, CF[name]]

        def constb(name, n=128):
            return cb[0:n, CB[name]]

        def sem(name):
            return ctx.enter_context(nc.semaphore(name))

        ld_first, ld_rest, ld_mask, ld_bf, ld_mask1, stored = map(sem, (
            "ld_first", "ld_rest", "ld_mask", "ld_bf", "ld_mask1", "stored"))
        ld_ctx = [sem(f"ld_ctx{i}") for i in range(4)]
        k_load = [[sem(f"k_load{s}_{h}") for h in range(2)] for s in range(2)]
        k_store = [sem(f"k_store{i}") for i in range(2)]
        (ln_var, ln_rstd, ln_norm, ln_T, ln_xT, x_res, x_ready) = map(sem, (
            "ln_var", "ln_rstd", "ln_norm", "ln_T", "ln_xT", "x_res", "x_ready"))
        (q_proj, q_split, q_spread, q_stack, k_projd, k_evac, k_cut, v_projd, v_evac) = map(sem, (
            "q_proj", "q_split", "q_spread", "q_stack", "k_projd", "k_evac", "k_cut", "v_projd", "v_evac"))
        (a_scored, a_maxed, neg_max, neg_T, q_full, b_scored, exped, pv_done, vp_ready, o_saved) = map(sem, (
            "a_scored", "a_maxed", "neg_max", "neg_T", "q_full", "b_scored", "exped", "pv_done", "vp_ready",
            "o_saved"))
        (o_comb, o_norm, o_T, o_Tc, y_proj) = map(sem, ("o_comb", "o_norm", "o_T", "o_Tc", "y_proj"))
        (preset, m_high, m_rest, m_mid, m_parts, m1_ready) = map(sem, (
            "preset", "m_high", "m_rest", "m_mid", "m_parts", "m1_ready"))
        chain = {e: sem(f"{e}_chain") for e in ("dve", "act", "pool")}
        count = {e: 0 for e in chain}
        named = {}

        def once(name):
            if name not in named:
                named[name] = sem(name)
            return named[name]

        def link(which, eng, ins):
            count[which] += 1
            ins.then_inc(chain[which], 1)
            eng.wait_ge(chain[which], count[which])

        def pieces():
            return [(0, 4 * AW), (4 * AW, 8 * AW), (8 * AW, 12 * AW), (12 * AW, T)]

        def ctx_piece(c1):
            return (c1 - 1) // (4 * AW)

        block = ctx.enter_context(nc.Block())

        @block.sync
        def _(sp):
            sp.dma_start(w[:, 0:W_EARLY], w_d[:, 0:W_EARLY]).then_inc(ld_first, 16)
            sp.dma_start(cols[:, :], cols_d).then_inc(ld_first, 16)
            for i, (a, b) in enumerate(pieces()):
                sp.dma_start(ctxT[:, a:b], ctx_d[:, a:b]).then_inc(ld_ctx[i], 16)
                if i == 0:
                    sp.dma_start(cf[:, :], cf_d).then_inc(ld_first, 16)
                    sp.dma_start(xs[:, 0, :], x_d).then_inc(ld_first, 16)
                    sp.dma_start(cb[:, :], cb_d).then_inc(ld_bf, 16)
            for half in range(2):
                sp.dma_start(mask[64 * half:64 * half + 64, :], mask0_d).then_inc(ld_mask, 16)
            sp.dma_start(rows[:, :], rows_d.broadcast_to([N, N_ROWS])).then_inc(ld_rest, 16)
            sp.dma_start(w[:, W_EARLY:W_ALL], w_d[:, W_EARLY:W_ALL]).then_inc(ld_rest, 16)

            for L in range(2):
                for i in range(ACH):
                    sp.wait_ge(k_cut, ACH * L + i + 1)
                    sp.dma_start(kscr[L][:, :, i * AW:(i + 1) * AW].rearrange("j p t -> p j t"),
                                 kparts[i % 2][:, :, :]).then_inc(k_store[i % 2], 16)
                for i in range(2):
                    sp.wait_ge(k_store[i], 16 * (ACH // 2) * (L + 1))
                if L == 1:
                    sp.wait_ge(x_ready, 1)
                    for half in range(2):
                        sp.dma_start(mask_lo[64 * half:64 * half + 64, 0:T // 2].bitcast(i32),
                                     mask1_d).then_inc(ld_mask1, 16)
                for p in range(PAIRS):
                    g = PAIRS * L + p
                    for piece, (a, b) in enumerate([(0, CUT), (CUT, T)]):
                        if g >= 2:
                            sp.wait_ge(b_scored, BCH * (g - 2) + (3 if piece == 0 else BCH))
                        for j, part in enumerate(K_PART):
                            sp.dma_start(keys[g % 2][16 * j:16 * j + 16, a:b],
                                         kscr[L][part, 16 * p:16 * p + 16, a:b]).then_inc(k_load[g % 2][piece], 16)
            sp.wait_ge(x_ready, 6)
            sp.dma_start(out_d, xs[:, 6, :]).then_inc(stored, 16)
            sp.wait_ge(stored, 16)

        @block.gpsimd
        def _(pool):
            def fill(ap, value):
                link("pool", pool, pool.memset(ap, value))

            fill(mhalf[:, :], -0.5)
            for i in range(2):
                fill(vpair[i][:, :, :], 0.0)
                fill(mcol[i][:, :], 0.0)
                fill(keys[i][QK:QKM, :], 1.0)
                fill(vpair[i][:, :, 0:18].rearrange("p t (h e) -> p t h e", e=9)[:, :, :, 8:9], 1.0)
            pool.memset(mask_lo[0:64, :], 0.0).then_inc(preset, 1)
            pool.wait_ge(preset, 1)

            def ln_power(k):
                pool.wait_ge(ln_var, k + 1)
                pool.tensor_tensor(stat[:, 9:10], stat[:, 8:9], mhalf[0:N, 0:1], ALU.pow).then_inc(ln_rstd, 1)
                pool.wait_ge(ln_rstd, k + 1)

            def add_bias(k, name):
                pool.wait_ge(x_ready, k)
                if k == 0:
                    pool.wait_ge(ld_first, 64)
                    pool.wait_ge(ld_rest, 32)
                pool.tensor_tensor(xb[:, :], xs[:, k, :], row(name), ALU.add).then_inc(x_res, 1)
                pool.wait_ge(x_res, k + 1)

            pool.wait_ge(ld_first, 64)
            ln_power(0)
            for c in range(BCH):
                s = slice(c * BW, (c + 1) * BW)
                pool.wait_ge(m_high, c + 1)
                pool.tensor_tensor(mrest[c % 2][64:128, :], mask[64:128, s], mask_hm[64:128, s],
                                   ALU.subtract).then_inc(m_rest, 1)
                pool.wait_ge(m_mid, c + 1)
                pool.tensor_tensor(mask_lo[64:128, s], mrest[c % 2][64:128, :], mask_hm[64:128, s],
                                   ALU.subtract).then_inc(m_parts, 1)
                pool.wait_ge(m_parts, c + 1)

            def pair_values(L):
                for p in range(PAIRS):
                    g = PAIRS * L + p
                    if p == 0:
                        pool.wait_ge(v_evac, VG * (L + 1))
                    if g >= 2:
                        pool.wait_ge(pv_done, BCH * (g - 1))
                    pool.tensor_copy(
                        vpair[g % 2][:, :, 0:18].rearrange("p t (h e) -> p t h e", e=9)[:, :, :, 0:8],
                        values[:, :, 16 * p:16 * p + 16].rearrange("p t (h e) -> p t h e", e=8)
                    ).then_inc(vp_ready, 1)
                    pool.wait_ge(vp_ready, g + 1)

            pair_values(0)
            add_bias(0, "bo0")
            ln_power(1)
            add_bias(1, "b_out")
            ln_power(2)
            add_bias(2, "b2")
            ln_power(3)
            pair_values(1)
            add_bias(3, "bo1")
            ln_power(4)
            pool.wait_ge(once("kk_sq"), 1)
            pool.tensor_tensor(kk_inv, kk_ss, mhalf[:, :], ALU.pow).then_inc(once("kk_pow"), 1)
            pool.wait_ge(once("kk_pow"), 1)
            pool.wait_ge(once("gn_var"), 1)
            pool.tensor_tensor(gn_rstd, gn_v, mhalf[:, :], ALU.pow).then_inc(once("gn_pow"), 1)
            pool.wait_ge(once("gn_pow"), 1)
            ln_power(5)

        @block.tensor
        def _(pe):
            mm = nc.tensor.matmul
            ident = const("ident")

            def ln_transpose(k):
                pe.wait_ge(ln_norm, k + 1)
                nc.tensor.transpose(outb[0][:, 0:N], xn[:, :], ident[0:N, 0:N]).then_inc(ln_T, 1)

            def project_keys(L):
                for i in range(ACH):
                    if L == 0:
                        pe.wait_ge(ld_ctx[ctx_piece((i + 1) * AW)], 16)
                    n = ACH * L + i
                    if n >= 2:
                        pe.wait_ge(k_evac, n - 1)
                    mm(bank[i % 2][:, 0:AW], W(f"Wk{L}"), ctxT[:, i * AW:(i + 1) * AW],
                       start=True, stop=True).then_inc(k_projd, 1)

            def project_values(L):
                for g in range(VG):
                    n = VG * L + g
                    if g >= 4:
                        pe.wait_ge(v_evac, n - 3)
                    u = wide[g % 4 // 2][:, 512 * (g % 2):512 * (g % 2) + 512]
                    for t in range(4 * g, min(4 * g + 4, TILES)):
                        last = mm(u[:, 128 * (t % 4):128 * (t % 4) + 128], ctxT[:, 128 * t:128 * t + 128],
                                  W(f"Wv{L}"), start=True, stop=True)
                    last.then_inc(v_projd, 1)

            def queries(L):
                pe.wait_ge(ln_xT, 1 if L == 0 else 4)
                mm(outb[1][:, 0:N], W(f"Wq{L}"), xnT[:, 0, :], start=True, stop=True).then_inc(q_proj, 1)
                pe.wait_ge(q_split, L + 1)
                pe.wait_ge(ld_bf, 16)
                if L == 1:
                    pe.wait_ge(v_evac, 2 * VG)
                spread = constb("spread").rearrange("p (i h r) -> p i h r", i=3, r=QK)
                for p in range(PAIRS):
                    for i in range(3):
                        last = mm(wide[0][0:QK, 128 * p:128 * p + 128], spread[:, i, p, :], qparts[:, i, :, :],
                                  start=(i == 0), stop=(i == 2))
                last.then_inc(q_spread, 1)

            def pass_a(L, p, a):
                g = PAIRS * L + p
                n = ACH * g + a
                if a == 0:
                    pe.wait_ge(k_load[p % 2][0], 96 * (g // 2 + 1))
                if a == CUT // AW:
                    pe.wait_ge(k_load[p % 2][1], 96 * (g // 2 + 1))
                if n >= 2:
                    pe.wait_ge(a_maxed, n - 1)
                mm(bank[a % 2][:, 0:AW], qstack[0:QK, p, :], keys[p % 2][0:QK, a * AW:(a + 1) * AW],
                   start=True, stop=True).then_inc(a_scored, 1)

            def max_rows(L, p):
                g = PAIRS * L + p
                pe.wait_ge(neg_max, g + 1)
                if g >= 2:
                    pe.wait_ge(o_saved, g - 1)
                mm(outb[p % 2][0:QKM, 128:256], mcol[p % 2][:, :], constb("ident"),
                   start=True, stop=True).then_inc(neg_T, 1)

            def pass_b(L, p, c):
                g = PAIRS * L + p
                n = BCH * g + c
                if c == 0:
                    pe.wait_ge(q_full, g + 1)
                    if g == 0:
                        pe.wait_ge(m_parts, BCH)
                        pe.wait_ge(v_evac, VG)
                if n >= 2:
                    pe.wait_ge(exped, n - 1)
                for i in range(BT):
                    t = slice(128 * (BT * c + i), 128 * (BT * c + i) + 128)
                    u = wide[n % 2][:, 128 * i:128 * i + 128]
                    mm(u, keys[p % 2][0:QKM, t], qstack[0:QKM, p, :], start=True, stop=False)
                    if L == 0:
                        mm(u, mask_hm[:, t], constb("rep"), start=False, stop=False)
                        last = mm(u, mask_lo[:, t], constb("rep"), start=False, stop=True)
                    else:
                        last = mm(u, mask_hm[:, t], constb("half"), start=False, stop=True)
                last.then_inc(b_scored, 1)

            def weigh(L, p, c):
                g = PAIRS * L + p
                n = BCH * g + c
                if c == 0:
                    pe.wait_ge(vp_ready, g + 1)
                pe.wait_ge(exped, n + 1)
                for i in range(BT):
                    t = BT * c + i
                    q = 32 * (t % 4)
                    last = mm(outb[p % 2][q:q + 32, 0:128], vpair[p % 2][:, t, :],
                              probs[n % 2][:, 128 * i:128 * i + 128], start=(t < 4), stop=(t >= TILES - 4))
                last.then_inc(pv_done, 1)

            A_PLAN = [3, 3, 3, 3, 2, 0, 0]

            def attention(L):
                pe.wait_ge(q_stack, L + 1)
                if L == 1:
                    pe.wait_ge(m1_ready, 1)
                for a in range(ACH):
                    pass_a(L, 0, a)
                max_rows(L, 0)
                for p in range(PAIRS):
                    a = 0
                    for c in range(BCH):
                        if p + 1 < PAIRS:
                            for _ in range(A_PLAN[c]):
                                pass_a(L, p + 1, a)
                                a += 1
                        pass_b(L, p, c)
                        if c:
                            weigh(L, p, c - 1)
                        elif p:
                            weigh(L, p - 1, BCH - 1)
                        if c == 5 and p + 1 < PAIRS:
                            max_rows(L, p + 1)
                weigh(L, PAIRS - 1, BCH - 1)

            def output(L):
                comb = const("comb").rearrange("p (h e) -> p h e", h=2)
                pe.wait_ge(o_saved, PAIRS * (L + 1))
                for h in range(H):
                    last = mm(outb[0][0:N, 9 * h:9 * h + 9], outs[:, h // 2, 64 * (h % 2):64 * (h % 2) + 64],
                              comb[:, h % 2, :], start=True, stop=True)
                last.then_inc(o_comb, 1)
                project_out(2 * L + 1, f"Wo{L}")

            def project_out(turn, name):
                pe.wait_ge(o_norm, turn)
                nc.tensor.transpose(outb[1][:, 0:N], o[:, :], ident[0:N, 0:N]).then_inc(o_T, 1)
                pe.wait_ge(o_Tc, turn)
                mm(outb[0][0:N, 256:384], oT[:, :], W(name), start=True, stop=True).then_inc(y_proj, 1)

            pe.wait_ge(ld_first, 64)
            ln_transpose(0)
            project_keys(0)
            queries(0)
            pe.wait_ge(q_stack, 1)
            project_values(0)
            attention(0)
            output(0)
            pe.wait_ge(ld_rest, 32)

            ln_transpose(1)
            project_keys(1)
            project_values(1)
            pe.wait_ge(ln_xT, 2)
            pe.wait_ge(v_evac, 2 * VG)
            for i, name in enumerate(("aq", "aqr", "ak", "akr")):
                mm(bank[0][:, 64 * i:64 * i + 64], W(name), xnT[:, 0, :], start=True, stop=True)
            mm(bank[1][:, 0:128], xnT[:, :, :], W("av"), start=True, stop=True).then_inc(once("self_proj"), 1)
            pe.wait_ge(once("self_kbd"), 1)
            for i in range(2):
                last = mm(wide[0][0:N, 512 * i:512 * i + 512], qrot, kbd[:, 512 * i:512 * i + 512],
                          start=True, stop=True)
            last.then_inc(once("self_scored"), 1)
            pe.wait_ge(once("self_exp"), 1)
            for p in range(PAIRS):
                last = nc.tensor.transpose(bank[0][:, 64 * p:64 * p + 64], prob[:, 128 * p:128 * p + 128],
                                           ident[0:N, 0:N])
            last.then_inc(once("self_T"), 1)
            pe.wait_ge(once("self_Tc"), 1)
            for p in range(PAIRS):
                last = mm(bank[1][0:N, 128 + 16 * p:144 + 16 * p], probT[:, p, :], v2[:, 16 * p:16 * p + 16],
                          start=True, stop=True)
            last.then_inc(once("self_out"), 1)
            project_out(2, "aout")

            ln_transpose(2)
            pe.wait_ge(ln_xT, 3)
            mm(bank[0][0:N, 0:H], xnT[:, 0, :], W("router"), start=True, stop=True).then_inc(once("routed"), 1)
            for f in range(FT):
                last = mm(bank[1][:, 64 * f:64 * f + 64], w[:, WCOLS["w1"].start + 128 * f:WCOLS["w1"].start + 128 * f + 128],
                          xnT[:, 0, :], start=True, stop=True)
            last.then_inc(once("ff_h"), 1)
            pe.wait_ge(once("ff_mask"), 1)
            for f in range(FT):
                last = mm(outb[1][:, 64 * f:64 * f + 64], fmask[:, 128 * f:128 * f + 128], constb("ident", N)[:, 0:N],
                          start=True, stop=True)
            last.then_inc(once("ff_maskT"), 1)
            pe.wait_ge(once("ff_relu"), 1)
            for f in range(FT):
                last = mm(outb[0][0:N, 256:384], hT[:, f, :], w[:, WCOLS["w2"].start + 128 * f:WCOLS["w2"].start + 128 * f + 128],
                          start=(f == 0), stop=(f == FT - 1))
            last.then_inc(y_proj, 1)

            pe.wait_ge(once("w_abs"), 1)
            pe.wait_ge(once("ones"), 1)
            mm(outb[1][:, 0:3], ones, wabs, start=True, stop=True).then_inc(once("w_mean"), 1)

            ln_transpose(3)
            queries(1)
            attention(1)
            output(1)

            ln_transpose(4)
            pe.wait_ge(once("mixed"), 1)
            for i, name in enumerate(("W_r", "W_k", "W_v")):
                mm(bank[0][:, 64 * i:64 * i + 64], W(name), mix[:, i, :], start=True, stop=True)
            mm(bank[1][0:64, 0:64], W("wla"), mix[:, 3, :], start=True, stop=True)
            mm(bank[1][0:64, 64:128], W("ala"), mix[:, 4, :], start=True, stop=True).then_inc(once("rwkv_proj"), 1)
            pe.wait_ge(once("lora_mid"), 1)
            mm(bank[1][:, 128:192], w[0:64, WCOLS["wlb"]], lmid[:, 0, :], start=True, stop=True)
            mm(bank[1][:, 192:256], w[0:64, WCOLS["alb"]], lmid[:, 1, :], start=True, stop=True).then_inc(once("lora_out"), 1)
            pe.wait_ge(once("rkv_copied"), 1)
            mm(outb[1][:, 0:64], W("gla"), rkv[:, 0, :], start=True, stop=True).then_inc(once("g_mid"), 1)
            pe.wait_ge(once("kk_squared"), 1)
            mm(outb[0][:, 0:64], const("group"), tmpA, start=True, stop=True).then_inc(once("kk_sum"), 1)
            pe.wait_ge(once("g_sig"), 1)
            mm(outb[1][:, 64:128], W("glb"), gsig, start=True, stop=True).then_inc(once("g_out"), 1)
            for i, name in enumerate(("r", "w", "k", "a", "b")):
                pe.wait_ge(once("spread_" + name), 1)
                dst = [wide[0][:, 0:512], wide[0][:, 512:1024], wide[1][:, 0:512], wide[1][:, 512:1024], bank[0][:, 0:512]][i]
                mm(dst, const("group"), diag[:, i, :], start=True, stop=True).then_inc(once("bc_" + name), 1)
            pe.wait_ge(once("rkk"), 1)
            mm(outb[1][:, 128:192], const("group"), tmpB, start=True, stop=True).then_inc(once("bonus_sum"), 1)
            pe.wait_ge(once("seg_blocks"), 1)
            pe.wait_ge(once("reads_done"), 1)
            for c in range(SEGS - 1):
                u = bank[c % 2][:, 0:128]
                if c >= 2:
                    pe.wait_ge(once("carry"), c - 1)
                last = mm(u, bdU[:, c, :], ident, start=True, stop=(c == 0))
                if c:
                    pe.wait_ge(once("carry"), c)
                    last = mm(u, bdP[:, c - 1, :], carryT[:, c - 1, :], start=False, stop=True)
                last.then_inc(once("carried"), 1)
            pe.wait_ge(once("carry"), SEGS - 1)
            for c in range(1, SEGS):
                last = mm(outb[0][:, 64 + 8 * c:72 + 8 * c], carryT[:, c - 1, :], pread[:, 1, :, c], start=True, stop=True)
            last.then_inc(once("seg_out"), 1)
            pe.wait_ge(once("o_seq"), 1)
            mm(outb[1][:, 192:256], const("group"), oseq, start=True, stop=True).then_inc(once("gn_sum"), 1)
            pe.wait_ge(once("gn_sq"), 1)
            mm(outb[1][:, 256:320], const("group"), tmpA, start=True, stop=True).then_inc(once("gn_sqsum"), 1)
            pe.wait_ge(once("gated"), 1)
            mm(outb[0][0:N, 256:384], gated, W("W_o"), start=True, stop=True).then_inc(y_proj, 1)

            pe.wait_ge(once("x_int"), 1)
            nc.tensor.transpose(outb[0][:, 0:N], xint, ident[0:N, 0:N]).then_inc(once("x_intT"), 1)
            pe.wait_ge(once("x_intTc"), 1)
            mm(bank[0][0:N, :], xiT, wq[:, 0, :], start=True, stop=True)
            mm(bank[1][0:N, :], xiT, wq[:, 1, :], start=True, stop=True).then_inc(once("gate_up"), 1)
            pe.wait_ge(once("h_int"), 1)
            for f in range(FT):
                last = nc.tensor.transpose(outb[1][:, 64 * f:64 * f + 64], hint[:, 128 * f:128 * f + 128], ident[0:N, 0:N])
            last.then_inc(once("h_intT"), 1)
            pe.wait_ge(once("h_intTc"), 1)
            for f in range(FT):
                last = mm(outb[0][0:N, 256:384], hiT[:, f, :], wq[:, 2, 128 * f:128 * f + 128],
                          start=(f == 0), stop=(f == FT - 1))
            last.then_inc(y_proj, 1)

        @block.scalar
        def _(act):
            A = nc.scalar.activation

            def evac_keys(L):
                for i in range(ACH):
                    n = ACH * L + i
                    act.wait_ge(k_projd, n + 1)
                    if n >= 2:
                        act.wait_ge(k_cut, n - 1)
                        act.wait_ge(k_store[i % 2], 16 * (n // 2))
                    A(kfull[i % 2][:, :], bank[i % 2][:, 0:AW], ACT.Identity, bias=col(f"bk{L}"))
                    A(kparts[i % 2][:, 0, :], bank[i % 2][:, 0:AW], ACT.Identity,
                      bias=col(f"bk{L}")).then_inc(k_evac, 1)

            def evac_values(L, g):
                act.wait_ge(v_projd, VG * L + g + 1)
                if g == 0 and L == 1:
                    act.wait_ge(vp_ready, PAIRS)
                m = min(4, TILES - 4 * g)
                u = wide[g % 4 // 2][:, 512 * (g % 2):512 * (g % 2) + 128 * m]
                A(values[:, 4 * g:4 * g + m, :].rearrange("p t c -> p (t c)"), u, ACT.Copy).then_inc(v_evac, 1)

            def mask_high(c):
                s = slice(c * BW, (c + 1) * BW)
                if c >= 2:
                    act.wait_ge(m_parts, c - 1)
                A(mask_hm[:, s], mask[:, s], ACT.Copy).then_inc(m_high, 1)

            def mask_middle(c):
                s = slice(c * BW, (c + 1) * BW)
                act.wait_ge(m_rest, c + 1)
                A(mask_hm[64:128, s], mrest[c % 2][64:128, :], ACT.Copy).then_inc(m_mid, 1)

            def exps(L):
                for n in range(BCH * PAIRS * L, BCH * PAIRS * (L + 1)):
                    act.wait_ge(b_scored, n + 1)
                    if n >= 2:
                        act.wait_ge(pv_done, n - 1)
                    A(probs[n % 2][:, :], wide[n % 2][:, 0:BW], ACT.Exp).then_inc(exped, 1)

            act.wait_ge(ld_first, 64)
            evac_keys(0)
            act.wait_ge(ld_mask, 32)
            for g in range(VG):
                evac_values(0, g)
                if g < BCH:
                    mask_high(g)
                if 1 <= g <= BCH:
                    mask_middle(g - 1)
            exps(0)

            evac_keys(1)
            for g in range(VG):
                evac_values(1, g)
            act.wait_ge(once("self_shift"), 1)
            A(prob, prob, ACT.Exp, scale=SCALE).then_inc(once("self_exp0"), 1)
            act.wait_ge(ld_mask1, 32)
            act.wait_ge(b_scored, BCH * PAIRS)
            A(mask_hm[:, :], mask_lo[:, 0:T // 2].bitcast(u8), ACT.Copy, scale=-BIG).then_inc(m1_ready, 1)
            act.wait_ge(ld_rest, 32)
            act.wait_ge(x_ready, 1)
            for i, name in enumerate(("gate", "up", "down")):
                last = A(wq[:, i, :], W(name), ACT.Abs, accum_out=wabs[:, i:i + 1])
            last.then_inc(once("w_abs"), 1)
            exps(1)

            act.wait_ge(once("rwkv_proj"), 1)
            A(lmid[:, 0, :], bank[1][0:64, 0:64], ACT.Tanh)
            A(lmid[:, 1, :], bank[1][0:64, 64:128], ACT.Copy).then_inc(once("lora_mid"), 1)
            act.wait_ge(once("lora_out"), 1)
            act.wait_ge(once("neg_bias"), 1)
            for i in range(2):
                last = A(expo[:, i, :], bank[1][:, 128 + 64 * i:192 + 64 * i], ACT.Exp, scale=-1.0, bias=nbias[:, i:i + 1])
            last.then_inc(once("lora_exp"), 1)
            act.wait_ge(once("g_mid"), 1)
            A(gexp, outb[1][:, 0:64], ACT.Exp, scale=-1.0).then_inc(once("g_exp"), 1)
            for i, name in enumerate(("r", "w", "k", "a", "b")):
                act.wait_ge(once("bc_" + name), 1)
                src = [wide[0][:, 0:512], wide[0][:, 512:1024], wide[1][:, 0:512], wide[1][:, 512:1024], bank[0][:, 0:512]][i]
                last = A(along[:, i, :], src, ACT.Copy).then_inc(once("along"), 1)
            for c in range(SEGS - 1):
                act.wait_ge(once("carried"), c + 1)
                A(carryT[:, c, :], bank[c % 2][:, 0:128], ACT.Copy).then_inc(once("carry"), 1)
            act.wait_ge(once("gate_scaled"), 1)
            A(den_, gate_, ACT.Exp, scale=-1.0).then_inc(once("gate_exp"), 1)

        @block.vector
        def _(dve):
            V = nc.vector

            def step(ins):
                link("dve", dve, ins)

            def norm(k, double=False):
                x = xs[:, k, :]
                step(V.bn_stats(stat[:, 0:6], x))
                step(V.bn_aggr(stat[:, 6:8], stat[:, 0:6]))
                V.tensor_scalar_add(stat[:, 8:9], stat[:, 7:8], 1e-5).then_inc(ln_var, 1)
                dve.wait_ge(ln_rstd, k + 1)
                V.tensor_scalar(xn[:, :], x, stat[:, 6:7], stat[:, 9:10], ALU.subtract, ALU.mult).then_inc(ln_norm, 1)
                if k < 5:
                    dve.wait_ge(ln_T, k + 1)
                    V.tensor_copy(xnT[:, :, :], outb[0][:, 0:N].unsqueeze(1).broadcast_to([C, 2, N])).then_inc(ln_xT, 1)
                else:
                    dve.wait_ge(ln_norm, k + 1)

            def cut_keys(L):
                for i in range(ACH):
                    b = i % 2
                    dve.wait_ge(k_evac, ACH * L + i + 1)
                    step(V.tensor_tensor(kfull[b][:, :], kfull[b][:, :], kparts[b][:, 0, :], ALU.subtract))
                    step(V.tensor_copy(kparts[b][:, 1, :], kfull[b][:, :]))
                    V.tensor_tensor(kparts[b][:, 2, :], kfull[b][:, :], kparts[b][:, 1, :], ALU.subtract).then_inc(k_cut, 1)

            def queries(L):
                twice = lambda ap: ap.unsqueeze(1).broadcast_to([C, 2, N])
                dve.wait_ge(q_proj, L + 1)
                step(V.tensor_scalar(qT[:, :], outb[1][:, 0:N], col(f"bq{L}"), SCALE, ALU.add, ALU.mult))
                step(V.tensor_copy(qparts[:, 0, :, :], twice(qT[:, :])))
                step(V.tensor_tensor(qres[:, :], qT[:, :], qparts[:, 0, 0, :], ALU.subtract))
                step(V.tensor_copy(qparts[:, 1, :, :], twice(qres[:, :])))
                V.tensor_tensor(qparts[:, 2, :, :], twice(qres[:, :]), qparts[:, 1, :, :], ALU.subtract).then_inc(q_split, 1)
                dve.wait_ge(q_spread, L + 1)
                V.tensor_tensor(qstack[0:QK, :, :], wide[0][0:QK, :].rearrange("p (h n) -> p h n", n=128),
                                const("hmask", QK).unsqueeze(1).broadcast_to([QK, PAIRS, 128]), ALU.mult).then_inc(q_stack, 1)

            def maxima(L, p, a):
                g = PAIRS * L + p
                n = ACH * g + a
                dve.wait_ge(a_scored, n + 1)
                if n >= 2:
                    dve.wait_ge(a_maxed, n - 1)
                m = mask if L == 0 else mask_hm
                V.tensor_tensor_reduce(out=junk[:, a % 2, :], in0=bank[a % 2][:, 0:AW], in1=m[:, a * AW:(a + 1) * AW],
                                       scale=1.0, scalar=-3e38, op0=ALU.add, op1=ALU.max,
                                       accum_out=cmax[p % 2][:, a:a + 1]).then_inc(a_maxed, 1)

            def negate(L, p):
                g = PAIRS * L + p
                mc, mr = mcol[p % 2], mres[:, p % 2:p % 2 + 1]
                dve.wait_ge(a_maxed, ACH * (g + 1))
                step(V.reduce_max(pmax[:, p:p + 1], cmax[p % 2][:, :], AX.X))
                step(V.tensor_scalar(mc[:, QK:QK + 1], pmax[:, p:p + 1], -1.0, None, ALU.mult))
                step(V.scalar_tensor_tensor(out=mr, in0=pmax[:, p:p + 1], scalar=-1.0, in1=mc[:, QK:QK + 1],
                                            op0=ALU.mult, op1=ALU.subtract))
                step(V.tensor_copy(mc[:, QK + 1:QK + 2], mr))
                V.tensor_tensor(mc[:, QK + 2:QK + 3], mr, mc[:, QK + 1:QK + 2], ALU.subtract).then_inc(neg_max, 1)
                dve.wait_ge(neg_T, g + 1)
                V.tensor_copy(qstack[QK:QKM, p, :], outb[p % 2][QK:QKM, 128:256]).then_inc(q_full, 1)

            def save(L, p):
                g = PAIRS * L + p
                dve.wait_ge(pv_done, BCH * (g + 1))
                V.tensor_copy(outs[:, p, :], outb[p % 2][:, 0:128]).then_inc(o_saved, 1)

            def attention(L):
                if L == 0:
                    dve.wait_ge(ld_mask, 32)
                    dve.wait_ge(preset, 1)
                else:
                    dve.wait_ge(m1_ready, 1)
                for p in range(PAIRS):
                    for a in range(ACH):
                        maxima(L, p, a)
                        if a == 5 and p >= 2:
                            save(L, p - 2)
                    negate(L, p)
                save(L, PAIRS - 2)
                save(L, PAIRS - 1)

            def output(L):
                dve.wait_ge(o_comb, L + 1)
                heads = outb[0][0:N, 0:9 * H].rearrange("p (h e) -> p h e", e=9)
                o3 = o[:, :].rearrange("p (h e) -> p h e", e=D)
                step(V.reciprocal(rsum[:, :], heads[:, :, 8]))
                step(V.tensor_tensor(o3, heads[:, :, 0:8], rsum[:, :].unsqueeze(2).broadcast_to([N, H, D]), ALU.mult))
                if L == 1:
                    step(V.tensor_scalar(stat[:, 12:13], pmax[0:N, 0:1], -0.5 * BIG, 3e38, ALU.is_lt, ALU.mult))
                    step(V.tensor_scalar(stat[:, 13:14], stat[:, 12:13], 10.0, None, ALU.mult))
                    step(V.tensor_tensor(stat[:, 14:15], stat[:, 13:14], stat[:, 13:14], ALU.subtract))
                    step(V.tensor_scalar(o[:, :], o[:, :], stat[:, 14:15], None, ALU.add))
                V.tensor_tensor(o[:, :], o[:, :], row(f"bv{L}"), ALU.add).then_inc(o_norm, 1)
                copy_oT(2 * L + 1)

            def copy_oT(turn):
                dve.wait_ge(o_T, turn)
                V.tensor_copy(oT[:, :], outb[1][:, 0:N]).then_inc(o_Tc, 1)

            def residual(k, biased=True):
                dve.wait_ge(y_proj, k)
                if biased:
                    dve.wait_ge(x_res, k)
                V.tensor_tensor(xs[:, k, :], outb[0][0:N, 256:384], xb[:, :] if biased else xs[:, k - 1, :],
                                ALU.add).then_inc(x_ready, 1)
                dve.wait_ge(x_ready, k)

            dve.wait_ge(ld_first, 64)
            norm(0)
            cut_keys(0)
            queries(0)
            dve.wait_ge(ld_rest, 32)
            attention(0)
            output(0)
            residual(1)

            norm(1)
            cut_keys(1)
            dve.wait_ge(once("self_proj"), 1)
            proj = bank[0][:, 0:256].rearrange("p (a r n) -> p a r n", a=2, r=2)
            turn2 = lambda name: const(name).unsqueeze(1).broadcast_to([128, 2, N])
            V.tensor_tensor(v2, bank[1][:, 0:128], const("vmask"), ALU.mult)
            V.tensor_tensor(qkrot, proj[:, :, 0, :], turn2("cos"), ALU.mult)
            step(V.tensor_tensor(qksin, proj[:, :, 1, :], turn2("sin"), ALU.mult))
            step(V.tensor_tensor(qkrot, qkrot, qksin, ALU.add))
            V.tensor_tensor(kbd.rearrange("p (h n) -> p h n", h=H), qkrot[:, 1, :].unsqueeze(1).broadcast_to([128, H, N]),
                            const("head").unsqueeze(2).broadcast_to([128, H, N]), ALU.mult).then_inc(once("self_kbd"), 1)
            dve.wait_ge(once("self_scored"), 1)
            s3 = wide[0][0:N, :].rearrange("p (h n) -> p h n", h=H)
            p3 = prob.rearrange("p (h n) -> p h n", h=H)
            step(V.reduce_max(smax, s3, AX.X))
            V.tensor_tensor(p3, s3, smax.unsqueeze(2).broadcast_to([N, H, N]), ALU.subtract).then_inc(once("self_shift"), 1)
            dve.wait_ge(once("self_exp0"), 1)
            step(V.reduce_sum(smax, p3, AX.X))
            V.reciprocal(rsum[:, :], smax).then_inc(once("self_exp"), 1)
            dve.wait_ge(once("self_T"), 1)
            V.tensor_copy(probT, bank[0][:, :].rearrange("p (h n) -> p h n", h=PAIRS)).then_inc(once("self_Tc"), 1)
            dve.wait_ge(once("self_out"), 1)
            V.tensor_tensor(o[:, :].rearrange("p (h e) -> p h e", e=D),
                            bank[1][0:N, 128:256].rearrange("p (h e) -> p h e", e=D),
                            rsum[:, :].unsqueeze(2).broadcast_to([N, H, D]), ALU.mult).then_inc(o_norm, 1)
            copy_oT(2)
            residual(2)

            norm(2)
            dve.wait_ge(once("routed"), 1)
            mine = logit.unsqueeze(2).broadcast_to([N, H, H])
            other = logit.unsqueeze(1).broadcast_to([N, H, H])
            over3, even3 = (x.rearrange("p (i j) -> p i j", i=H) for x in (over, even))
            step(V.tensor_tensor(logit, bank[0][0:N, 0:H], row("router_b"), ALU.add))
            V.tensor_tensor(over3, other, mine, ALU.is_gt)
            step(V.tensor_tensor(even3, other, mine, ALU.is_equal))
            step(V.tensor_tensor(even, even, const("before", N), ALU.mult))
            step(V.tensor_tensor(over, over, even, ALU.add))
            step(V.reduce_sum(rank, over3, AX.X))
            V.tensor_scalar(fmask.rearrange("p (i b) -> p i b", i=H), rank.unsqueeze(2).broadcast_to([N, H, INNER // H]),
                            3.5, None, ALU.is_lt).then_inc(once("ff_mask"), 1)
            dve.wait_ge(once("ff_h"), 1)
            step(V.tensor_tensor(hpre.rearrange("p (f n) -> p f n", f=FT),
                                 bank[1][:, 0:256].rearrange("p (f n) -> p f n", f=FT),
                                 col("b1").unsqueeze(2).broadcast_to([128, FT, N]), ALU.add))
            dve.wait_ge(once("ff_maskT"), 1)
            V.scalar_tensor_tensor(out=hT_, in0=hpre, scalar=0.0, in1=outb[1][:, 0:256], op0=ALU.max,
                                   op1=ALU.mult).then_inc(once("ff_relu"), 1)
            residual(3)

            V.memset(ones, 1.0).then_inc(once("ones"), 1)
            dve.wait_ge(once("w_mean"), 1)
            step(V.tensor_scalar(wmean, outb[1][:, 0:3], 1.0 / (INNER * C), 1e-5, ALU.mult, ALU.max))
            step(V.reciprocal(winv, wmean))
            for i, name in enumerate(("gate", "up", "down")):
                V.tensor_scalar(wtmp[:, 0, :], W(name), winv[:, i:i + 1], 0.5, ALU.mult, ALU.is_gt)
                step(V.tensor_scalar(wtmp[:, 1, :], W(name), winv[:, i:i + 1], -0.5, ALU.mult, ALU.is_lt))
                step(V.tensor_tensor(wq[:, i, :], wtmp[:, 0, :], wtmp[:, 1, :], ALU.subtract))

            norm(3)
            queries(1)
            attention(1)
            output(1)
            residual(4)

            norm(4)
            x = xnT[:, 0, :]
            V.tensor_scalar(nbias, cols[:, COLS["w_bias"].start:COLS["w_bias"].start + 2], -1.0, None, ALU.mult).then_inc(once("neg_bias"), 1)
            dve.wait_ge(ln_xT, 5)
            V.tensor_scalar(delta[:, 0:1], x[:, 0:1], -1.0, None, ALU.mult)
            step(V.tensor_tensor(delta[:, 1:N], x[:, 0:N - 1], x[:, 1:N], ALU.subtract))
            for i, name in enumerate(("x_r", "x_k", "x_v", "x_w", "x_a")):
                last = V.scalar_tensor_tensor(out=mix[:, i, :], in0=delta, scalar=col(name), in1=x, op0=ALU.mult, op1=ALU.add)
            last.then_inc(once("mixed"), 1)
            dve.wait_ge(once("rwkv_proj"), 1)
            V.tensor_copy(rkv, bank[0][:, 0:192].rearrange("p (m n) -> p m n", m=3)).then_inc(once("rkv_copied"), 1)
            dve.wait_ge(once("rkv_copied"), 1)
            r, k, v = (rkv[:, i, :] for i in range(3))
            step(V.tensor_scalar(kk, k, col("k_k"), None, ALU.mult))
            V.tensor_tensor(tmpA, kk, kk, ALU.mult).then_inc(once("kk_squared"), 1)

            def spread(i, name, vec):
                V.tensor_tensor(diag[:, i, :].rearrange("p (n j) -> p n j", j=D), vec.unsqueeze(2).broadcast_to([128, N, D]),
                                const("eye8").unsqueeze(1).broadcast_to([128, N, D]), ALU.mult).then_inc(once("spread_" + name), 1)

            spread(0, "r", r)
            dve.wait_ge(once("kk_sum"), 1)
            V.tensor_scalar(kk_ss, outb[0][:, 0:64], 1e-24, None, ALU.max).then_inc(once("kk_sq"), 1)
            dve.wait_ge(once("lora_exp"), 1)
            step(V.tensor_scalar(expo, expo, 1.0, None, ALU.add))
            step(V.reciprocal(sig, expo))
            step(V.tensor_scalar(sig[:, 0, :], sig[:, 0, :], float(np.exp(-0.5)), None, ALU.mult))
            spread(1, "w", sig[:, 0, :])
            a = sig[:, 1, :]
            step(V.tensor_scalar(kmix, a, -1.0, col("k_a"), ALU.add, ALU.mult))
            step(V.scalar_tensor_tensor(out=kmix, in0=kmix, scalar=1.0, in1=k, op0=ALU.add, op1=ALU.mult))
            spread(2, "k", kmix)
            dve.wait_ge(once("kk_pow"), 1)
            step(V.scalar_tensor_tensor(out=nkk, in0=kk, scalar=-1.0, in1=kk_inv, op0=ALU.mult, op1=ALU.mult))
            spread(3, "a", nkk)
            step(V.scalar_tensor_tensor(out=bvec, in0=nkk, scalar=-1.0, in1=a, op0=ALU.mult, op1=ALU.mult))
            spread(4, "b", bvec)
            V.scalar_tensor_tensor(out=tmpB, in0=r, scalar=col("r_k"), in1=kmix, op0=ALU.mult, op1=ALU.mult).then_inc(once("rkk"), 1)
            dve.wait_ge(once("g_exp"), 1)
            step(V.tensor_scalar(gexp, gexp, 1.0, None, ALU.add))
            V.reciprocal(gsig, gexp).then_inc(once("g_sig"), 1)
            V.memset(first[:, :, 0, :], 0.0)
            step(V.tensor_copy(first[:, :, 1, :], const("eye8").unsqueeze(1).broadcast_to([128, SEGS, D])))
            dve.wait_ge(once("along"), 3)
            step(V.tensor_tensor(vk.rearrange("p (n j) -> p n j", j=D), v.unsqueeze(2).broadcast_to([128, N, D]),
                                 along[:, 2, :].rearrange("p (n j) -> p n j", j=D), ALU.mult))
            dve.wait_ge(once("along"), 5)

            def at(vec, s, y=True):
                u = vec.rearrange("p (c s j) -> p s c j", c=SEGS, s=STEPS)[:, s, :, :]
                return u.unsqueeze(2).broadcast_to([128, SEGS, 2, D]) if y else u

            before = first
            for s in range(STEPS):
                after = states[:, s, :, :, :]
                V.tensor_tensor(prod2, before, at(along[:, 1, :], s), ALU.mult)
                step(V.tensor_tensor(prod, before, at(along[:, 3, :], s), ALU.mult))
                step(V.reduce_sum(sa, prod, AX.X))
                step(V.tensor_tensor(prod, sa.unsqueeze(3).broadcast_to([128, SEGS, 2, D]), at(along[:, 4, :], s), ALU.mult))
                step(V.tensor_tensor(after, prod, prod2, ALU.add))
                step(V.tensor_tensor(after[:, :, 0, :], after[:, :, 0, :], at(vk, s, False), ALU.add))
                before = after
            for kind, dst, c0 in ((0, bdU, 0), (1, bdP, 1)):
                m = SEGS - 1 - c0
                last = V.tensor_tensor(dst.rearrange("p c (h j) -> p c h j", h=H),
                                       states[:, STEPS - 1, c0:SEGS - 1, kind, :].unsqueeze(2).broadcast_to([128, m, H, D]),
                                       const("head").unsqueeze(1).unsqueeze(3).broadcast_to([128, m, H, D]), ALU.mult)
            last.then_inc(once("seg_blocks"), 1)
            for y in range(2):
                last = V.tensor_tensor(rd[:, y, :].rearrange("p (s c j) -> p s c j", s=STEPS, c=SEGS), states[:, :, :, y, :],
                                       along[:, 0, :].rearrange("p (c s j) -> p s c j", c=SEGS, s=STEPS), ALU.mult)
            step(last)
            V.reduce_sum(pread.rearrange("p y s c -> p (y s c)"), rd.rearrange("p y (n j) -> p (y n) j", j=D), AX.X).then_inc(once("reads_done"), 1)
            dve.wait_ge(once("reads_done"), 1)
            dve.wait_ge(once("seg_out"), 1)
            V.tensor_copy(oseq[:, 0:8], pread[:, 0, :, 0])
            V.tensor_tensor(oseq[:, 8:64].rearrange("p (c s) -> p c s", s=STEPS),
                            outb[0][:, 72:128].rearrange("p (c s) -> p c s", s=STEPS),
                            pread[:, 0, :, 1:SEGS].rearrange("p s c -> p c s"), ALU.add).then_inc(once("o_seq"), 1)
            dve.wait_ge(once("gn_sum"), 1)
            step(V.scalar_tensor_tensor(out=oseq, in0=outb[1][:, 192:256], scalar=-1.0 / D, in1=oseq, op0=ALU.mult, op1=ALU.add))
            step(V.tensor_tensor(bonus, outb[1][:, 128:192], v, ALU.mult))
            V.tensor_tensor(tmpA, oseq, oseq, ALU.mult).then_inc(once("gn_sq"), 1)
            dve.wait_ge(once("gn_sqsum"), 1)
            V.tensor_scalar(gn_v, outb[1][:, 256:320], 1.0 / D, 1e-5, ALU.mult, ALU.add).then_inc(once("gn_var"), 1)
            dve.wait_ge(once("gn_pow"), 1)
            step(V.tensor_tensor(onrm, oseq, gn_rstd, ALU.mult))
            step(V.tensor_scalar(onrm, onrm, col("gn_w"), col("gn_b"), ALU.mult, ALU.add))
            step(V.tensor_tensor(onrm, onrm, bonus, ALU.add))
            V.scalar_tensor_tensor(out=gated, in0=outb[1][:, 64:128], scalar=col("g_bias"), in1=onrm, op0=ALU.add,
                                   op1=ALU.mult).then_inc(once("gated"), 1)
            residual(5, biased=False)

            MAGIC = 1.5 * 2.0 ** 23

            def quantise(src, tmp, dst, at0):
                step(V.scalar_tensor_tensor(out=tmp, in0=src, scalar=-1.0, in1=src, op0=ALU.mult, op1=ALU.max))
                step(V.reduce_max(am[:, at0:at0 + 1], tmp, AX.X))
                step(V.tensor_scalar(am[:, at0:at0 + 1], am[:, at0:at0 + 1], 1e-5, None, ALU.max))
                V.tensor_scalar(am[:, at0 + 1:at0 + 2], am[:, at0:at0 + 1], 1.0 / 127.0, None, ALU.mult)
                step(V.reciprocal(am[:, at0 + 2:at0 + 3], am[:, at0:at0 + 1]))
                step(V.tensor_scalar(am[:, at0 + 2:at0 + 3], am[:, at0 + 2:at0 + 3], 127.0, None, ALU.mult))
                step(V.tensor_scalar(tmp, src, am[:, at0 + 2:at0 + 3], MAGIC, ALU.mult, ALU.add))
                step(V.tensor_scalar(tmp, tmp, MAGIC, 127.0, ALU.subtract, ALU.min))
                return V.tensor_scalar(dst, tmp, -128.0, None, ALU.max)

            norm(5)
            quantise(xn[:, :], absx, xint, 0).then_inc(once("x_int"), 1)
            dve.wait_ge(once("x_intT"), 1)
            V.tensor_copy(xiT, outb[0][:, 0:N]).then_inc(once("x_intTc"), 1)
            step(V.tensor_scalar(am[:, 6:8], wmean[0:N, 0:2], am[:, 1:2], None, ALU.mult))
            dve.wait_ge(once("gate_up"), 1)
            V.tensor_scalar(gate_, bank[0][0:N, :], am[:, 6:7], None, ALU.mult).then_inc(once("gate_scaled"), 1)
            dve.wait_ge(once("gate_scaled"), 1)
            step(V.scalar_tensor_tensor(out=up_, in0=bank[1][0:N, :], scalar=am[:, 7:8], in1=gate_, op0=ALU.mult, op1=ALU.mult))
            dve.wait_ge(once("gate_exp"), 1)
            step(V.tensor_scalar(den_, den_, 1.0, None, ALU.add))
            step(V.reciprocal(den_, den_))
            step(V.tensor_tensor(up_, up_, den_, ALU.mult))
            quantise(up_, gate_, hint, 3).then_inc(once("h_int"), 1)
            dve.wait_ge(once("h_intT"), 1)
            V.tensor_copy(hiT, outb[1][:, 0:256].rearrange("p (f n) -> p f n", f=FT)).then_inc(once("h_intTc"), 1)
            step(V.tensor_scalar(am[:, 6:7], wmean[0:N, 2:3], am[:, 4:5], None, ALU.mult))
            dve.wait_ge(y_proj, 6)
            V.scalar_tensor_tensor(out=xs[:, 6, :], in0=outb[0][0:N, 256:384], scalar=am[:, 6:7], in1=xs[:, 5, :],
                                   op0=ALU.mult, op1=ALU.add).then_inc(x_ready, 1)


def constants():
    f = np.zeros((128, N_CF), np.float32)
    p = np.arange(128)
    f[:, CF["ident"]] = np.eye(128)
    f[:, CF["group"]] = p[:, None] // D == p[None, :] // D
    r = np.arange(QK)
    f[:QK, CF["hmask"]] = (r[:, None] % 16) // D == p[None, :] // N
    for hh in range(2):
        for e in range(9):
            f[p % 32 == 9 * hh + e, CF["comb"].start + 9 * hh + e] = 1
    f[:, CF["head"]] = p[:, None] // D == np.arange(H)[None, :]
    f[:, CF["vmask"]] = p[:, None] // N == (p[None, :] // D) % 2
    theta = (1.0 / 10000.0 ** (np.arange(0, D, 2, dtype=np.float32) / D)).astype(np.float32)
    angle = np.outer(np.arange(N, dtype=np.float32), theta).astype(np.float32)
    angle = np.concatenate([angle, angle], axis=-1)
    f[:, CF["cos"]] = np.cos(angle).T[p % D]
    f[:, CF["sin"]] = np.sin(angle).T[p % D] * np.where(p % D < D // 2, -1, 1)[:, None]
    i = np.arange(H)
    f[:, CF["before"]] = (i[None, :] < i[:, None]).reshape(1, H * H)
    f[:, CF["eye8"]] = p[:, None] % D == np.arange(D)[None, :]
    b = np.zeros((128, N_CB), np.float32)
    b[:, CB["ident"]] = np.eye(128)
    b[:, CB["rep"]] = p[:, None] % N == p[None, :] % N
    b[:, CB["half"]] = 0.5 * (p[:, None] % N == p[None, :] % N)
    spread = np.zeros((128, 3, PAIRS, QK), np.float32)
    for j, part in enumerate(Q_PART):
        for h in range(PAIRS):
            for e in range(16):
                spread[16 * h + e, part, h, 16 * j + e] = 1
    b[:, CB["spread"]] = spread.reshape(128, -1)
    return f, b


def kernel(**inputs):
    import concourse.bacc as _bacc
    import ml_dtypes
    from concourse import mybir as _mybir
    from concourse.bass_utils import run_bass_kernel_spmd as _run

    v = {n: np.asarray(a) for n, a in inputs.items()}
    qkv = v["L0_attn_w_qkv"]
    turned = (np.arange(C) // D) * D + (np.arange(C) + D // 2) % D

    def pad(a):
        return np.concatenate([a, np.zeros((128 - a.shape[0], a.shape[1]), a.dtype)], axis=0)

    def by_rows(a):
        return a.reshape(FT, 128, C).transpose(1, 0, 2).reshape(128, FT * C)

    parts = {
        "aq": qkv[:, 0:C], "aqr": qkv[:, 0:C][:, turned], "ak": qkv[:, C:2 * C], "akr": qkv[:, C:2 * C][:, turned],
        "av": qkv[:, 2 * C:3 * C], "aout": v["L0_attn_w_out"], "router": v["L0_ffn_router_w"].T,
        "w1": v["L0_ffn_w1"].T, "w2": by_rows(v["L0_ffn_w2"].T), "W_r": v["L1_attn_W_r"], "W_k": v["L1_attn_W_k"],
        "W_v": v["L1_attn_W_v"], "W_o": v["L1_attn_W_o"], "wla": v["L1_attn_w_lora_a"], "wlb": pad(v["L1_attn_w_lora_b"]),
        "ala": v["L1_attn_a_lora_a"], "alb": pad(v["L1_attn_a_lora_b"]), "gla": v["L1_attn_g_lora_a"],
        "glb": v["L1_attn_g_lora_b"], "gate": v["L1_ffn_w_gate"].T, "up": v["L1_ffn_w_up"].T,
        "down": by_rows(v["L1_ffn_w_down"].T),
    }
    for L in range(2):
        for m in "qkvo":
            parts[f"W{m}{L}"] = v[f"L{L}_xattn_W{m}"].T
    columns = {
        "bk0": v["L0_xattn_bk"], "bq0": v["L0_xattn_bq"], "bk1": v["L1_xattn_bk"], "bq1": v["L1_xattn_bq"],
        "x_r": v["L1_attn_x_r"], "x_w": v["L1_attn_x_w"], "x_k": v["L1_attn_x_k"], "x_v": v["L1_attn_x_v"],
        "x_a": v["L1_attn_x_a"], "k_k": v["L1_attn_k_k"], "k_a": v["L1_attn_k_a"], "r_k": v["L1_attn_r_k"].reshape(C),
        "w_bias": v["L1_attn_w_lora_bias"], "a_bias": v["L1_attn_a_lora_bias"], "g_bias": v["L1_attn_g_lora_bias"],
        "gn_w": v["L1_attn_gn_weight"], "gn_b": v["L1_attn_gn_bias"],
    }
    columns = {n: a[:, None] for n, a in columns.items()}
    columns["b1"] = v["L0_ffn_b1"].reshape(FT, 128).T
    bias_rows = {"bv0": v["L0_xattn_bv"], "bo0": v["L0_xattn_bo"], "bv1": v["L1_xattn_bv"], "bo1": v["L1_xattn_bo"],
                 "b_out": v["L0_attn_b_out"], "b2": v["L0_ffn_b2"], "router_b": v["L0_ffn_router_b"]}
    cf, cb = constants()
    arrays = {
        "x": v["x"][0], "ctxT": v["ctx_1024"][0].T, "mask0": v["mask_BxSxS2_ff0"][0],
        "mask1": v["mask_SxS2_bk1"].view(np.int32),
        "weights": np.concatenate([parts[n] for n in WCOLS], axis=1),
        "columns": np.concatenate([columns[n] for n in COLS], axis=1),
        "rows": np.concatenate([bias_rows[n] for n in ROWS])[None, :],
        "tables": cf, "tables_bf16": cb.astype(ml_dtypes.bfloat16),
    }
    arrays = {n: np.ascontiguousarray(a) for n, a in arrays.items()}
    nc = _bacc.Bacc("TRN2", target_bir_lowering=False, num_devices=1)
    args = [nc.dram_tensor("in_" + n, a.shape, _mybir.dt.from_np(a.dtype), kind="ExternalInput").ap() for n, a in arrays.items()]
    out = nc.dram_tensor("out", (N, C), _mybir.dt.float32, kind="ExternalOutput").ap()
    program(nc, *args, out)
    r = _run(nc, [{"in_" + n: a for n, a in arrays.items()}], core_ids=[0])
    return r.results[0]["out"].reshape(1, N, C)
```

```python
import numpy as np
import concourse.bass as bass
from concourse import mybir
from contextlib import ExitStack

N, C, T = 64, 128, 6272
H, D = 16, 8
PAIRS = H // 2
TILES = T // 128
BCH, BT = 7, TILES // 7
BW = BT * 128
ACH = 14
AW = T // ACH
CUT = 6 * AW
VG = (TILES + 3) // 4
UNITS = ACH + VG
INNER = 512
FT = INNER // 128
STEPS, SEGS = 8, N // 8
BIG = 1e30
SCALE = float(1.0 / np.sqrt(np.float32(D)))
Q_PART = [0, 1, 2, 0, 1, 0]
K_PART = [0, 0, 0, 1, 1, 2]
QK = len(Q_PART) * 2 * D
QKM = QK + 3

WCOLS = {}
def _lay(names, into, start=0):
    for n, w in names:
        into[n] = slice(start, start + w)
        start += w
    return start

W_EARLY = _lay([("Wk0", C), ("Wv0", C), ("Wq0", C), ("Wo0", C)], WCOLS)
W_ALL = _lay([("Wk1", C), ("Wv1", C), ("Wq1", C), ("Wo1", C), ("aq", C), ("aqr", C), ("ak", C), ("akr", C),
              ("av", C), ("aout", C), ("router", H), ("w1", INNER), ("w2", INNER), ("W_r", C), ("W_k", C),
              ("W_v", C), ("W_o", C), ("wla", 64), ("wlb", C), ("ala", 64), ("alb", C), ("gla", C),
              ("glb", C), ("gate", INNER), ("up", INNER), ("down", INNER)], WCOLS, W_EARLY)
COLS = {}
N_COLS = _lay([("bk0", 1), ("bq0", 1), ("bk1", 1), ("bq1", 1), ("b1", FT), ("x_r", 1), ("x_w", 1), ("x_k", 1),
               ("x_v", 1), ("x_a", 1), ("k_k", 1), ("k_a", 1), ("r_k", 1), ("w_bias", 1), ("a_bias", 1),
               ("g_bias", 1), ("gn_w", 1), ("gn_b", 1)], COLS)
ROWS = {}
N_ROWS = _lay([("bv0", C), ("bo0", C), ("bv1", C), ("bo1", C), ("b_out", C), ("b2", C), ("router_b", H)], ROWS)
CF = {}
N_CF = _lay([("ident", 128), ("group", 128), ("hmask", 128), ("comb", 18), ("head", H), ("vmask", 128),
             ("cos", N), ("sin", N), ("before", H * H), ("eye8", D)], CF)
CB = {}
N_CB = _lay([("ident", 128), ("rep", 128), ("half", 128), ("spread", 3 * PAIRS * QK)], CB)


def program(nc, x_d, ctx_d, mask0_d, mask1_d, w_d, cols_d, rows_d, cf_d, cb_d, out_d):
    fp32, bf16, u8, i32 = mybir.dt.float32, mybir.dt.bfloat16, mybir.dt.uint8, mybir.dt.int32
    ALU, ACT, AX = mybir.AluOpType, mybir.ActivationFunctionType, mybir.AxisListType

    ctx = ExitStack()
    with ctx:
        def sb(name, shape, dt=fp32):
            return ctx.enter_context(nc.sbuf_tensor(name, shape, dt))

        bank = [ctx.enter_context(nc.psum_tensor(f"bank{i}", [128, 512], fp32)) for i in range(2)]
        wide = [ctx.enter_context(nc.psum_tensor(f"wide{i}", [128, 1024], fp32)) for i in range(2)]
        outb = [ctx.enter_context(nc.psum_tensor(f"outb{i}", [128, 512], fp32)) for i in range(2)]

        w = sb("w", [128, W_ALL])
        cols = sb("cols", [128, N_COLS])
        rows = sb("rows", [N, N_ROWS])
        cf = sb("cf", [128, N_CF])
        cb = sb("cb", [128, N_CB], bf16)
        ctxT = sb("ctxT", [128, T])
        keys = [sb(f"keys{i}", [128, T], bf16) for i in range(2)]
        mask = sb("mask", [128, T])
        mask_hm = sb("mask_hm", [128, T], bf16)
        mask_lo = sb("mask_lo", [128, T], bf16)
        values = sb("values", [128, TILES, C])
        vpair = [sb(f"vpair{i}", [128, TILES, 32]) for i in range(2)]
        probs = [sb(f"probs{i}", [128, BW]) for i in range(2)]
        kfull = [sb(f"kfull{i}", [128, AW]) for i in range(2)]
        kparts = [sb(f"kparts{i}", [128, 3, AW], bf16) for i in range(2)]
        mrest = [sb(f"mrest{i}", [128, BW]) for i in range(2)]
        qstack = sb("qstack", [128, PAIRS, 128], bf16)
        qparts = sb("qparts", [128, 3, 2, N], bf16)
        outs = sb("outs", [128, PAIRS, 128])
        junk = sb("junk", [128, 2, AW], bf16)
        cmax = [sb(f"cmax{i}", [128, ACH]) for i in range(2)]
        pmax = sb("pmax", [128, PAIRS])
        mcol = [sb(f"mcol{i}", [128, QKM], bf16) for i in range(2)]
        mres = sb("mres", [128, 2])
        xs = sb("xs", [N, 7, C])
        xb = sb("xb", [N, C])
        xn = sb("xn", [N, C])
        xnT = sb("xnT", [C, 2, N])
        qT = sb("qT", [C, N])
        qres = sb("qres", [C, N])
        stat = sb("stat", [N, 16])
        mhalf = sb("mhalf", [128, N])
        o = sb("o", [N, C])
        oT = sb("oT", [C, N])
        rsum = sb("rsum", [N, H])
        place = {"mask": 0, "ctxT": 0, "values": 0}
        home = {"mask": mask[:, :], "ctxT": ctxT[:, :], "values": values[:, :, :].rearrange("p t c -> p (t c)")}

        def take(where, n, parts=128):
            a = place[where]
            place[where] = a + n
            return home[where][0:parts, a:a + n]

        wq = take("mask", 3 * INNER // 2).bitcast(bf16).rearrange("p (m f) -> p m f", m=3)
        wabs, wmean, winv, ones = take("mask", 3), take("mask", 3), take("mask", 3), take("mask", 128)
        wtmp = take("mask", 2 * INNER).rearrange("p (a f) -> p a f", a=2)
        more_parts = [take("mask", 3 * AW // 2).bitcast(bf16).rearrange("p (j t) -> p j t", j=3) for _ in range(2)]
        begin = place["mask"]
        qkrot = take("mask", 128).rearrange("p (a n) -> p a n", a=2)
        qksin = take("mask", 128).rearrange("p (a n) -> p a n", a=2)
        qrot = qkrot[:, 0, :]
        kbd = take("mask", H * N)
        prob = take("mask", H * N, N)
        smax = take("mask", H, N)
        probT = take("mask", PAIRS * N).rearrange("p (h n) -> p h n", h=PAIRS)
        v2 = take("mask", C)
        place["mask"] = begin
        logit, rank = take("mask", H, N), take("mask", H, N)
        over, even = take("mask", H * H, N), take("mask", H * H, N)
        fmask = take("mask", INNER // 2, N).bitcast(bf16)
        hpre, hT_ = take("mask", FT * N), take("mask", FT * N)
        hT = hT_.rearrange("p (f n) -> p f n", f=FT)
        place["mask"] = begin
        delta = take("mask", N)
        mix = take("mask", 5 * N).rearrange("p (m n) -> p m n", m=5)
        lmid = take("mask", 2 * N, 64).rearrange("p (m n) -> p m n", m=2)
        rkv = take("mask", 3 * N).rearrange("p (m n) -> p m n", m=3)
        sig = take("mask", 2 * N).rearrange("p (m n) -> p m n", m=2)
        expo = take("mask", 2 * N).rearrange("p (m n) -> p m n", m=2)
        nbias = take("mask", 2)
        gexp, gsig, kk, kk_ss, kk_inv, nkk, bvec, kmix, tmpA, tmpB = [take("mask", N) for _ in range(10)]
        oseq, gn_v, gn_rstd, gated, onrm, bonus = [take("mask", N) for _ in range(6)]
        sa = take("mask", SEGS * 2).rearrange("p (c y) -> p c y", c=SEGS)
        prod = take("mask", SEGS * 2 * D).rearrange("p (c y j) -> p c y j", c=SEGS, y=2)
        prod2 = take("mask", SEGS * 2 * D).rearrange("p (c y j) -> p c y j", c=SEGS, y=2)
        first = take("mask", SEGS * 2 * D).rearrange("p (c y j) -> p c y j", c=SEGS, y=2)
        diag = take("ctxT", 5 * N * D).rearrange("p (v n) -> p v n", v=5)
        bdU = take("ctxT", (SEGS - 1) * 128).rearrange("p (c n) -> p c n", n=128)
        bdP = take("ctxT", (SEGS - 2) * 128).rearrange("p (c n) -> p c n", n=128)
        carryT = take("ctxT", (SEGS - 1) * 128).rearrange("p (c n) -> p c n", n=128)
        along = take("values", 5 * N * D).rearrange("p (v n) -> p v n", v=5)
        vk = take("values", N * D)
        states = take("values", STEPS * SEGS * 2 * D).rearrange("p (s c y j) -> p s c y j", s=STEPS, c=SEGS, y=2)
        rd = take("values", 2 * N * D).rearrange("p (y n) -> p y n", y=2)
        pread = take("values", 2 * N).rearrange("p (y s c) -> p y s c", y=2, s=STEPS)
        absx, xint = take("values", C, N), take("values", C, N)
        xiT = take("values", N // 2).bitcast(bf16)
        am = take("values", 8, N)
        place["ctxT"] = 0
        gate_, up_, den_, hint = [take("ctxT", INNER, N) for _ in range(4)]
        hiT = take("values", FT * N // 2).bitcast(bf16).rearrange("p (f n) -> p f n", f=FT)
        kscr = [nc.dram_tensor(f"key_parts{i}", [3, 128, T], bf16, kind="Internal").ap() for i in range(2)]

        def W(name):
            return w[:, WCOLS[name]]

        def col(name):
            return cols[:, COLS[name]]

        def row(name):
            return rows[:, ROWS[name]]

        def const(name, n=128):
            return cf[0:n, CF[name]]

        def constb(name, n=128):
            return cb[0:n, CB[name]]

        def sem(name):
            return ctx.enter_context(nc.semaphore(name))

        ld_first, ld_rest, ld_bf, ld_mask1, stored = map(sem, (
            "ld_first", "ld_rest", "ld_bf", "ld_mask1", "stored"))
        ld_mask = [sem(f"ld_mask0_{i}") for i in range(BCH)]
        ld_ctx = [sem(f"ld_ctx{i}") for i in range(4)]
        k_load = [[sem(f"k_load{s}_{h}") for h in range(2)] for s in range(2)]
        k_store = [sem(f"k_store{i}") for i in range(6)]
        (ln_var, ln_rstd, ln_norm, ln_T, ln_xT, x_res, x_ready) = map(sem, (
            "ln_var", "ln_rstd", "ln_norm", "ln_T", "ln_xT", "x_res", "x_ready"))
        (q_proj, q_split, q_spread, q_stack, projd, evac, k_rest, k_mid, k_cut) = map(sem, (
            "q_proj", "q_split", "q_spread", "q_stack", "projd", "evac", "k_rest", "k_mid", "k_cut"))
        (a_scored, a_maxed, neg_max, neg_T, q_full, b_scored, exped, pv_done, vp_ready, o_saved) = map(sem, (
            "a_scored", "a_maxed", "neg_max", "neg_T", "q_full", "b_scored", "exped", "pv_done", "vp_ready",
            "o_saved"))
        (o_comb, o_norm, o_T, o_Tc, y_proj) = map(sem, ("o_comb", "o_norm", "o_T", "o_Tc", "y_proj"))
        (preset, m_high, m_rest, m_mid, m_parts, m1_ready) = map(sem, (
            "preset", "m_high", "m_rest", "m_mid", "m_parts", "m1_ready"))
        chain = {e: sem(f"{e}_chain") for e in ("dve", "act", "pool")}
        count = {e: 0 for e in chain}
        named = {}

        def once(name):
            if name not in named:
                named[name] = sem(name)
            return named[name]

        def link(which, eng, ins):
            count[which] += 1
            ins.then_inc(chain[which], 1)
            eng.wait_ge(chain[which], count[which])

        def pieces():
            return [(0, 4 * AW), (4 * AW, 8 * AW), (8 * AW, 12 * AW), (12 * AW, T)]

        def ctx_piece(c1):
            return (c1 - 1) // (4 * AW)

        def units(L):
            k, v = 0, 0
            for u in range(UNITS):
                if k < ACH and (L == 0 or u % 3 < 2):
                    yield "k", k
                    k += 1
                else:
                    yield "v", v
                    v += 1

        PLAN = [list(units(L)) for L in range(2)]
        BEFORE_A = 9
        MASKS_FROM = 8
        RING = [6, 4]
        EARLY = 4

        def unit_bank(L, u):
            if L == 0:
                return wide[u % 4 // 2][:, 512 * (u % 2):512 * (u % 2) + 512]
            if u < EARLY:
                return bank[u % 2][:, :]
            return wide[1][:, 512 * (u % 2):512 * (u % 2) + 512]

        def key_ring(L, i):
            f, r = i % 4, i % RING[L]
            if f < 2:
                full = kfull[f][:, :]
            else:
                full = (probs if L == 0 else mrest)[f - 2][:, 0:AW]
            if r < 2:
                parts = kparts[r][:, :, :]
            elif L == 0:
                parts = keys[1][:, 3 * AW * (r - 2):3 * AW * (r - 1)].rearrange("p (j t) -> p j t", j=3)
            else:
                parts = more_parts[r - 2]
            return full, parts, k_store[r], 16 * (i // RING[L] + (stored_by(r, ACH) if L else 0))

        def stored_by(r, n):
            return len(range(r, n, RING[0]))

        pair_of_ones = float(np.array([0x3F803F80], np.uint32).view(np.float32)[0])
        block = ctx.enter_context(nc.Block())

        @block.sync
        def _(sp):
            def load_ctx(i):
                a, b = pieces()[i]
                sp.dma_start(ctxT[:, a:b], ctx_d[:, a:b]).then_inc(ld_ctx[i], 16)

            sp.dma_start(xs[:, 0, :], x_d).then_inc(ld_first, 16)
            sp.dma_start(w[:, 0:W_EARLY], w_d[:, 0:W_EARLY]).then_inc(ld_first, 16)
            sp.dma_start(cols[:, :], cols_d).then_inc(ld_first, 16)
            sp.dma_start(cf[:, :], cf_d).then_inc(ld_first, 16)
            for i in range(4):
                load_ctx(i)
            sp.dma_start(cb[:, :], cb_d).then_inc(ld_bf, 16)

            def load_mask(piece):
                a, b = BW * piece, BW * (piece + 1)
                for half in range(2):
                    sp.dma_start(mask[64 * half:64 * half + 64, a:b], mask0_d[:, a:b]).then_inc(ld_mask[piece], 16)


            def load_keys(L, p, piece):
                g = PAIRS * L + p
                a, b = [(0, CUT), (CUT, T)][piece]
                if g >= 2:
                    sp.wait_ge(b_scored, BCH * (g - 2) + (3 if piece == 0 else BCH))
                for j, part in enumerate(K_PART):
                    sp.dma_start(keys[g % 2][16 * j:16 * j + 16, a:b],
                                 kscr[L][part, 16 * p:16 * p + 16, a:b]).then_inc(k_load[g % 2][piece], 16)

            for L in range(2):
                for i in range(ACH):
                    if L == 1 and i == 2:
                        sp.wait_ge(x_ready, 1)
                        for half in range(2):
                            sp.dma_start(mask_lo[64 * half:64 * half + 64, 0:T // 2].bitcast(i32),
                                         mask1_d).then_inc(ld_mask1, 16)
                    _, parts, store, before = key_ring(L, i)
                    sp.wait_ge(k_cut, ACH * L + i + 1)
                    sp.dma_start(kscr[L][:, :, i * AW:(i + 1) * AW].rearrange("j p t -> p j t"),
                                 parts).then_inc(store, 16)
                    if L == 0 and i < BCH:
                        load_mask(i)
                    if L == 0 and i == CUT // AW + 2:
                        for r in range(RING[0]):
                            sp.wait_ge(k_store[r], 16 * stored_by(r, CUT // AW))
                        load_keys(0, 0, 0)
                for i in range(ACH - RING[L], ACH):
                    _, _, store, before = key_ring(L, i)
                    sp.wait_ge(store, before + 16)
                for p in range(PAIRS):
                    for piece in range(2):
                        if (L, p, piece) != (0, 0, 0):
                            load_keys(L, p, piece)
                    if L == 0 and p == 1:
                        sp.dma_start(rows[:, :], rows_d.broadcast_to([N, N_ROWS])).then_inc(ld_rest, 16)
                        sp.dma_start(w[:, W_EARLY:W_ALL], w_d[:, W_EARLY:W_ALL]).then_inc(ld_rest, 16)
            sp.wait_ge(x_ready, 6)
            sp.dma_start(out_d, xs[:, 6, :]).then_inc(stored, 16)
            sp.wait_ge(stored, 16)

        @block.gpsimd
        def _(pool):
            def fill(ap, value):
                link("pool", pool, pool.memset(ap, value))

            def ln_power(k):
                pool.wait_ge(ln_var, k + 1)
                pool.tensor_tensor(stat[:, 9:10], stat[:, 8:9], mhalf[0:N, 0:1], ALU.pow).then_inc(ln_rstd, 1)
                pool.wait_ge(ln_rstd, k + 1)

            def add_bias(k, name):
                pool.wait_ge(x_ready, k)
                if k == 0:
                    pool.wait_ge(ld_first, 64)
                    pool.wait_ge(ld_rest, 32)
                pool.tensor_tensor(xb[:, :], xs[:, k, :], row(name), ALU.add).then_inc(x_res, 1)
                pool.wait_ge(x_res, k + 1)

            fill(mhalf[:, :], -0.5)
            ln_power(0)
            for i in range(2):
                heads = vpair[i][:, :, 0:18].rearrange("p t (h e) -> p t h e", e=9)
                fill(vpair[i][:, :, 18:32], 0.0)
                fill(heads[:, :, :, 8:9], 1.0)
                fill(mcol[i][:, :], 0.0)
            fill(mask_lo[0:64, :].bitcast(fp32), 0.0)

            def mask_rest(c):
                s = slice(c * BW, (c + 1) * BW)
                pool.wait_ge(m_high, c + 1)
                pool.tensor_tensor(mrest[c % 2][64:128, :], mask[64:128, s], mask_hm[64:128, s],
                                   ALU.subtract).then_inc(m_rest, 1)
                pool.wait_ge(m_rest, c + 1)

            mask_rest(0)
            for c in range(BCH):
                s = slice(c * BW, (c + 1) * BW)
                if c + 1 < BCH:
                    mask_rest(c + 1)
                pool.wait_ge(m_mid, c + 1)
                pool.tensor_tensor(mask_lo[64:128, s], mrest[c % 2][64:128, :], mask_hm[64:128, s],
                                   ALU.subtract).then_inc(m_parts, 1)
                pool.wait_ge(m_parts, c + 1)

            def pair_values(L):
                for p in range(PAIRS):
                    if (L, p) == (0, 1):
                        for r in range(2, RING[0]):
                            pool.wait_ge(k_store[r], 16 * stored_by(r, ACH))
                        pool.memset(keys[1][QK:QKM, :].bitcast(fp32), pair_of_ones).then_inc(preset, 1)
                        pool.wait_ge(preset, 1)
                    g = PAIRS * L + p
                    if p == 0:
                        pool.wait_ge(evac, UNITS * (L + 1))
                    if g >= 2:
                        pool.wait_ge(pv_done, BCH * (g - 1))
                    pool.tensor_copy(
                        vpair[g % 2][:, :, 0:18].rearrange("p t (h e) -> p t h e", e=9)[:, :, :, 0:8],
                        values[:, :, 16 * p:16 * p + 16].rearrange("p t (h e) -> p t h e", e=8)
                    ).then_inc(vp_ready, 1)
                    pool.wait_ge(vp_ready, g + 1)

            def cut_keys(chunks):
                for i in chunks:
                    full, parts, store, before = key_ring(1, i)
                    pool.wait_ge(evac, UNITS + PLAN[1].index(("k", i)) + 1)
                    link("pool", pool, pool.tensor_tensor(parts[:, 1, :], full, parts[:, 0, :], ALU.subtract))
                    link("pool", pool, pool.tensor_tensor(full, full, parts[:, 0, :], ALU.subtract))
                    pool.tensor_tensor(parts[:, 2, :], full, parts[:, 1, :], ALU.subtract).then_inc(k_cut, 1)
                    pool.wait_ge(k_cut, ACH + i + 1)

            pair_values(0)
            cut_keys(range(0, 2))
            add_bias(0, "bo0")
            cut_keys(range(2, 3))
            ln_power(1)
            add_bias(1, "b_out")
            cut_keys(range(3, 7))
            ln_power(2)
            add_bias(2, "b2")
            cut_keys(range(7, 9))
            ln_power(3)
            cut_keys(range(9, ACH))
            pair_values(1)
            add_bias(3, "bo1")
            ln_power(4)
            pool.wait_ge(once("kk_sq"), 1)
            pool.tensor_tensor(kk_inv, kk_ss, mhalf[:, :], ALU.pow).then_inc(once("kk_pow"), 1)
            pool.wait_ge(once("kk_pow"), 1)
            pool.wait_ge(once("gn_var"), 1)
            pool.tensor_tensor(gn_rstd, gn_v, mhalf[:, :], ALU.pow).then_inc(once("gn_pow"), 1)
            pool.wait_ge(once("gn_pow"), 1)
            ln_power(5)

        @block.tensor
        def _(pe):
            mm = nc.tensor.matmul
            ident = const("ident")

            def ln_transpose(k):
                pe.wait_ge(ln_norm, k + 1)
                nc.tensor.transpose(outb[0][:, 0:N], xn[:, :], ident[0:N, 0:N]).then_inc(ln_T, 1)

            def project(L, u):
                kind, i = PLAN[L][u]
                n = UNITS * L + u
                dst = unit_bank(L, u)
                if L == 0:
                    pe.wait_ge(ld_ctx[ctx_piece((i + 1) * AW if kind == "k" else min(T, 512 * (i + 1)))], 16)
                    if u >= 4:
                        pe.wait_ge(evac, n - 3)
                elif u >= 2:
                    pe.wait_ge(evac, n - 1)
                if kind == "k":
                    last = mm(dst[:, 0:AW], W(f"Wk{L}"), ctxT[:, i * AW:(i + 1) * AW], start=True, stop=True)
                else:
                    for t in range(4 * i, min(4 * i + 4, TILES)):
                        last = mm(dst[:, 128 * (t % 4):128 * (t % 4) + 128], ctxT[:, 128 * t:128 * t + 128],
                                  W(f"Wv{L}"), start=True, stop=True)
                last.then_inc(projd, 1)

            upto = [0, 0]

            def more(L, n):
                for u in range(upto[L], min(upto[L] + n, UNITS)):
                    if L == 1 and u == 0:
                        pe.wait_ge(ld_rest, 32)
                    if L == 1 and u < 2:
                        pe.wait_ge(a_maxed, ACH * PAIRS)
                    if L == 1 and u == EARLY:
                        pe.wait_ge(exped, BCH * PAIRS)
                    project(L, u)
                upto[L] = max(upto[L], min(upto[L] + n, UNITS))

            def queries(L):
                pe.wait_ge(ln_xT, 1 if L == 0 else 4)
                mm(outb[1][:, 0:N], W(f"Wq{L}"), xnT[:, 0, :], start=True, stop=True).then_inc(q_proj, 1)
                more(L, ACH if L == 0 else 2)
                pe.wait_ge(q_split, L + 1)
                pe.wait_ge(ld_bf, 16)
                spread = constb("spread").rearrange("p (i h r) -> p i h r", i=3, r=QK)
                for p in range(PAIRS):
                    for i in range(3):
                        last = mm(bank[p // 4][0:QK, 128 * (p % 4):128 * (p % 4) + 128], spread[:, i, p, :], qparts[:, i, :, :],
                                  start=(i == 0), stop=(i == 2))
                last.then_inc(q_spread, 1)
                more(L, UNITS - BEFORE_A - upto[0] if L == 0 else 1)

            def pass_a(L, p, a):
                g = PAIRS * L + p
                n = ACH * g + a
                if a == 0:
                    pe.wait_ge(k_load[p % 2][0], 96 * (g // 2 + 1))
                if a == CUT // AW:
                    pe.wait_ge(k_load[p % 2][1], 96 * (g // 2 + 1))
                if n >= 2:
                    pe.wait_ge(a_maxed, n - 1)
                mm(bank[a % 2][:, 0:AW], qstack[0:QK, p, :], keys[p % 2][0:QK, a * AW:(a + 1) * AW],
                   start=True, stop=True).then_inc(a_scored, 1)

            def max_rows(L, p):
                g = PAIRS * L + p
                pe.wait_ge(neg_max, g + 1)
                if g >= 2:
                    pe.wait_ge(o_saved, g - 1)
                mm(outb[p % 2][0:QKM, 128:256], mcol[p % 2][:, :], constb("ident"),
                   start=True, stop=True).then_inc(neg_T, 1)

            def pass_b(L, p, c, tiles):
                g = PAIRS * L + p
                n = BCH * g + c
                if 0 in tiles:
                    if c == 0:
                        pe.wait_ge(q_full, g + 1)
                        if g == 1:
                            pe.wait_ge(preset, 1)
                        if p == 0:
                            pe.wait_ge(evac, UNITS * (L + 1))
                    if g == 0:
                        pe.wait_ge(m_parts, c + 1)
                    if n >= 2:
                        pe.wait_ge(exped, n - 1)
                for i in tiles:
                    t = slice(128 * (BT * c + i), 128 * (BT * c + i) + 128)
                    u = wide[n % 2][:, 128 * i:128 * i + 128]
                    mm(u, keys[p % 2][0:QKM, t], qstack[0:QKM, p, :], start=True, stop=False)
                    if L == 0:
                        mm(u, mask_hm[:, t], constb("rep"), start=False, stop=False)
                        last = mm(u, mask_lo[:, t], constb("rep"), start=False, stop=True)
                    else:
                        last = mm(u, mask_hm[:, t], constb("half"), start=False, stop=True)
                if BT - 1 in tiles:
                    last.then_inc(b_scored, 1)

            def weigh(L, p, c):
                g = PAIRS * L + p
                n = BCH * g + c
                if c == 0:
                    pe.wait_ge(vp_ready, g + 1)
                pe.wait_ge(exped, n + 1)
                for i in range(BT):
                    t = BT * c + i
                    q = 32 * (t % 4)
                    last = mm(outb[p % 2][q:q + 32, 0:128], vpair[p % 2][:, t, :],
                              probs[n % 2][:, 128 * i:128 * i + 128], start=(t < 4), stop=(t >= TILES - 4))
                last.then_inc(pv_done, 1)

            A_PLAN = [3, 3, 3, 3, 2, 0, 0]

            def attention(L):
                pe.wait_ge(q_stack, L + 1)
                if L == 1:
                    pe.wait_ge(m1_ready, 1)
                for a in range(ACH):
                    pass_a(L, 0, a)
                    more(L, 1)
                max_rows(L, 0)
                for p in range(PAIRS):
                    todo = iter(range(ACH) if p + 1 < PAIRS else ())

                    def next_a(wanted):
                        if wanted:
                            pass_a(L, p + 1, next(todo))

                    for c in range(BCH):
                        n = A_PLAN[c] if p + 1 < PAIRS else 0
                        next_a(n > 0)
                        pass_b(L, p, c, range(0, 4))
                        next_a(n > 1)
                        pass_b(L, p, c, range(4, BT))
                        next_a(n > 2)
                        if c:
                            weigh(L, p, c - 1)
                        elif p:
                            weigh(L, p - 1, BCH - 1)
                        if c == 5 and p + 1 < PAIRS:
                            max_rows(L, p + 1)
                        if L == 0 and p == PAIRS - 1 and c in (0, 2, 4, 6):
                            more(1, 1)
                weigh(L, PAIRS - 1, BCH - 1)

            def output(L):
                comb = const("comb").rearrange("p (h e) -> p h e", h=2)
                pe.wait_ge(o_saved, PAIRS * (L + 1))
                for h in range(H):
                    last = mm(outb[0][0:N, 9 * h:9 * h + 9], outs[:, h // 2, 64 * (h % 2):64 * (h % 2) + 64],
                              comb[:, h % 2, :], start=True, stop=True)
                last.then_inc(o_comb, 1)
                if L == 0:
                    more(1, 1)
                project_out(2 * L + 1, f"Wo{L}")

            def project_out(turn, name):
                pe.wait_ge(o_norm, turn)
                nc.tensor.transpose(outb[1][:, 0:N], o[:, :], ident[0:N, 0:N]).then_inc(o_T, 1)
                pe.wait_ge(o_Tc, turn)
                mm(outb[0][0:N, 256:384], oT[:, :], W(name), start=True, stop=True).then_inc(y_proj, 1)

            pe.wait_ge(ld_first, 64)
            ln_transpose(0)
            queries(0)
            attention(0)
            output(0)

            more(1, 2)
            ln_transpose(1)
            pe.wait_ge(ln_xT, 2)
            pe.wait_ge(evac, UNITS + EARLY)
            for i, name in enumerate(("aq", "aqr", "ak", "akr")):
                mm(bank[0][:, 64 * i:64 * i + 64], W(name), xnT[:, 0, :], start=True, stop=True)
            mm(bank[1][:, 0:128], xnT[:, :, :], W("av"), start=True, stop=True).then_inc(once("self_proj"), 1)
            more(1, 2)
            pe.wait_ge(once("self_kbd"), 1)
            for i in range(2):
                last = mm(wide[0][0:N, 512 * i:512 * i + 512], qrot, kbd[:, 512 * i:512 * i + 512],
                          start=True, stop=True)
            last.then_inc(once("self_scored"), 1)
            more(1, 4)
            pe.wait_ge(once("self_exp"), 1)
            for p in range(PAIRS):
                last = nc.tensor.transpose(bank[0][:, 64 * p:64 * p + 64], prob[:, 128 * p:128 * p + 128],
                                           ident[0:N, 0:N])
            last.then_inc(once("self_T"), 1)
            pe.wait_ge(once("self_Tc"), 1)
            for p in range(PAIRS):
                last = mm(bank[1][0:N, 128 + 16 * p:144 + 16 * p], probT[:, p, :], v2[:, 16 * p:16 * p + 16],
                          start=True, stop=True)
            last.then_inc(once("self_out"), 1)
            project_out(2, "aout")

            more(1, 2)
            ln_transpose(2)
            pe.wait_ge(ln_xT, 3)
            mm(bank[0][0:N, 0:H], xnT[:, 0, :], W("router"), start=True, stop=True).then_inc(once("routed"), 1)
            for f in range(FT):
                last = mm(bank[1][:, 64 * f:64 * f + 64], w[:, WCOLS["w1"].start + 128 * f:WCOLS["w1"].start + 128 * f + 128],
                          xnT[:, 0, :], start=True, stop=True)
            last.then_inc(once("ff_h"), 1)
            more(1, 2)
            pe.wait_ge(once("ff_mask"), 1)
            for f in range(FT):
                last = mm(outb[1][:, 64 * f:64 * f + 64], fmask[:, 128 * f:128 * f + 128], constb("ident", N)[:, 0:N],
                          start=True, stop=True)
            last.then_inc(once("ff_maskT"), 1)
            pe.wait_ge(once("ff_relu"), 1)
            for f in range(FT):
                last = mm(outb[0][0:N, 256:384], hT[:, f, :], w[:, WCOLS["w2"].start + 128 * f:WCOLS["w2"].start + 128 * f + 128],
                          start=(f == 0), stop=(f == FT - 1))
            last.then_inc(y_proj, 1)

            pe.wait_ge(once("w_abs"), 1)
            pe.wait_ge(once("ones"), 1)
            mm(outb[1][:, 0:3], ones, wabs, start=True, stop=True).then_inc(once("w_mean"), 1)

            more(1, 2)
            ln_transpose(3)
            queries(1)
            attention(1)
            output(1)

            ln_transpose(4)
            pe.wait_ge(once("mixed"), 1)
            for i, name in enumerate(("W_r", "W_k", "W_v")):
                mm(bank[0][:, 64 * i:64 * i + 64], W(name), mix[:, i, :], start=True, stop=True)
            mm(bank[1][0:64, 0:64], W("wla"), mix[:, 3, :], start=True, stop=True)
            mm(bank[1][0:64, 64:128], W("ala"), mix[:, 4, :], start=True, stop=True).then_inc(once("rwkv_proj"), 1)
            pe.wait_ge(once("lora_mid"), 1)
            mm(bank[1][:, 128:192], w[0:64, WCOLS["wlb"]], lmid[:, 0, :], start=True, stop=True)
            mm(bank[1][:, 192:256], w[0:64, WCOLS["alb"]], lmid[:, 1, :], start=True, stop=True).then_inc(once("lora_out"), 1)
            pe.wait_ge(once("rkv_copied"), 1)
            mm(outb[1][:, 0:64], W("gla"), rkv[:, 0, :], start=True, stop=True).then_inc(once("g_mid"), 1)
            pe.wait_ge(once("kk_squared"), 1)
            mm(outb[0][:, 0:64], const("group"), tmpA, start=True, stop=True).then_inc(once("kk_sum"), 1)
            pe.wait_ge(once("g_sig"), 1)
            mm(outb[1][:, 64:128], W("glb"), gsig, start=True, stop=True).then_inc(once("g_out"), 1)
            for i, name in enumerate(("r", "w", "k", "a", "b")):
                pe.wait_ge(once("spread_" + name), 1)
                dst = [wide[0][:, 0:512], wide[0][:, 512:1024], wide[1][:, 0:512], wide[1][:, 512:1024], bank[0][:, 0:512]][i]
                mm(dst, const("group"), diag[:, i, :], start=True, stop=True).then_inc(once("bc_" + name), 1)
            pe.wait_ge(once("rkk"), 1)
            mm(outb[1][:, 128:192], const("group"), tmpB, start=True, stop=True).then_inc(once("bonus_sum"), 1)
            pe.wait_ge(once("seg_blocks"), 1)
            pe.wait_ge(once("reads_done"), 1)
            for c in range(SEGS - 1):
                u = bank[c % 2][:, 0:128]
                if c >= 2:
                    pe.wait_ge(once("carry"), c - 1)
                last = mm(u, bdU[:, c, :], ident, start=True, stop=(c == 0))
                if c:
                    pe.wait_ge(once("carry"), c)
                    last = mm(u, bdP[:, c - 1, :], carryT[:, c - 1, :], start=False, stop=True)
                last.then_inc(once("carried"), 1)
            pe.wait_ge(once("carry"), SEGS - 1)
            for c in range(1, SEGS):
                last = mm(outb[0][:, 64 + 8 * c:72 + 8 * c], carryT[:, c - 1, :], pread[:, 1, :, c], start=True, stop=True)
            last.then_inc(once("seg_out"), 1)
            pe.wait_ge(once("o_seq"), 1)
            mm(outb[1][:, 192:256], const("group"), oseq, start=True, stop=True).then_inc(once("gn_sum"), 1)
            pe.wait_ge(once("gn_sq"), 1)
            mm(outb[1][:, 256:320], const("group"), tmpA, start=True, stop=True).then_inc(once("gn_sqsum"), 1)
            pe.wait_ge(once("gated"), 1)
            mm(outb[0][0:N, 256:384], gated, W("W_o"), start=True, stop=True).then_inc(y_proj, 1)

            pe.wait_ge(once("x_int"), 1)
            nc.tensor.transpose(outb[0][:, 0:N], xint, ident[0:N, 0:N]).then_inc(once("x_intT"), 1)
            pe.wait_ge(once("x_intTc"), 1)
            pe.wait_ge(once("ternary"), 3)
            mm(bank[0][0:N, :], xiT, wq[:, 0, :], start=True, stop=True)
            mm(bank[1][0:N, :], xiT, wq[:, 1, :], start=True, stop=True).then_inc(once("gate_up"), 1)
            pe.wait_ge(once("h_int"), 1)
            for f in range(FT):
                last = nc.tensor.transpose(outb[1][:, 64 * f:64 * f + 64], hint[:, 128 * f:128 * f + 128], ident[0:N, 0:N])
            last.then_inc(once("h_intT"), 1)
            pe.wait_ge(once("h_intTc"), 1)
            for f in range(FT):
                last = mm(outb[0][0:N, 256:384], hiT[:, f, :], wq[:, 2, 128 * f:128 * f + 128],
                          start=(f == 0), stop=(f == FT - 1))
            last.then_inc(y_proj, 1)

        @block.scalar
        def _(act):
            A = nc.scalar.activation

            def evacuate(L, u):
                kind, i = PLAN[L][u]
                src = unit_bank(L, u)
                act.wait_ge(projd, UNITS * L + u + 1)
                if kind == "k":
                    full, parts, store, before = key_ring(L, i)
                    if i >= 4:
                        act.wait_ge(k_cut, ACH * L + i - 3)
                    if before:
                        act.wait_ge(store, before)
                    A(full, src[:, 0:AW], ACT.Identity, bias=col(f"bk{L}"))
                    A(parts[:, 0, :], src[:, 0:AW], ACT.Identity, bias=col(f"bk{L}")).then_inc(evac, 1)
                else:
                    if i == 0 and L == 1:
                        act.wait_ge(vp_ready, PAIRS)
                    m = min(4, TILES - 4 * i)
                    A(values[:, 4 * i:4 * i + m, :].rearrange("p t c -> p (t c)"), src[:, 0:128 * m],
                      ACT.Copy).then_inc(evac, 1)

            def mask_high(c):
                s = slice(c * BW, (c + 1) * BW)
                A(mask_hm[:, s], mask[:, s], ACT.Copy).then_inc(m_high, 1)

            def mask_middle(c):
                s = slice(c * BW, (c + 1) * BW)
                act.wait_ge(m_rest, c + 1)
                A(mask_hm[64:128, s], mrest[c % 2][64:128, :], ACT.Copy).then_inc(m_mid, 1)

            def exps(L):
                for n in range(BCH * PAIRS * L, BCH * PAIRS * (L + 1)):
                    act.wait_ge(b_scored, n + 1)
                    if n >= 2:
                        act.wait_ge(pv_done, n - 1)
                    A(probs[n % 2][:, :], wide[n % 2][:, 0:BW], ACT.Exp).then_inc(exped, 1)
                    late = n - BCH * (PAIRS - 1)
                    if L == 0 and late in (0, 2, 4, 6):
                        evacuate(1, late // 2)

            act.wait_ge(ld_first, 64)
            m = 0
            for u in range(UNITS):
                evacuate(0, u)
                if u >= MASKS_FROM and u % 2 == 0 and m <= BCH:
                    if m < BCH:
                        act.wait_ge(ld_mask[m], 32)
                        mask_high(m)
                    if m:
                        mask_middle(m - 1)
                    m += 1
            exps(0)
            for u in range(EARLY, 12):
                evacuate(1, u)
            act.wait_ge(once("self_shift"), 1)
            A(prob, prob, ACT.Exp, scale=SCALE).then_inc(once("self_exp0"), 1)
            for u in range(12, 17):
                evacuate(1, u)
            act.wait_ge(ld_rest, 32)
            act.wait_ge(x_ready, 1)
            for i, name in enumerate(("gate", "up", "down")):
                last = A(wq[:, i, :], W(name), ACT.Abs, accum_out=wabs[:, i:i + 1])
            last.then_inc(once("w_abs"), 1)
            act.wait_ge(ld_mask1, 32)
            act.wait_ge(b_scored, BCH * PAIRS)
            A(mask_hm[:, :], mask_lo[:, 0:T // 2].bitcast(u8), ACT.Copy, scale=-BIG).then_inc(m1_ready, 1)
            for u in range(17, UNITS):
                evacuate(1, u)
            exps(1)

            act.wait_ge(once("rwkv_proj"), 1)
            A(lmid[:, 0, :], bank[1][0:64, 0:64], ACT.Tanh)
            A(lmid[:, 1, :], bank[1][0:64, 64:128], ACT.Copy).then_inc(once("lora_mid"), 1)
            act.wait_ge(once("lora_out"), 1)
            act.wait_ge(once("neg_bias"), 1)
            for i in range(2):
                last = A(expo[:, i, :], bank[1][:, 128 + 64 * i:192 + 64 * i], ACT.Exp, scale=-1.0, bias=nbias[:, i:i + 1])
            last.then_inc(once("lora_exp"), 1)
            act.wait_ge(once("g_mid"), 1)
            A(gexp, outb[1][:, 0:64], ACT.Exp, scale=-1.0).then_inc(once("g_exp"), 1)
            for i, name in enumerate(("r", "w", "k", "a", "b")):
                act.wait_ge(once("bc_" + name), 1)
                src = [wide[0][:, 0:512], wide[0][:, 512:1024], wide[1][:, 0:512], wide[1][:, 512:1024], bank[0][:, 0:512]][i]
                last = A(along[:, i, :], src, ACT.Copy).then_inc(once("along"), 1)
            for c in range(SEGS - 1):
                act.wait_ge(once("carried"), c + 1)
                A(carryT[:, c, :], bank[c % 2][:, 0:128], ACT.Copy).then_inc(once("carry"), 1)
            act.wait_ge(once("gate_scaled"), 1)
            A(den_, gate_, ACT.Exp, scale=-1.0).then_inc(once("gate_exp"), 1)

        @block.vector
        def _(dve):
            V = nc.vector

            def step(ins):
                link("dve", dve, ins)

            def norm(k, double=False):
                x = xs[:, k, :]
                step(V.bn_stats(stat[:, 0:6], x))
                step(V.bn_aggr(stat[:, 6:8], stat[:, 0:6]))
                V.tensor_scalar_add(stat[:, 8:9], stat[:, 7:8], 1e-5).then_inc(ln_var, 1)
                dve.wait_ge(ln_rstd, k + 1)
                V.tensor_scalar(xn[:, :], x, stat[:, 6:7], stat[:, 9:10], ALU.subtract, ALU.mult).then_inc(ln_norm, 1)
                if k < 5:
                    dve.wait_ge(ln_T, k + 1)
                    V.tensor_copy(xnT[:, :, :], outb[0][:, 0:N].unsqueeze(1).broadcast_to([C, 2, N])).then_inc(ln_xT, 1)
                else:
                    dve.wait_ge(ln_norm, k + 1)

            def cut_keys(chunks):
                for i in chunks[::2]:
                    (full0, parts0), (full1, parts1) = key_ring(0, i)[0:2], key_ring(0, i + 1)[0:2]
                    dve.wait_ge(evac, PLAN[0].index(("k", i)) + 1)
                    V.tensor_tensor(full0, full0, parts0[:, 0, :], ALU.subtract).then_inc(k_rest, 1)
                    dve.wait_ge(evac, PLAN[0].index(("k", i + 1)) + 1)
                    V.tensor_tensor(full1, full1, parts1[:, 0, :], ALU.subtract).then_inc(k_rest, 1)
                    dve.wait_ge(k_rest, i + 1)
                    V.tensor_copy(parts0[:, 1, :], full0).then_inc(k_mid, 1)
                    dve.wait_ge(k_rest, i + 2)
                    V.tensor_copy(parts1[:, 1, :], full1).then_inc(k_mid, 1)
                    dve.wait_ge(k_mid, i + 1)
                    V.tensor_tensor(parts0[:, 2, :], full0, parts0[:, 1, :], ALU.subtract).then_inc(k_cut, 1)
                    dve.wait_ge(k_mid, i + 2)
                    V.tensor_tensor(parts1[:, 2, :], full1, parts1[:, 1, :], ALU.subtract).then_inc(k_cut, 1)

            def queries(L):
                twice = lambda ap: ap.unsqueeze(1).broadcast_to([C, 2, N])
                dve.wait_ge(q_proj, L + 1)
                step(V.tensor_scalar(qT[:, :], outb[1][:, 0:N], col(f"bq{L}"), SCALE, ALU.add, ALU.mult))
                step(V.tensor_copy(qparts[:, 0, :, :], twice(qT[:, :])))
                step(V.tensor_tensor(qres[:, :], qT[:, :], qparts[:, 0, 0, :], ALU.subtract))
                step(V.tensor_copy(qparts[:, 1, :, :], twice(qres[:, :])))
                V.tensor_tensor(qparts[:, 2, :, :], twice(qres[:, :]), qparts[:, 1, :, :], ALU.subtract).then_inc(q_split, 1)

            def stack_queries(L):
                dve.wait_ge(q_spread, L + 1)
                for i in range(2):
                    last = V.tensor_tensor(qstack[0:QK, 4 * i:4 * i + 4, :],
                                           bank[i][0:QK, :].rearrange("p (h n) -> p h n", n=128),
                                           const("hmask", QK).unsqueeze(1).broadcast_to([QK, 4, 128]), ALU.mult)
                last.then_inc(q_stack, 1)

            def maxima(L, p, a):
                g = PAIRS * L + p
                n = ACH * g + a
                dve.wait_ge(a_scored, n + 1)
                if n >= 2:
                    dve.wait_ge(a_maxed, n - 1)
                m = mask if L == 0 else mask_hm
                V.tensor_tensor_reduce(out=junk[:, a % 2, :], in0=bank[a % 2][:, 0:AW], in1=m[:, a * AW:(a + 1) * AW],
                                       scale=1.0, scalar=-3e38, op0=ALU.add, op1=ALU.max,
                                       accum_out=cmax[p % 2][:, a:a + 1]).then_inc(a_maxed, 1)

            def negate(L, p):
                g = PAIRS * L + p
                mc, mr = mcol[p % 2], mres[:, p % 2:p % 2 + 1]
                dve.wait_ge(a_maxed, ACH * (g + 1))
                step(V.reduce_max(pmax[:, p:p + 1], cmax[p % 2][:, :], AX.X))
                step(V.tensor_scalar(mc[:, QK:QK + 1], pmax[:, p:p + 1], -1.0, None, ALU.mult))
                step(V.scalar_tensor_tensor(out=mr, in0=pmax[:, p:p + 1], scalar=-1.0, in1=mc[:, QK:QK + 1],
                                            op0=ALU.mult, op1=ALU.subtract))
                step(V.tensor_copy(mc[:, QK + 1:QK + 2], mr))
                V.tensor_tensor(mc[:, QK + 2:QK + 3], mr, mc[:, QK + 1:QK + 2], ALU.subtract).then_inc(neg_max, 1)
                dve.wait_ge(neg_T, g + 1)
                V.tensor_copy(qstack[QK:QKM, p, :], outb[p % 2][QK:QKM, 128:256]).then_inc(q_full, 1)

            def ternary(i):
                name = ("gate", "up", "down")[i]
                V.tensor_scalar(wtmp[:, 0, :], W(name), winv[:, i:i + 1], 0.5, ALU.mult, ALU.is_gt)
                step(V.tensor_scalar(wtmp[:, 1, :], W(name), winv[:, i:i + 1], -0.5, ALU.mult, ALU.is_lt))
                V.tensor_tensor(wq[:, i, :], wtmp[:, 0, :], wtmp[:, 1, :], ALU.subtract).then_inc(once("ternary"), 1)

            def save(L, p):
                g = PAIRS * L + p
                dve.wait_ge(pv_done, BCH * (g + 1))
                V.tensor_copy(outs[:, p, :], outb[p % 2][:, 0:128]).then_inc(o_saved, 1)

            def attention(L):
                if L == 0:
                    for piece in range(BCH):
                        dve.wait_ge(ld_mask[piece], 32)
                else:
                    dve.wait_ge(m1_ready, 1)
                for p in range(PAIRS):
                    for a in range(ACH):
                        maxima(L, p, a)
                        if a == 5 and p >= 2:
                            save(L, p - 2)
                        if L == 1 and a == 8 and 1 <= p <= 3:
                            ternary(p - 1)
                    negate(L, p)
                save(L, PAIRS - 2)
                save(L, PAIRS - 1)

            def output(L):
                dve.wait_ge(o_comb, L + 1)
                heads = outb[0][0:N, 0:9 * H].rearrange("p (h e) -> p h e", e=9)
                o3 = o[:, :].rearrange("p (h e) -> p h e", e=D)
                step(V.reciprocal(rsum[:, :], heads[:, :, 8]))
                step(V.tensor_tensor(o3, heads[:, :, 0:8], rsum[:, :].unsqueeze(2).broadcast_to([N, H, D]), ALU.mult))
                if L == 1:
                    step(V.tensor_scalar(stat[:, 12:13], pmax[0:N, 0:1], -0.5 * BIG, 3e38, ALU.is_lt, ALU.mult))
                    step(V.tensor_scalar(stat[:, 13:14], stat[:, 12:13], 10.0, None, ALU.mult))
                    step(V.tensor_tensor(stat[:, 14:15], stat[:, 13:14], stat[:, 13:14], ALU.subtract))
                    step(V.tensor_scalar(o[:, :], o[:, :], stat[:, 14:15], None, ALU.add))
                V.tensor_tensor(o[:, :], o[:, :], row(f"bv{L}"), ALU.add).then_inc(o_norm, 1)
                copy_oT(2 * L + 1)

            def copy_oT(turn):
                dve.wait_ge(o_T, turn)
                V.tensor_copy(oT[:, :], outb[1][:, 0:N]).then_inc(o_Tc, 1)

            def residual(k, biased=True):
                dve.wait_ge(y_proj, k)
                if biased:
                    dve.wait_ge(x_res, k)
                V.tensor_tensor(xs[:, k, :], outb[0][0:N, 256:384], xb[:, :] if biased else xs[:, k - 1, :],
                                ALU.add).then_inc(x_ready, 1)
                dve.wait_ge(x_ready, k)

            V.memset(keys[0][QK:QKM, :].bitcast(fp32), pair_of_ones)
            dve.wait_ge(ld_first, 64)
            norm(0)
            queries(0)
            cut_keys(range(0, 10))
            stack_queries(0)
            cut_keys(range(10, ACH))
            attention(0)
            output(0)
            residual(1)

            norm(1)
            dve.wait_ge(once("self_proj"), 1)
            proj = bank[0][:, 0:256].rearrange("p (a r n) -> p a r n", a=2, r=2)
            turn2 = lambda name: const(name).unsqueeze(1).broadcast_to([128, 2, N])
            V.tensor_tensor(v2, bank[1][:, 0:128], const("vmask"), ALU.mult)
            V.tensor_tensor(qkrot, proj[:, :, 0, :], turn2("cos"), ALU.mult)
            step(V.tensor_tensor(qksin, proj[:, :, 1, :], turn2("sin"), ALU.mult))
            step(V.tensor_tensor(qkrot, qkrot, qksin, ALU.add))
            V.tensor_tensor(kbd.rearrange("p (h n) -> p h n", h=H), qkrot[:, 1, :].unsqueeze(1).broadcast_to([128, H, N]),
                            const("head").unsqueeze(2).broadcast_to([128, H, N]), ALU.mult).then_inc(once("self_kbd"), 1)
            dve.wait_ge(once("self_scored"), 1)
            s3 = wide[0][0:N, :].rearrange("p (h n) -> p h n", h=H)
            p3 = prob.rearrange("p (h n) -> p h n", h=H)
            step(V.reduce_max(smax, s3, AX.X))
            V.tensor_tensor(p3, s3, smax.unsqueeze(2).broadcast_to([N, H, N]), ALU.subtract).then_inc(once("self_shift"), 1)
            dve.wait_ge(once("self_exp0"), 1)
            step(V.reduce_sum(smax, p3, AX.X))
            V.reciprocal(rsum[:, :], smax).then_inc(once("self_exp"), 1)
            dve.wait_ge(once("self_T"), 1)
            V.tensor_copy(probT, bank[0][:, :].rearrange("p (h n) -> p h n", h=PAIRS)).then_inc(once("self_Tc"), 1)
            dve.wait_ge(once("self_out"), 1)
            V.tensor_tensor(o[:, :].rearrange("p (h e) -> p h e", e=D),
                            bank[1][0:N, 128:256].rearrange("p (h e) -> p h e", e=D),
                            rsum[:, :].unsqueeze(2).broadcast_to([N, H, D]), ALU.mult).then_inc(o_norm, 1)
            copy_oT(2)
            residual(2)

            norm(2)
            dve.wait_ge(once("routed"), 1)
            mine = logit.unsqueeze(2).broadcast_to([N, H, H])
            other = logit.unsqueeze(1).broadcast_to([N, H, H])
            over3, even3 = (x.rearrange("p (i j) -> p i j", i=H) for x in (over, even))
            step(V.tensor_tensor(logit, bank[0][0:N, 0:H], row("router_b"), ALU.add))
            V.tensor_tensor(over3, other, mine, ALU.is_gt)
            step(V.tensor_tensor(even3, other, mine, ALU.is_equal))
            step(V.tensor_tensor(even, even, const("before", N), ALU.mult))
            step(V.tensor_tensor(over, over, even, ALU.add))
            step(V.reduce_sum(rank, over3, AX.X))
            V.tensor_scalar(fmask.rearrange("p (i b) -> p i b", i=H), rank.unsqueeze(2).broadcast_to([N, H, INNER // H]),
                            3.5, None, ALU.is_lt).then_inc(once("ff_mask"), 1)
            dve.wait_ge(once("ff_h"), 1)
            step(V.tensor_tensor(hpre.rearrange("p (f n) -> p f n", f=FT),
                                 bank[1][:, 0:256].rearrange("p (f n) -> p f n", f=FT),
                                 col("b1").unsqueeze(2).broadcast_to([128, FT, N]), ALU.add))
            dve.wait_ge(once("ff_maskT"), 1)
            V.scalar_tensor_tensor(out=hT_, in0=hpre, scalar=0.0, in1=outb[1][:, 0:256], op0=ALU.max,
                                   op1=ALU.mult).then_inc(once("ff_relu"), 1)
            residual(3)

            V.memset(ones, 1.0).then_inc(once("ones"), 1)
            dve.wait_ge(once("w_mean"), 1)
            step(V.tensor_scalar(wmean, outb[1][:, 0:3], 1.0 / (INNER * C), 1e-5, ALU.mult, ALU.max))
            step(V.reciprocal(winv, wmean))
            norm(3)
            queries(1)
            stack_queries(1)
            attention(1)
            output(1)
            residual(4)

            norm(4)
            x = xnT[:, 0, :]
            V.tensor_scalar(nbias, cols[:, COLS["w_bias"].start:COLS["w_bias"].start + 2], -1.0, None, ALU.mult).then_inc(once("neg_bias"), 1)
            dve.wait_ge(ln_xT, 5)
            V.tensor_scalar(delta[:, 0:1], x[:, 0:1], -1.0, None, ALU.mult)
            step(V.tensor_tensor(delta[:, 1:N], x[:, 0:N - 1], x[:, 1:N], ALU.subtract))
            for i, name in enumerate(("x_r", "x_k", "x_v", "x_w", "x_a")):
                last = V.scalar_tensor_tensor(out=mix[:, i, :], in0=delta, scalar=col(name), in1=x, op0=ALU.mult, op1=ALU.add)
            last.then_inc(once("mixed"), 1)
            dve.wait_ge(once("rwkv_proj"), 1)
            V.tensor_copy(rkv, bank[0][:, 0:192].rearrange("p (m n) -> p m n", m=3)).then_inc(once("rkv_copied"), 1)
            dve.wait_ge(once("rkv_copied"), 1)
            r, k, v = (rkv[:, i, :] for i in range(3))
            step(V.tensor_scalar(kk, k, col("k_k"), None, ALU.mult))
            V.tensor_tensor(tmpA, kk, kk, ALU.mult).then_inc(once("kk_squared"), 1)

            def spread(i, name, vec):
                V.tensor_tensor(diag[:, i, :].rearrange("p (n j) -> p n j", j=D), vec.unsqueeze(2).broadcast_to([128, N, D]),
                                const("eye8").unsqueeze(1).broadcast_to([128, N, D]), ALU.mult).then_inc(once("spread_" + name), 1)

            spread(0, "r", r)
            dve.wait_ge(once("kk_sum"), 1)
            V.tensor_scalar(kk_ss, outb[0][:, 0:64], 1e-24, None, ALU.max).then_inc(once("kk_sq"), 1)
            dve.wait_ge(once("lora_exp"), 1)
            step(V.tensor_scalar(expo, expo, 1.0, None, ALU.add))
            step(V.reciprocal(sig, expo))
            step(V.tensor_scalar(sig[:, 0, :], sig[:, 0, :], float(np.exp(-0.5)), None, ALU.mult))
            spread(1, "w", sig[:, 0, :])
            a = sig[:, 1, :]
            step(V.tensor_scalar(kmix, a, -1.0, col("k_a"), ALU.add, ALU.mult))
            step(V.scalar_tensor_tensor(out=kmix, in0=kmix, scalar=1.0, in1=k, op0=ALU.add, op1=ALU.mult))
            spread(2, "k", kmix)
            dve.wait_ge(once("kk_pow"), 1)
            step(V.scalar_tensor_tensor(out=nkk, in0=kk, scalar=-1.0, in1=kk_inv, op0=ALU.mult, op1=ALU.mult))
            spread(3, "a", nkk)
            step(V.scalar_tensor_tensor(out=bvec, in0=nkk, scalar=-1.0, in1=a, op0=ALU.mult, op1=ALU.mult))
            spread(4, "b", bvec)
            V.scalar_tensor_tensor(out=tmpB, in0=r, scalar=col("r_k"), in1=kmix, op0=ALU.mult, op1=ALU.mult).then_inc(once("rkk"), 1)
            dve.wait_ge(once("g_exp"), 1)
            step(V.tensor_scalar(gexp, gexp, 1.0, None, ALU.add))
            V.reciprocal(gsig, gexp).then_inc(once("g_sig"), 1)
            V.memset(first[:, :, 0, :], 0.0)
            step(V.tensor_copy(first[:, :, 1, :], const("eye8").unsqueeze(1).broadcast_to([128, SEGS, D])))
            dve.wait_ge(once("along"), 3)
            step(V.tensor_tensor(vk.rearrange("p (n j) -> p n j", j=D), v.unsqueeze(2).broadcast_to([128, N, D]),
                                 along[:, 2, :].rearrange("p (n j) -> p n j", j=D), ALU.mult))
            dve.wait_ge(once("along"), 5)

            def at(vec, s, y=True):
                u = vec.rearrange("p (c s j) -> p s c j", c=SEGS, s=STEPS)[:, s, :, :]
                return u.unsqueeze(2).broadcast_to([128, SEGS, 2, D]) if y else u

            before = first
            for s in range(STEPS):
                after = states[:, s, :, :, :]
                V.tensor_tensor(prod2, before, at(along[:, 1, :], s), ALU.mult)
                step(V.tensor_tensor(prod, before, at(along[:, 3, :], s), ALU.mult))
                step(V.reduce_sum(sa, prod, AX.X))
                step(V.tensor_tensor(prod, sa.unsqueeze(3).broadcast_to([128, SEGS, 2, D]), at(along[:, 4, :], s), ALU.mult))
                step(V.tensor_tensor(after, prod, prod2, ALU.add))
                step(V.tensor_tensor(after[:, :, 0, :], after[:, :, 0, :], at(vk, s, False), ALU.add))
                before = after
            for kind, dst, c0 in ((0, bdU, 0), (1, bdP, 1)):
                m = SEGS - 1 - c0
                last = V.tensor_tensor(dst.rearrange("p c (h j) -> p c h j", h=H),
                                       states[:, STEPS - 1, c0:SEGS - 1, kind, :].unsqueeze(2).broadcast_to([128, m, H, D]),
                                       const("head").unsqueeze(1).unsqueeze(3).broadcast_to([128, m, H, D]), ALU.mult)
            last.then_inc(once("seg_blocks"), 1)
            for y in range(2):
                last = V.tensor_tensor(rd[:, y, :].rearrange("p (s c j) -> p s c j", s=STEPS, c=SEGS), states[:, :, :, y, :],
                                       along[:, 0, :].rearrange("p (c s j) -> p s c j", c=SEGS, s=STEPS), ALU.mult)
            step(last)
            V.reduce_sum(pread.rearrange("p y s c -> p (y s c)"), rd.rearrange("p y (n j) -> p (y n) j", j=D), AX.X).then_inc(once("reads_done"), 1)
            dve.wait_ge(once("reads_done"), 1)
            dve.wait_ge(once("seg_out"), 1)
            V.tensor_copy(oseq[:, 0:8], pread[:, 0, :, 0])
            V.tensor_tensor(oseq[:, 8:64].rearrange("p (c s) -> p c s", s=STEPS),
                            outb[0][:, 72:128].rearrange("p (c s) -> p c s", s=STEPS),
                            pread[:, 0, :, 1:SEGS].rearrange("p s c -> p c s"), ALU.add).then_inc(once("o_seq"), 1)
            dve.wait_ge(once("gn_sum"), 1)
            step(V.scalar_tensor_tensor(out=oseq, in0=outb[1][:, 192:256], scalar=-1.0 / D, in1=oseq, op0=ALU.mult, op1=ALU.add))
            step(V.tensor_tensor(bonus, outb[1][:, 128:192], v, ALU.mult))
            V.tensor_tensor(tmpA, oseq, oseq, ALU.mult).then_inc(once("gn_sq"), 1)
            dve.wait_ge(once("gn_sqsum"), 1)
            V.tensor_scalar(gn_v, outb[1][:, 256:320], 1.0 / D, 1e-5, ALU.mult, ALU.add).then_inc(once("gn_var"), 1)
            dve.wait_ge(once("gn_pow"), 1)
            step(V.tensor_tensor(onrm, oseq, gn_rstd, ALU.mult))
            step(V.tensor_scalar(onrm, onrm, col("gn_w"), col("gn_b"), ALU.mult, ALU.add))
            step(V.tensor_tensor(onrm, onrm, bonus, ALU.add))
            V.scalar_tensor_tensor(out=gated, in0=outb[1][:, 64:128], scalar=col("g_bias"), in1=onrm, op0=ALU.add,
                                   op1=ALU.mult).then_inc(once("gated"), 1)
            residual(5, biased=False)

            MAGIC = 1.5 * 2.0 ** 23

            def quantise(src, tmp, dst, at0):
                step(V.scalar_tensor_tensor(out=tmp, in0=src, scalar=-1.0, in1=src, op0=ALU.mult, op1=ALU.max))
                step(V.reduce_max(am[:, at0:at0 + 1], tmp, AX.X))
                step(V.tensor_scalar(am[:, at0:at0 + 1], am[:, at0:at0 + 1], 1e-5, None, ALU.max))
                V.tensor_scalar(am[:, at0 + 1:at0 + 2], am[:, at0:at0 + 1], 1.0 / 127.0, None, ALU.mult)
                step(V.reciprocal(am[:, at0 + 2:at0 + 3], am[:, at0:at0 + 1]))
                step(V.tensor_scalar(am[:, at0 + 2:at0 + 3], am[:, at0 + 2:at0 + 3], 127.0, None, ALU.mult))
                step(V.tensor_scalar(tmp, src, am[:, at0 + 2:at0 + 3], MAGIC, ALU.mult, ALU.add))
                step(V.tensor_scalar(tmp, tmp, MAGIC, 127.0, ALU.subtract, ALU.min))
                return V.tensor_scalar(dst, tmp, -128.0, None, ALU.max)

            norm(5)
            quantise(xn[:, :], absx, xint, 0).then_inc(once("x_int"), 1)
            dve.wait_ge(once("x_intT"), 1)
            V.tensor_copy(xiT, outb[0][:, 0:N]).then_inc(once("x_intTc"), 1)
            step(V.tensor_scalar(am[:, 6:8], wmean[0:N, 0:2], am[:, 1:2], None, ALU.mult))
            dve.wait_ge(once("gate_up"), 1)
            V.tensor_scalar(gate_, bank[0][0:N, :], am[:, 6:7], None, ALU.mult).then_inc(once("gate_scaled"), 1)
            dve.wait_ge(once("gate_scaled"), 1)
            step(V.scalar_tensor_tensor(out=up_, in0=bank[1][0:N, :], scalar=am[:, 7:8], in1=gate_, op0=ALU.mult, op1=ALU.mult))
            dve.wait_ge(once("gate_exp"), 1)
            step(V.tensor_scalar(den_, den_, 1.0, None, ALU.add))
            step(V.reciprocal(den_, den_))
            step(V.tensor_tensor(up_, up_, den_, ALU.mult))
            quantise(up_, gate_, hint, 3).then_inc(once("h_int"), 1)
            dve.wait_ge(once("h_intT"), 1)
            V.tensor_copy(hiT, outb[1][:, 0:256].rearrange("p (f n) -> p f n", f=FT)).then_inc(once("h_intTc"), 1)
            step(V.tensor_scalar(am[:, 6:7], wmean[0:N, 2:3], am[:, 4:5], None, ALU.mult))
            dve.wait_ge(y_proj, 6)
            V.scalar_tensor_tensor(out=xs[:, 6, :], in0=outb[0][0:N, 256:384], scalar=am[:, 6:7], in1=xs[:, 5, :],
                                   op0=ALU.mult, op1=ALU.add).then_inc(x_ready, 1)


def constants():
    f = np.zeros((128, N_CF), np.float32)
    p = np.arange(128)
    f[:, CF["ident"]] = np.eye(128)
    f[:, CF["group"]] = p[:, None] // D == p[None, :] // D
    r = np.arange(QK)
    f[:QK, CF["hmask"]] = (r[:, None] % 16) // D == p[None, :] // N
    for hh in range(2):
        for e in range(9):
            f[p % 32 == 9 * hh + e, CF["comb"].start + 9 * hh + e] = 1
    f[:, CF["head"]] = p[:, None] // D == np.arange(H)[None, :]
    f[:, CF["vmask"]] = p[:, None] // N == (p[None, :] // D) % 2
    theta = (1.0 / 10000.0 ** (np.arange(0, D, 2, dtype=np.float32) / D)).astype(np.float32)
    angle = np.outer(np.arange(N, dtype=np.float32), theta).astype(np.float32)
    angle = np.concatenate([angle, angle], axis=-1)
    f[:, CF["cos"]] = np.cos(angle).T[p % D]
    f[:, CF["sin"]] = np.sin(angle).T[p % D] * np.where(p % D < D // 2, -1, 1)[:, None]
    i = np.arange(H)
    f[:, CF["before"]] = (i[None, :] < i[:, None]).reshape(1, H * H)
    f[:, CF["eye8"]] = p[:, None] % D == np.arange(D)[None, :]
    b = np.zeros((128, N_CB), np.float32)
    b[:, CB["ident"]] = np.eye(128)
    b[:, CB["rep"]] = p[:, None] % N == p[None, :] % N
    b[:, CB["half"]] = 0.5 * (p[:, None] % N == p[None, :] % N)
    spread = np.zeros((128, 3, PAIRS, QK), np.float32)
    for j, part in enumerate(Q_PART):
        for h in range(PAIRS):
            for e in range(16):
                spread[16 * h + e, part, h, 16 * j + e] = 1
    b[:, CB["spread"]] = spread.reshape(128, -1)
    return f, b


def kernel(**inputs):
    import concourse.bacc as _bacc
    import ml_dtypes
    from concourse import mybir as _mybir
    from concourse.bass_utils import run_bass_kernel_spmd as _run

    v = {n: np.asarray(a) for n, a in inputs.items()}
    qkv = v["L0_attn_w_qkv"]
    turned = (np.arange(C) // D) * D + (np.arange(C) + D // 2) % D

    def pad(a):
        return np.concatenate([a, np.zeros((128 - a.shape[0], a.shape[1]), a.dtype)], axis=0)

    def by_rows(a):
        return a.reshape(FT, 128, C).transpose(1, 0, 2).reshape(128, FT * C)

    parts = {
        "aq": qkv[:, 0:C], "aqr": qkv[:, 0:C][:, turned], "ak": qkv[:, C:2 * C], "akr": qkv[:, C:2 * C][:, turned],
        "av": qkv[:, 2 * C:3 * C], "aout": v["L0_attn_w_out"], "router": v["L0_ffn_router_w"].T,
        "w1": v["L0_ffn_w1"].T, "w2": by_rows(v["L0_ffn_w2"].T), "W_r": v["L1_attn_W_r"], "W_k": v["L1_attn_W_k"],
        "W_v": v["L1_attn_W_v"], "W_o": v["L1_attn_W_o"], "wla": v["L1_attn_w_lora_a"], "wlb": pad(v["L1_attn_w_lora_b"]),
        "ala": v["L1_attn_a_lora_a"], "alb": pad(v["L1_attn_a_lora_b"]), "gla": v["L1_attn_g_lora_a"],
        "glb": v["L1_attn_g_lora_b"], "gate": v["L1_ffn_w_gate"].T, "up": v["L1_ffn_w_up"].T,
        "down": by_rows(v["L1_ffn_w_down"].T),
    }
    for L in range(2):
        for m in "qkvo":
            parts[f"W{m}{L}"] = v[f"L{L}_xattn_W{m}"].T
    columns = {
        "bk0": v["L0_xattn_bk"], "bq0": v["L0_xattn_bq"], "bk1": v["L1_xattn_bk"], "bq1": v["L1_xattn_bq"],
        "x_r": v["L1_attn_x_r"], "x_w": v["L1_attn_x_w"], "x_k": v["L1_attn_x_k"], "x_v": v["L1_attn_x_v"],
        "x_a": v["L1_attn_x_a"], "k_k": v["L1_attn_k_k"], "k_a": v["L1_attn_k_a"], "r_k": v["L1_attn_r_k"].reshape(C),
        "w_bias": v["L1_attn_w_lora_bias"], "a_bias": v["L1_attn_a_lora_bias"], "g_bias": v["L1_attn_g_lora_bias"],
        "gn_w": v["L1_attn_gn_weight"], "gn_b": v["L1_attn_gn_bias"],
    }
    columns = {n: a[:, None] for n, a in columns.items()}
    columns["b1"] = v["L0_ffn_b1"].reshape(FT, 128).T
    bias_rows = {"bv0": v["L0_xattn_bv"], "bo0": v["L0_xattn_bo"], "bv1": v["L1_xattn_bv"], "bo1": v["L1_xattn_bo"],
                 "b_out": v["L0_attn_b_out"], "b2": v["L0_ffn_b2"], "router_b": v["L0_ffn_router_b"]}
    cf, cb = constants()
    arrays = {
        "x": v["x"][0], "ctxT": v["ctx_1024"][0].T, "mask0": v["mask_BxSxS2_ff0"][0],
        "mask1": v["mask_SxS2_bk1"].view(np.int32),
        "weights": np.concatenate([parts[n] for n in WCOLS], axis=1),
        "columns": np.concatenate([columns[n] for n in COLS], axis=1),
        "rows": np.concatenate([bias_rows[n] for n in ROWS])[None, :],
        "tables": cf, "tables_bf16": cb.astype(ml_dtypes.bfloat16),
    }
    arrays = {n: np.ascontiguousarray(a) for n, a in arrays.items()}
    nc = _bacc.Bacc("TRN2", target_bir_lowering=False, num_devices=1)
    args = [nc.dram_tensor("in_" + n, a.shape, _mybir.dt.from_np(a.dtype), kind="ExternalInput").ap() for n, a in arrays.items()]
    out = nc.dram_tensor("out", (N, C), _mybir.dt.float32, kind="ExternalOutput").ap()
    program(nc, *args, out)
    r = _run(nc, [{"in_" + n: a for n, a in arrays.items()}], core_ids=[0])
    return r.results[0]["out"].reshape(1, N, C)
```

```python
import numpy as np
import concourse.bass as bass
from concourse import mybir
from contextlib import ExitStack

N, C, T = 64, 128, 6272
H, D = 16, 8
PAIRS = H // 2
TILES = T // 128
BCH, BT = 7, TILES // 7
BW = BT * 128
ACH = 14
AW = T // ACH
CUT = 6 * AW
CUT2 = 11 * AW
VG = (TILES + 3) // 4
UNITS = ACH + VG
INNER = 512
FT = INNER // 128
STEPS, SEGS = 8, N // 8
BIG = 1e30
SCALE = float(1.0 / np.sqrt(np.float32(D)))
Q_PART = [0, 1, 2, 0, 1, 0]
K_PART = [0, 0, 0, 1, 1, 2]
QK = len(Q_PART) * 2 * D
QKM = QK + 3

WCOLS = {}
def _lay(names, into, start=0):
    for n, w in names:
        into[n] = slice(start, start + w)
        start += w
    return start

W_EARLY = _lay([("Wk0", C), ("Wv0", C), ("Wq0", C), ("Wo0", C)], WCOLS)
W_ALL = _lay([("Wk1", C), ("Wv1", C), ("Wq1", C), ("Wo1", C), ("aq", C), ("aqr", C), ("ak", C), ("akr", C),
              ("av", C), ("aout", C), ("router", H), ("w1", INNER), ("w2", INNER), ("W_r", C), ("W_k", C),
              ("W_v", C), ("W_o", C), ("wla", 64), ("wlb", C), ("ala", 64), ("alb", C), ("gla", C),
              ("glb", C), ("gate", INNER), ("up", INNER), ("down", INNER)], WCOLS, W_EARLY)
COLS = {}
N_COLS = _lay([("bk0", 1), ("bq0", 1), ("bk1", 1), ("bq1", 1), ("b1", FT), ("x_r", 1), ("x_w", 1), ("x_k", 1),
               ("x_v", 1), ("x_a", 1), ("k_k", 1), ("k_a", 1), ("r_k", 1), ("w_bias", 1), ("a_bias", 1),
               ("g_bias", 1), ("gn_w", 1), ("gn_b", 1)], COLS)
ROWS = {}
N_ROWS = _lay([("bv0", C), ("bo0", C), ("bv1", C), ("bo1", C), ("b_out", C), ("b2", C), ("router_b", H)], ROWS)
CF = {}
N_CF = _lay([("ident", 128), ("group", 128), ("hmask", 128), ("comb", 18), ("head", H), ("vmask", 128),
             ("cos", N), ("sin", N), ("before", H * H), ("eye8", D)], CF)
CB = {}
N_CB = _lay([("ident", 128), ("rep", 128), ("half", 128), ("spread", 3 * PAIRS * QK)], CB)




def program(nc, x_d, ctx_d, mask0_d, mask1_d, w_d, cols_d, rows_d, cf_d, cb_d, out_d):
    fp32, bf16, u8, i32 = mybir.dt.float32, mybir.dt.bfloat16, mybir.dt.uint8, mybir.dt.int32
    ALU, ACT, AX = mybir.AluOpType, mybir.ActivationFunctionType, mybir.AxisListType

    ctx = ExitStack()
    with ctx:
        def sb(name, shape, dt=fp32):
            return ctx.enter_context(nc.sbuf_tensor(name, shape, dt))

        bank = [ctx.enter_context(nc.psum_tensor(f"bank{i}", [128, 512], fp32)) for i in range(2)]
        wide = [ctx.enter_context(nc.psum_tensor(f"wide{i}", [128, 1024], fp32)) for i in range(2)]
        outb = [ctx.enter_context(nc.psum_tensor(f"outb{i}", [128, 512], fp32)) for i in range(2)]

        w = sb("w", [128, W_ALL])
        cols = sb("cols", [128, N_COLS])
        rows = sb("rows", [N, N_ROWS])
        cf = sb("cf", [128, N_CF])
        cb = sb("cb", [128, N_CB], bf16)
        ctxT = sb("ctxT", [128, T])
        keys = [sb(f"keys{i}", [128, T], bf16) for i in range(2)]
        mask = sb("mask", [128, T])
        mask_hm = sb("mask_hm", [128, T], bf16)
        mask_lo = sb("mask_lo", [128, T], bf16)
        values = sb("values", [128, TILES, C])
        vpair = [sb(f"vpair{i}", [128, TILES, 32]) for i in range(2)]
        probs = [sb(f"probs{i}", [128, BW]) for i in range(2)]
        kfull = [sb(f"kfull{i}", [128, AW]) for i in range(2)]
        kparts = [sb(f"kparts{i}", [128, 3, AW], bf16) for i in range(2)]
        mrest = [sb(f"mrest{i}", [128, BW]) for i in range(2)]
        qstack = sb("qstack", [128, PAIRS, 128], bf16)
        qparts = sb("qparts", [128, 3, 2, N], bf16)
        outs = sb("outs", [128, PAIRS, 128])
        junk = sb("junk", [128, 2, AW], bf16)
        cmax = [sb(f"cmax{i}", [128, ACH]) for i in range(2)]
        pmax = sb("pmax", [128, PAIRS])
        mcol = [sb(f"mcol{i}", [128, QKM], bf16) for i in range(2)]
        mres = sb("mres", [128, 2])
        xs = sb("xs", [N, 7, C])
        xb = sb("xb", [N, C])
        xn = sb("xn", [N, C])
        xnT = sb("xnT", [C, 2, N])
        qT = sb("qT", [C, N])
        qres = sb("qres", [C, N])
        stat = sb("stat", [N, 16])
        mhalf = sb("mhalf", [128, N])
        o = sb("o", [N, C])
        oT = sb("oT", [C, N])
        rsum = sb("rsum", [N, H])
        place = {"mask": 0, "ctxT": 0, "values": 0}
        home = {"mask": mask[:, :], "ctxT": ctxT[:, :], "values": values[:, :, :].rearrange("p t c -> p (t c)")}

        def take(where, n, parts=128):
            a = place[where]
            place[where] = a + n
            return home[where][0:parts, a:a + n]

        wq = take("mask", 3 * INNER // 2).bitcast(bf16).rearrange("p (m f) -> p m f", m=3)
        wabs, wmean, winv, ones = take("mask", 3), take("mask", 3), take("mask", 3), take("mask", 128)
        wtmp = take("mask", 2 * INNER).rearrange("p (a f) -> p a f", a=2)
        more_parts = [take("mask", 3 * AW // 2).bitcast(bf16).rearrange("p (j t) -> p j t", j=3) for _ in range(2)]
        begin = place["mask"]
        qkrot = take("mask", 128).rearrange("p (a n) -> p a n", a=2)
        qksin = take("mask", 128).rearrange("p (a n) -> p a n", a=2)
        qrot = qkrot[:, 0, :]
        kbd = take("mask", H * N)
        prob = take("mask", PAIRS * N)
        smax, ssum = take("mask", PAIRS), take("mask", PAIRS)
        probT = take("mask", PAIRS * N).rearrange("p (j g n) -> p j g n", j=PAIRS // 2, g=2)
        v2 = take("mask", C)
        place["mask"] = begin
        logit, rank = take("mask", H, N), take("mask", H, N)
        over, even = take("mask", H * H, N), take("mask", H * H, N)
        fmask = take("mask", INNER // 2, N).bitcast(bf16)
        hpre, hT_ = take("mask", FT * N), take("mask", FT * N)
        hT = hT_.rearrange("p (f n) -> p f n", f=FT)
        place["mask"] = begin
        delta = take("mask", N)
        mix = take("mask", 5 * N).rearrange("p (m n) -> p m n", m=5)
        lmid = take("mask", 2 * N, 64).rearrange("p (m n) -> p m n", m=2)
        rkv = take("mask", 3 * N).rearrange("p (m n) -> p m n", m=3)
        sig = take("mask", 2 * N).rearrange("p (m n) -> p m n", m=2)
        expo = take("mask", 2 * N).rearrange("p (m n) -> p m n", m=2)
        nbias = take("mask", 2)
        gexp, gsig, kk, nkk, bvec, kmix, tmpA, tmpB = [take("mask", N) for _ in range(8)]
        oseq, gated, onrm, bonus = [take("mask", N) for _ in range(4)]
        head_sum, head_inv, head_wide = take("mask", H, N), take("mask", H, N), take("mask", C, N)
        sa = take("mask", SEGS * 2).rearrange("p (c y) -> p c y", c=SEGS)
        prod = take("mask", SEGS * 2 * D).rearrange("p (c y j) -> p c y j", c=SEGS, y=2)
        prod2 = take("mask", SEGS * 2 * D).rearrange("p (c y j) -> p c y j", c=SEGS, y=2)
        first = take("mask", SEGS * 2 * D).rearrange("p (c y j) -> p c y j", c=SEGS, y=2)
        diag = take("ctxT", 5 * N * D).rearrange("p (v n) -> p v n", v=5)
        bdU = take("ctxT", (SEGS - 1) * 128).rearrange("p (c n) -> p c n", n=128)
        bdP = take("ctxT", (SEGS - 2) * 128).rearrange("p (c n) -> p c n", n=128)
        carryT = take("ctxT", (SEGS - 1) * 128).rearrange("p (c n) -> p c n", n=128)
        along = take("values", 5 * N * D).rearrange("p (v n) -> p v n", v=5)
        vk = take("values", N * D)
        states = take("values", STEPS * SEGS * 2 * D).rearrange("p (s c y j) -> p s c y j", s=STEPS, c=SEGS, y=2)
        rd = take("values", 2 * N * D).rearrange("p (y n) -> p y n", y=2)
        pread = take("values", 2 * N).rearrange("p (y s c) -> p y s c", y=2, s=STEPS)
        xint, xclip = take("values", C, N), take("values", N)
        hclip = take("values", FT * N).rearrange("p (f n) -> p f n", f=FT)
        xiT = take("values", N // 2).bitcast(bf16)
        am = take("values", 9, N)
        place["ctxT"] = 0
        up_, den_, hint = [take("ctxT", INNER, N) for _ in range(3)]
        hiT = take("values", FT * N // 2).bitcast(bf16).rearrange("p (f n) -> p f n", f=FT)
        kscr = [nc.dram_tensor(f"key_parts{i}", [3, 128, T], bf16, kind="Internal").ap() for i in range(2)]

        def W(name):
            return w[:, WCOLS[name]]

        def col(name):
            return cols[:, COLS[name]]

        def row(name):
            return rows[:, ROWS[name]]

        def const(name, n=128):
            return cf[0:n, CF[name]]

        def constb(name, n=128):
            return cb[0:n, CB[name]]

        def sem(name):
            return ctx.enter_context(nc.semaphore(name))

        ld_first, ld_rest, ld_bf, ld_mask1, stored = map(sem, (
            "ld_first", "ld_rest", "ld_bf", "ld_mask1", "stored"))
        ld_mask = [sem(f"ld_mask0_{i}") for i in range(BCH)]
        ld_ctx = [sem(f"ld_ctx{i}") for i in range(4)]
        k_load = [[sem(f"k_load{s}_{h}") for h in range(2)] for s in range(2)]
        k_load_mid = sem("k_load_mid")
        k_store = [sem(f"k_store{i}") for i in range(6)]
        (ln_var, ln_rstd, ln_norm, ln_T, ln_xT, x_res, x_ready) = map(sem, (
            "ln_var", "ln_rstd", "ln_norm", "ln_T", "ln_xT", "x_res", "x_ready"))
        (q_proj, q_split, q_spread, q_stack, projd, evac, k_rest, k_mid, k_cut) = map(sem, (
            "q_proj", "q_split", "q_spread", "q_stack", "projd", "evac", "k_rest", "k_mid", "k_cut"))
        (a_scored, a_maxed, neg_max, neg_T, q_full, b_scored, exped, pv_done, vp_ready, o_saved) = map(sem, (
            "a_scored", "a_maxed", "neg_max", "neg_T", "q_full", "b_scored", "exped", "pv_done", "vp_ready",
            "o_saved"))
        (o_comb, o_norm, o_T, o_Tc, y_proj) = map(sem, ("o_comb", "o_norm", "o_T", "o_Tc", "y_proj"))
        (preset, m_high, m_rest, m_mid, m_parts, m1_ready) = map(sem, (
            "preset", "m_high", "m_rest", "m_mid", "m_parts", "m1_ready"))
        chain = {e: sem(f"{e}_chain") for e in ("dve", "act", "pool")}
        count = {e: 0 for e in chain}
        named = {}

        def once(name):
            if name not in named:
                named[name] = sem(name)
            return named[name]

        def link(which, eng, ins):
            count[which] += 1
            ins.then_inc(chain[which], 1)
            eng.wait_ge(chain[which], count[which])

        def pieces():
            return [(0, 4 * AW), (4 * AW, 8 * AW), (8 * AW, 12 * AW), (12 * AW, T)]

        def ctx_piece(c1):
            return (c1 - 1) // (4 * AW)

        def units(L):
            k, v = 0, 0
            for u in range(UNITS):
                if k < ACH and (L == 0 or u % 3 < 2):
                    yield "k", k
                    k += 1
                else:
                    yield "v", v
                    v += 1

        PLAN = [list(units(L)) for L in range(2)]
        RING = [6, 4]
        EARLY = 4
        BEFORE_A = 9
        MASKS_AFTER = [8, 10, 12, 13, 18, 23, 26, 26]
        MASK1_AFTER = [13, 15, 17, 20]

        ORDER = "wkabr"

        def along_bank(i):
            return bank[0][:, 0:512] if i == 4 else wide[i // 2][:, 512 * (i % 2):512 * (i % 2) + 512]

        def unit_bank(L, u):
            if L == 0:
                return wide[u % 4 // 2][:, 512 * (u % 2):512 * (u % 2) + 512]
            if u < EARLY:
                return bank[u % 2][:, :]
            return wide[1][:, 512 * (u % 2):512 * (u % 2) + 512]

        def key_ring(L, i):
            f, r = i % 4, i % RING[L]
            if f < 2:
                full = kfull[f][:, :]
            else:
                full = (probs if L == 0 else mrest)[f - 2][:, 0:AW]
            if r < 2:
                parts = kparts[r][:, :, :]
            elif L == 0:
                parts = keys[1][:, 3 * AW * (r - 2):3 * AW * (r - 1)].rearrange("p (j t) -> p j t", j=3)
            else:
                parts = more_parts[r - 2]
            return full, parts, k_store[r], 16 * (i // RING[L] + (stored_by(r, ACH) if L else 0))

        def stored_by(r, n):
            return len(range(r, n, RING[0]))

        pair_of_ones = float(np.array([0x3F803F80], np.uint32).view(np.float32)[0])
        block = ctx.enter_context(nc.Block())

        @block.sync
        def _(sp):
            def load_ctx(i):
                a, b = pieces()[i]
                sp.dma_start(ctxT[:, a:b], ctx_d[:, a:b]).then_inc(ld_ctx[i], 16)

            sp.dma_start(xs[:, 0, :], x_d).then_inc(ld_first, 16)
            sp.dma_start(w[:, 0:W_EARLY], w_d[:, 0:W_EARLY]).then_inc(ld_first, 16)
            sp.dma_start(cols[:, :], cols_d).then_inc(ld_first, 16)
            sp.dma_start(cf[:, :], cf_d).then_inc(ld_first, 16)
            for i in range(4):
                load_ctx(i)
            sp.dma_start(cb[:, :], cb_d).then_inc(ld_bf, 16)

            def load_mask(piece):
                a, b = BW * piece, BW * (piece + 1)
                for half in range(2):
                    sp.dma_start(mask[64 * half:64 * half + 64, a:b], mask0_d[:, a:b]).then_inc(ld_mask[piece], 16)

            def load_keys(L, p, piece, mid=False):
                g = PAIRS * L + p
                a, b = [(0, CUT), (CUT if p else CUT2, T)][piece]
                done = k_load[g % 2][piece]
                if mid:
                    a, b, done = CUT, CUT2, k_load_mid
                if g >= 2:
                    sp.wait_ge(b_scored, BCH * (g - 2) + (3 if piece == 0 else BCH))
                for part in range(3):
                    j, n = K_PART.index(part), K_PART.count(part)
                    sp.dma_start(keys[g % 2][16 * j:16 * (j + n), a:b],
                                 kscr[L][part, 16 * p:16 * p + 16, a:b].unsqueeze(0).broadcast_to([n, 16, b - a])
                                 ).then_inc(done, 16)

            def in_dram(L, n):
                for j in range(n - RING[L], n):
                    _, _, store, before = key_ring(L, j)
                    sp.wait_ge(store, before + 16)

            for L in range(2):
                for i in range(ACH):
                    if L == 1 and i == 2:
                        sp.wait_ge(x_ready, 1)
                        for half in range(2):
                            sp.dma_start(mask_lo[64 * half:64 * half + 64, 0:T // 2].bitcast(i32),
                                         mask1_d).then_inc(ld_mask1, 16)
                    _, parts, store, before = key_ring(L, i)
                    if (L, i) == (1, ACH - 1):
                        sp.wait_ge(once("k_last_cut"), 1)
                    else:
                        sp.wait_ge(k_cut, ACH * L + i + 1)
                    sp.dma_start(kscr[L][:, :, i * AW:(i + 1) * AW].rearrange("j p t -> p j t"),
                                 parts).then_inc(store, 16)
                    if L == 0 and i < BCH:
                        load_mask(i)
                    if i == CUT // AW + 2:
                        in_dram(L, CUT // AW)
                        load_keys(L, 0, 0)
                in_dram(L, CUT2 // AW)
                load_keys(L, 0, 0, mid=True)
                in_dram(L, ACH)
                for p in range(PAIRS):
                    for piece in range(2):
                        if (p, piece) != (0, 0):
                            load_keys(L, p, piece)
                    if L == 0 and p == 1:
                        sp.dma_start(rows[:, :], rows_d.broadcast_to([N, N_ROWS])).then_inc(ld_rest, 16)
                        sp.dma_start(w[:, W_EARLY:W_ALL], w_d[:, W_EARLY:W_ALL]).then_inc(ld_rest, 16)
            sp.wait_ge(x_ready, 6)
            sp.dma_start(out_d, xs[:, 6, :]).then_inc(stored, 16)
            sp.wait_ge(stored, 16)

        @block.gpsimd
        def _(pool):
            def fill(ap, value):
                link("pool", pool, pool.memset(ap, value))

            def ln_power(k):
                pool.wait_ge(ln_var, k + 1)
                pool.tensor_tensor(stat[:, 9:10], stat[:, 8:9], mhalf[0:N, 0:1], ALU.pow).then_inc(ln_rstd, 1)
                pool.wait_ge(ln_rstd, k + 1)

            def add_bias(k, name):
                pool.wait_ge(x_ready, k)
                if k == 0:
                    pool.wait_ge(ld_first, 64)
                    pool.wait_ge(ld_rest, 32)
                pool.tensor_tensor(xb[:, :], xs[:, k, :], row(name), ALU.add).then_inc(x_res, 1)
                pool.wait_ge(x_res, k + 1)

            fill(mhalf[:, :], -0.5)
            ln_power(0)
            for i in range(2):
                heads = vpair[i][:, :, 0:18].rearrange("p t (h e) -> p t h e", e=9)
                fill(vpair[i][:, :, 18:32], 0.0)
                fill(heads[:, :, :, 8:9], 1.0)
                fill(mcol[i][:, :], 0.0)
            fill(mask_lo[0:64, :].bitcast(fp32), 0.0)

            def mask_rest(c):
                s = slice(c * BW, (c + 1) * BW)
                pool.wait_ge(m_high, c + 1)
                pool.tensor_tensor(mrest[c % 2][64:128, :], mask[64:128, s], mask_hm[64:128, s],
                                   ALU.subtract).then_inc(m_rest, 1)
                pool.wait_ge(m_rest, c + 1)

            def pair_values(L, pairs):
                for p in pairs:
                    if (L, p) == (0, 1):
                        for r in range(2, RING[0]):
                            pool.wait_ge(k_store[r], 16 * stored_by(r, ACH))
                        pool.memset(keys[1][QK:QKM, :].bitcast(fp32), pair_of_ones).then_inc(preset, 1)
                        pool.wait_ge(preset, 1)
                    g = PAIRS * L + p
                    if p == 0:
                        pool.wait_ge(evac, UNITS * (L + 1))
                    if g >= 2:
                        pool.wait_ge(pv_done, BCH * (g - 1))
                    pool.tensor_copy(
                        vpair[g % 2][:, :, 0:18].rearrange("p t (h e) -> p t h e", e=9)[:, :, :, 0:8],
                        values[:, :, 16 * p:16 * p + 16].rearrange("p t (h e) -> p t h e", e=8)
                    ).then_inc(vp_ready, 1)
                    pool.wait_ge(vp_ready, g + 1)

            mask_rest(0)
            for c in range(BCH):
                s = slice(c * BW, (c + 1) * BW)
                if c + 1 < BCH:
                    mask_rest(c + 1)
                pool.wait_ge(m_mid, c + 1)
                pool.tensor_tensor(mask_lo[64:128, s], mrest[c % 2][64:128, :], mask_hm[64:128, s],
                                   ALU.subtract).then_inc(m_parts, 1)
                pool.wait_ge(m_parts, c + 1)
                if c == 4:
                    pair_values(0, range(1))
            def cut_keys(chunks):
                for i in chunks:
                    full, parts, store, before = key_ring(1, i)
                    pool.wait_ge(evac, UNITS + PLAN[1].index(("k", i)) + 1)
                    link("pool", pool, pool.tensor_tensor(parts[:, 1, :], full, parts[:, 0, :], ALU.subtract))
                    link("pool", pool, pool.tensor_tensor(full, full, parts[:, 0, :], ALU.subtract))
                    pool.tensor_tensor(parts[:, 2, :], full, parts[:, 1, :], ALU.subtract).then_inc(k_cut, 1)
                    pool.wait_ge(k_cut, ACH + i + 1)

            pair_values(0, range(1, PAIRS))
            cut_keys(range(0, 2))
            add_bias(0, "bo0")
            cut_keys(range(2, 3))
            ln_power(1)
            add_bias(1, "b_out")
            cut_keys(range(3, 9))
            ln_power(2)
            add_bias(2, "b2")
            cut_keys(range(9, 12))
            ln_power(3)
            cut_keys(range(12, ACH - 1))
            pair_values(1, range(PAIRS))
            add_bias(3, "bo1")
            ln_power(4)
            pool.wait_ge(once("kk_sq"), 1)
            pool.tensor_tensor(head_inv, head_sum, mhalf[0:N, 0:H], ALU.pow).then_inc(once("kk_pow"), 1)
            pool.wait_ge(once("kk_pow"), 1)
            pool.wait_ge(once("gn_var"), 1)
            pool.tensor_tensor(head_inv, head_sum, mhalf[0:N, 0:H], ALU.pow).then_inc(once("gn_pow"), 1)
            pool.wait_ge(once("gn_pow"), 1)
            ln_power(5)

        @block.tensor
        def _(pe):
            mm = nc.tensor.matmul
            ident = const("ident")

            def ln_transpose(k):
                pe.wait_ge(ln_norm, k + 1)
                nc.tensor.transpose(outb[0][:, 0:N], xn[:, :], ident[0:N, 0:N]).then_inc(ln_T, 1)

            def project(L, u):
                kind, i = PLAN[L][u]
                n = UNITS * L + u
                dst = unit_bank(L, u)
                if L == 0:
                    pe.wait_ge(ld_ctx[ctx_piece((i + 1) * AW if kind == "k" else min(T, 512 * (i + 1)))], 16)
                    if u >= 4:
                        pe.wait_ge(evac, n - 3)
                elif u >= 2:
                    pe.wait_ge(evac, n - 1)
                if kind == "k":
                    last = mm(dst[:, 0:AW], W(f"Wk{L}"), ctxT[:, i * AW:(i + 1) * AW], start=True, stop=True)
                else:
                    for t in range(4 * i, min(4 * i + 4, TILES)):
                        last = mm(dst[:, 128 * (t % 4):128 * (t % 4) + 128], ctxT[:, 128 * t:128 * t + 128],
                                  W(f"Wv{L}"), start=True, stop=True)
                last.then_inc(projd, 1)

            upto = [0, 0]

            def more(L, n):
                for u in range(upto[L], min(upto[L] + n, UNITS)):
                    if L == 1 and u == 0:
                        pe.wait_ge(ld_rest, 32)
                    if L == 1 and u < 2:
                        pe.wait_ge(a_maxed, ACH * PAIRS)
                    if L == 1 and u == EARLY:
                        pe.wait_ge(exped, BCH * PAIRS)
                    project(L, u)
                upto[L] = max(upto[L], min(upto[L] + n, UNITS))

            def queries(L):
                pe.wait_ge(ln_xT, 1 if L == 0 else 4)
                mm(outb[1][:, 0:N], W(f"Wq{L}"), xnT[:, 0, :], start=True, stop=True).then_inc(q_proj, 1)
                more(L, ACH if L == 0 else 2)
                pe.wait_ge(q_split, L + 1)
                pe.wait_ge(ld_bf, 16)
                spread = constb("spread").rearrange("p (i h r) -> p i h r", i=3, r=QK)
                for p in range(PAIRS):
                    for i in range(3):
                        last = mm(bank[p // 4][0:QK, 128 * (p % 4):128 * (p % 4) + 128], spread[:, i, p, :], qparts[:, i, :, :],
                                  start=(i == 0), stop=(i == 2))
                last.then_inc(q_spread, 1)
                more(L, UNITS - BEFORE_A - upto[0] if L == 0 else 0)

            def pass_a(L, p, a):
                g = PAIRS * L + p
                n = ACH * g + a
                if a == 0:
                    pe.wait_ge(k_load[p % 2][0], 48 * (g // 2 + 1))
                if a == CUT // AW and p == 0:
                    pe.wait_ge(k_load_mid, 48 * (L + 1))
                if a == (CUT if p else CUT2) // AW:
                    pe.wait_ge(k_load[p % 2][1], 48 * (g // 2 + 1))
                if n >= 2:
                    pe.wait_ge(a_maxed, n - 1)
                mm(bank[a % 2][:, 0:AW], qstack[0:QK, p, :], keys[p % 2][0:QK, a * AW:(a + 1) * AW],
                   start=True, stop=True).then_inc(a_scored, 1)

            def max_rows(L, p):
                g = PAIRS * L + p
                pe.wait_ge(neg_max, g + 1)
                if g >= 2:
                    pe.wait_ge(o_saved, g - 1)
                mm(outb[p % 2][0:QKM, 128:256], mcol[p % 2][:, :], constb("ident"),
                   start=True, stop=True).then_inc(neg_T, 1)

            def pass_b(L, p, c, tiles):
                g = PAIRS * L + p
                n = BCH * g + c
                if 0 in tiles:
                    if c == 0:
                        pe.wait_ge(q_full, g + 1)
                        if g == 1:
                            pe.wait_ge(preset, 1)
                        if p == 0:
                            pe.wait_ge(evac, UNITS * (L + 1))
                    if g == 0:
                        pe.wait_ge(m_parts, c + 1)
                    if n >= 2:
                        pe.wait_ge(exped, n - 1)
                for i in tiles:
                    t = slice(128 * (BT * c + i), 128 * (BT * c + i) + 128)
                    u = wide[n % 2][:, 128 * i:128 * i + 128]
                    mm(u, keys[p % 2][0:QKM, t], qstack[0:QKM, p, :], start=True, stop=False)
                    if L == 0:
                        mm(u, mask_hm[:, t], constb("rep"), start=False, stop=False)
                        last = mm(u, mask_lo[:, t], constb("rep"), start=False, stop=True)
                    else:
                        last = mm(u, mask_hm[:, t], constb("half"), start=False, stop=True)
                if BT - 1 in tiles:
                    last.then_inc(b_scored, 1)

            def weigh(L, p, c):
                g = PAIRS * L + p
                n = BCH * g + c
                if c == 0:
                    pe.wait_ge(vp_ready, g + 1)
                pe.wait_ge(exped, n + 1)
                for i in range(BT):
                    t = BT * c + i
                    q = 32 * (t % 4)
                    last = mm(outb[p % 2][q:q + 32, 0:128], vpair[p % 2][:, t, :],
                              probs[n % 2][:, 128 * i:128 * i + 128], start=(t < 4), stop=(t >= TILES - 4))
                last.then_inc(pv_done, 1)

            A_PLAN = [3, 3, 3, 3, 2, 0, 0]

            def attention(L):
                pe.wait_ge(q_stack, L + 1)
                if L == 1:
                    pe.wait_ge(m1_ready, 4)
                for a in range(ACH):
                    pass_a(L, 0, a)
                    more(L, 1)
                max_rows(L, 0)
                for p in range(PAIRS):
                    todo = iter(range(ACH) if p + 1 < PAIRS else ())

                    def next_a(wanted):
                        if wanted:
                            pass_a(L, p + 1, next(todo))

                    for c in range(BCH):
                        n = A_PLAN[c] if p + 1 < PAIRS else 0
                        next_a(n > 0)
                        pass_b(L, p, c, range(0, 4))
                        next_a(n > 1)
                        pass_b(L, p, c, range(4, BT))
                        next_a(n > 2)
                        if c == BCH - 1 and p + 1 < PAIRS:
                            max_rows(L, p + 1)
                        if c:
                            weigh(L, p, c - 1)
                        elif p:
                            weigh(L, p - 1, BCH - 1)
                        if L == 0 and p == PAIRS - 1 and c in (0, 2, 4, 6):
                            more(1, 1)
                weigh(L, PAIRS - 1, BCH - 1)

            def output(L):
                comb = const("comb").rearrange("p (h e) -> p h e", h=2)
                pe.wait_ge(o_saved, PAIRS * (L + 1))
                for h in range(H):
                    last = mm(outb[0][0:N, 9 * h:9 * h + 9], outs[:, h // 2, 64 * (h % 2):64 * (h % 2) + 64],
                              comb[:, h % 2, :], start=True, stop=True)
                last.then_inc(o_comb, 1)
                if L == 0:
                    more(1, 1)
                project_out(2 * L + 1, f"Wo{L}")

            def project_out(turn, name):
                pe.wait_ge(o_norm, turn)
                nc.tensor.transpose(outb[1][:, 0:N], o[:, :], ident[0:N, 0:N]).then_inc(o_T, 1)
                pe.wait_ge(o_Tc, turn)
                mm(outb[0][0:N, 256:384], oT[:, :], W(name), start=True, stop=True).then_inc(y_proj, 1)

            pe.wait_ge(ld_first, 64)
            ln_transpose(0)
            queries(0)
            attention(0)
            output(0)

            more(1, 2)
            ln_transpose(1)
            pe.wait_ge(ln_xT, 2)
            pe.wait_ge(evac, UNITS + EARLY)
            for i, name in enumerate(("aq", "aqr", "ak", "akr")):
                mm(bank[0][:, 64 * i:64 * i + 64], W(name), xnT[:, 0, :], start=True, stop=True)
            mm(bank[1][:, 0:128], xnT[:, :, :], W("av"), start=True, stop=True).then_inc(once("self_proj"), 1)
            more(1, 2)
            pe.wait_ge(once("self_kbd"), 1)
            for half in range(2):
                last = mm(wide[0][64 * half:64 * half + 64, 0:512], qrot, kbd[:, 512 * half:512 * half + 512],
                          start=True, stop=True)
            last.then_inc(once("self_scored"), 1)
            more(1, 5)
            pe.wait_ge(once("self_exp"), 1)
            for j in range(PAIRS // 2):
                last = nc.tensor.transpose(bank[0][:, 128 * j:128 * j + 128], prob[:, 128 * j:128 * j + 128], ident)
            last.then_inc(once("self_T"), 1)
            more(1, 1)
            pe.wait_ge(once("self_Tc"), 1)
            for p in range(PAIRS):
                last = mm(bank[1][0:N, 128 + 16 * p:144 + 16 * p], probT[:, p % 4, p // 4, :], v2[:, 16 * p:16 * p + 16],
                          start=True, stop=True)
            last.then_inc(once("self_out"), 1)
            project_out(2, "aout")

            more(1, 3)
            ln_transpose(2)
            pe.wait_ge(ln_xT, 3)
            mm(bank[0][0:N, 0:H], xnT[:, 0, :], W("router"), start=True, stop=True).then_inc(once("routed"), 1)
            for f in range(FT):
                last = mm(bank[1][:, 64 * f:64 * f + 64], w[:, WCOLS["w1"].start + 128 * f:WCOLS["w1"].start + 128 * f + 128],
                          xnT[:, 0, :], start=True, stop=True)
            last.then_inc(once("ff_h"), 1)
            more(1, 3)
            pe.wait_ge(once("ff_mask"), 1)
            for f in range(FT):
                last = mm(outb[1][:, 64 * f:64 * f + 64], fmask[:, 128 * f:128 * f + 128], constb("ident", N)[:, 0:N],
                          start=True, stop=True)
            last.then_inc(once("ff_maskT"), 1)
            pe.wait_ge(once("ff_relu"), 1)
            for f in range(FT):
                last = mm(outb[0][0:N, 256:384], hT[:, f, :], w[:, WCOLS["w2"].start + 128 * f:WCOLS["w2"].start + 128 * f + 128],
                          start=(f == 0), stop=(f == FT - 1))
            last.then_inc(y_proj, 1)

            more(1, 2)
            ln_transpose(3)
            queries(1)
            pe.wait_ge(once("w_abs"), 1)
            pe.wait_ge(once("ones"), 1)
            mm(outb[1][:, 0:3], ones, wabs, start=True, stop=True).then_inc(once("w_mean"), 1)
            attention(1)
            output(1)

            ln_transpose(4)
            pe.wait_ge(once("mixed"), 1)
            for i, name in enumerate(("W_r", "W_k", "W_v")):
                mm(bank[0][:, 64 * i:64 * i + 64], W(name), mix[:, i, :], start=True, stop=True)
            mm(bank[1][0:64, 0:64], W("wla"), mix[:, 3, :], start=True, stop=True)
            mm(bank[1][0:64, 64:128], W("ala"), mix[:, 4, :], start=True, stop=True).then_inc(once("rwkv_proj"), 1)
            pe.wait_ge(once("lora_mid"), 1)
            mm(bank[1][:, 128:192], w[0:64, WCOLS["wlb"]], lmid[:, 0, :], start=True, stop=True)
            mm(bank[1][:, 192:256], w[0:64, WCOLS["alb"]], lmid[:, 1, :], start=True, stop=True).then_inc(once("lora_out"), 1)
            pe.wait_ge(once("rkv_copied"), 1)
            mm(outb[1][:, 0:64], W("gla"), rkv[:, 0, :], start=True, stop=True).then_inc(once("g_mid"), 1)
            pe.wait_ge(once("kk_squared"), 1)
            mm(outb[0][0:N, 0:H], tmpA, const("head"), start=True, stop=True).then_inc(once("kk_sum"), 1)

            def over_rows(event):
                pe.wait_ge(once(event + "_spread"), 1)
                mm(outb[0][:, 64:128], head_wide, ident[0:N, 0:N],
                   start=True, stop=True).then_inc(once(event + "_inv"), 1)

            for name in ORDER:
                if name == "k":
                    over_rows("kk")
                pe.wait_ge(once("spread_" + name), 1)
                i = "rwkab".index(name)
                mm(along_bank(i), const("group"), diag[:, i, :], start=True, stop=True).then_inc(once("bc_" + name), 1)
            pe.wait_ge(once("g_sig"), 1)
            mm(outb[1][:, 64:128], W("glb"), gsig, start=True, stop=True).then_inc(once("g_out"), 1)
            pe.wait_ge(once("rkk"), 1)
            mm(outb[1][:, 128:192], const("group"), tmpB, start=True, stop=True).then_inc(once("bonus_sum"), 1)
            pe.wait_ge(once("seg_blocks"), 1)

            def carried_reads(c):
                return mm(outb[0][:, 64 + 8 * c:72 + 8 * c], carryT[:, c - 1, :], pread[:, 1, :, c], start=True, stop=True)

            for c in range(SEGS - 1):
                u = bank[c % 2][:, 0:128]
                if c >= 2:
                    pe.wait_ge(once("carry"), c - 1)
                last = mm(u, bdU[:, c, :], ident, start=True, stop=(c == 0))
                if c:
                    pe.wait_ge(once("carry"), c)
                    last = mm(u, bdP[:, c - 1, :], carryT[:, c - 1, :], start=False, stop=True)
                last.then_inc(once("carried"), 1)
                if c == 2:
                    pe.wait_ge(once("reads_done"), 1)
                if c >= 2:
                    carried_reads(c - 1)
            carried_reads(SEGS - 2)
            pe.wait_ge(once("carry"), SEGS - 1)
            carried_reads(SEGS - 1).then_inc(once("seg_out"), 1)
            pe.wait_ge(once("o_seq"), 1)
            mm(outb[1][:, 192:256], const("group"), oseq, start=True, stop=True).then_inc(once("gn_sum"), 1)
            pe.wait_ge(once("gn_sq"), 1)
            mm(outb[0][0:N, 0:H], tmpA, const("head"), start=True, stop=True).then_inc(once("gn_sqsum"), 1)
            over_rows("gn")
            pe.wait_ge(once("gated"), 1)
            mm(outb[0][0:N, 256:384], gated, W("W_o"), start=True, stop=True).then_inc(y_proj, 1)

            pe.wait_ge(once("x_int"), 1)
            nc.tensor.transpose(outb[0][:, 0:N], xint, ident[0:N, 0:N]).then_inc(once("x_intT"), 1)
            pe.wait_ge(once("x_intTc"), 1)
            pe.wait_ge(once("ternary"), 3)
            mm(bank[0][0:N, :], xiT, wq[:, 0, :], start=True, stop=True)
            mm(bank[1][0:N, :], xiT, wq[:, 1, :], start=True, stop=True).then_inc(once("gate_up"), 1)
            pe.wait_ge(once("h_int"), 1)
            for f in range(FT):
                last = nc.tensor.transpose(outb[1][:, 64 * f:64 * f + 64], hint[:, 128 * f:128 * f + 128], ident[0:N, 0:N])
            last.then_inc(once("h_intT"), 1)
            pe.wait_ge(once("h_intTc"), 1)
            for f in range(FT):
                last = mm(outb[0][0:N, 256:384], hiT[:, f, :], wq[:, 2, 128 * f:128 * f + 128],
                          start=(f == 0), stop=(f == FT - 1))
            last.then_inc(y_proj, 1)

        @block.scalar
        def _(act):
            A = nc.scalar.activation

            def evacuate(L, u):
                kind, i = PLAN[L][u]
                src = unit_bank(L, u)
                act.wait_ge(projd, UNITS * L + u + 1)
                if kind == "k":
                    full, parts, store, before = key_ring(L, i)
                    if i >= 4:
                        act.wait_ge(k_cut, ACH * L + i - 3)
                    if before:
                        act.wait_ge(store, before)
                    A(full, src[:, 0:AW], ACT.Identity, bias=col(f"bk{L}"))
                    A(parts[:, 0, :], src[:, 0:AW], ACT.Identity, bias=col(f"bk{L}")).then_inc(evac, 1)
                else:
                    if i == 0 and L == 1:
                        act.wait_ge(vp_ready, PAIRS)
                    m = min(4, TILES - 4 * i)
                    A(values[:, 4 * i:4 * i + m, :].rearrange("p t c -> p (t c)"), src[:, 0:128 * m],
                      ACT.Copy).then_inc(evac, 1)

            def mask_high(c):
                s = slice(c * BW, (c + 1) * BW)
                A(mask_hm[:, s], mask[:, s], ACT.Copy).then_inc(m_high, 1)

            def mask_middle(c):
                s = slice(c * BW, (c + 1) * BW)
                act.wait_ge(m_rest, c + 1)
                A(mask_hm[64:128, s], mrest[c % 2][64:128, :], ACT.Copy).then_inc(m_mid, 1)

            def exps(L):
                for n in range(BCH * PAIRS * L, BCH * PAIRS * (L + 1)):
                    act.wait_ge(b_scored, n + 1)
                    if n >= 2:
                        act.wait_ge(pv_done, n - 1)
                    A(probs[n % 2][:, :], wide[n % 2][:, 0:BW], ACT.Exp).then_inc(exped, 1)
                    late = n - BCH * (PAIRS - 1)
                    if L == 0 and late in (0, 2, 4, 6):
                        evacuate(1, late // 2)

            act.wait_ge(ld_first, 64)
            m = 0
            for u in range(UNITS):
                evacuate(0, u)
                for _ in range(MASKS_AFTER.count(u)):
                    if m < BCH:
                        act.wait_ge(ld_mask[m], 32)
                        mask_high(m)
                    if m:
                        mask_middle(m - 1)
                    m += 1
            exps(0)
            for u in range(EARLY, 12):
                evacuate(1, u)
            act.wait_ge(once("self_shift"), 1)
            A(prob, prob, ACT.Exp, scale=SCALE).then_inc(once("self_exp0"), 1)
            for u in range(12, 21):
                evacuate(1, u)
                if u in MASK1_AFTER:
                    i = MASK1_AFTER.index(u)
                    if i == 0:
                        act.wait_ge(ld_mask1, 32)
                        act.wait_ge(b_scored, BCH * PAIRS)
                    a, b = pieces()[i]
                    A(mask_hm[:, a:b], mask_lo[:, 0:T // 2].bitcast(u8)[:, a:b], ACT.Copy, scale=-BIG).then_inc(m1_ready, 1)
            act.wait_ge(ld_rest, 32)
            act.wait_ge(x_ready, 1)
            for i, name in enumerate(("gate", "up", "down")):
                last = A(wq[:, i, :], W(name), ACT.Abs, accum_out=wabs[:, i:i + 1])
            last.then_inc(once("w_abs"), 1)
            for u in range(21, UNITS):
                evacuate(1, u)
            exps(1)

            act.wait_ge(once("rwkv_proj"), 1)
            A(lmid[:, 0, :], bank[1][0:64, 0:64], ACT.Tanh)
            A(lmid[:, 1, :], bank[1][0:64, 64:128], ACT.Copy).then_inc(once("lora_mid"), 1)
            act.wait_ge(once("lora_out"), 1)
            act.wait_ge(once("neg_bias"), 1)
            for i in range(2):
                last = A(expo[:, i, :], bank[1][:, 128 + 64 * i:192 + 64 * i], ACT.Exp, scale=-1.0, bias=nbias[:, i:i + 1])
            last.then_inc(once("lora_exp"), 1)
            act.wait_ge(once("g_mid"), 1)
            A(gexp, outb[1][:, 0:64], ACT.Exp, scale=-1.0).then_inc(once("g_exp"), 1)
            for name in ORDER:
                i = "rwkab".index(name)
                act.wait_ge(once("bc_" + name), 1)
                A(along[:, i, :], along_bank(i), ACT.Copy).then_inc(once("along"), 1)
            act.wait_ge(once("gate_scale"), 1)
            act.wait_ge(once("gate_up"), 1)
            A(den_, bank[0][0:N, :], ACT.Exp, scale=am[:, 8:9]).then_inc(once("gate_exp"), 1)

        @block.vector
        def _(dve):
            V = nc.vector

            def step(ins):
                link("dve", dve, ins)

            def norm(k, double=False):
                x = xs[:, k, :]
                step(V.bn_stats(stat[:, 0:6], x))
                step(V.bn_aggr(stat[:, 6:8], stat[:, 0:6]))
                V.tensor_scalar_add(stat[:, 8:9], stat[:, 7:8], 1e-5).then_inc(ln_var, 1)
                dve.wait_ge(ln_rstd, k + 1)
                V.tensor_scalar(xn[:, :], x, stat[:, 6:7], stat[:, 9:10], ALU.subtract, ALU.mult).then_inc(ln_norm, 1)
                if k < 5:
                    dve.wait_ge(ln_T, k + 1)
                    V.tensor_copy(xnT[:, :, :], outb[0][:, 0:N].unsqueeze(1).broadcast_to([C, 2, N])).then_inc(ln_xT, 1)
                else:
                    dve.wait_ge(ln_norm, k + 1)

            def cut_keys(chunks):
                for i in chunks[::2]:
                    (full0, parts0), (full1, parts1) = key_ring(0, i)[0:2], key_ring(0, i + 1)[0:2]
                    dve.wait_ge(evac, PLAN[0].index(("k", i)) + 1)
                    V.tensor_tensor(full0, full0, parts0[:, 0, :], ALU.subtract).then_inc(k_rest, 1)
                    dve.wait_ge(evac, PLAN[0].index(("k", i + 1)) + 1)
                    V.tensor_tensor(full1, full1, parts1[:, 0, :], ALU.subtract).then_inc(k_rest, 1)
                    dve.wait_ge(k_rest, i + 1)
                    V.tensor_copy(parts0[:, 1, :], full0).then_inc(k_mid, 1)
                    dve.wait_ge(k_rest, i + 2)
                    V.tensor_copy(parts1[:, 1, :], full1).then_inc(k_mid, 1)
                    dve.wait_ge(k_mid, i + 1)
                    V.tensor_tensor(parts0[:, 2, :], full0, parts0[:, 1, :], ALU.subtract).then_inc(k_cut, 1)
                    dve.wait_ge(k_mid, i + 2)
                    V.tensor_tensor(parts1[:, 2, :], full1, parts1[:, 1, :], ALU.subtract).then_inc(k_cut, 1)

            def cut_last():
                full, parts, store, before = key_ring(1, ACH - 1)
                dve.wait_ge(evac, UNITS + PLAN[1].index(("k", ACH - 1)) + 1)
                step(V.tensor_tensor(full, full, parts[:, 0, :], ALU.subtract))
                step(V.tensor_copy(parts[:, 1, :], full))
                V.tensor_tensor(parts[:, 2, :], full, parts[:, 1, :], ALU.subtract).then_inc(once("k_last_cut"), 1)

            def queries(L):
                twice = lambda ap: ap.unsqueeze(1).broadcast_to([C, 2, N])
                dve.wait_ge(q_proj, L + 1)
                step(V.tensor_scalar(qT[:, :], outb[1][:, 0:N], col(f"bq{L}"), SCALE, ALU.add, ALU.mult))
                step(V.tensor_copy(qparts[:, 0, :, :], twice(qT[:, :])))
                step(V.tensor_tensor(qres[:, :], qT[:, :], qparts[:, 0, 0, :], ALU.subtract))
                step(V.tensor_copy(qparts[:, 1, :, :], twice(qres[:, :])))
                V.tensor_tensor(qparts[:, 2, :, :], twice(qres[:, :]), qparts[:, 1, :, :], ALU.subtract).then_inc(q_split, 1)

            def stack_queries(L):
                dve.wait_ge(q_spread, L + 1)
                for i in range(2):
                    last = V.tensor_tensor(qstack[0:QK, 4 * i:4 * i + 4, :],
                                           bank[i][0:QK, :].rearrange("p (h n) -> p h n", n=128),
                                           const("hmask", QK).unsqueeze(1).broadcast_to([QK, 4, 128]), ALU.mult)
                last.then_inc(q_stack, 1)

            def maxima(L, p, a):
                g = PAIRS * L + p
                n = ACH * g + a
                dve.wait_ge(a_scored, n + 1)
                if n >= 2:
                    dve.wait_ge(a_maxed, n - 1)
                if g == 0 and a % 2 == 0:
                    dve.wait_ge(ld_mask[a * AW // BW], 32)
                m = mask if L == 0 else mask_hm
                V.tensor_tensor_reduce(out=junk[:, a % 2, :], in0=bank[a % 2][:, 0:AW], in1=m[:, a * AW:(a + 1) * AW],
                                       scale=1.0, scalar=-3e38, op0=ALU.add, op1=ALU.max,
                                       accum_out=cmax[p % 2][:, a:a + 1]).then_inc(a_maxed, 1)

            def negate(L, p):
                g = PAIRS * L + p
                mc, mr = mcol[p % 2], mres[:, p % 2:p % 2 + 1]
                dve.wait_ge(a_maxed, ACH * (g + 1))
                step(V.reduce_max(pmax[:, p:p + 1], cmax[p % 2][:, :], AX.X))
                step(V.tensor_scalar(mc[:, QK:QK + 1], pmax[:, p:p + 1], -1.0, None, ALU.mult))
                step(V.scalar_tensor_tensor(out=mr, in0=pmax[:, p:p + 1], scalar=-1.0, in1=mc[:, QK:QK + 1],
                                            op0=ALU.mult, op1=ALU.subtract))
                step(V.tensor_copy(mc[:, QK + 1:QK + 2], mr))
                V.tensor_tensor(mc[:, QK + 2:QK + 3], mr, mc[:, QK + 1:QK + 2], ALU.subtract).then_inc(neg_max, 1)
                dve.wait_ge(neg_T, g + 1)
                V.tensor_copy(qstack[QK:QKM, p, :], outb[p % 2][QK:QKM, 128:256]).then_inc(q_full, 1)

            def ternary(i):
                name = ("gate", "up", "down")[i]
                V.tensor_scalar(wtmp[:, 0, :], W(name), winv[:, i:i + 1], 0.5, ALU.mult, ALU.is_gt)
                step(V.tensor_scalar(wtmp[:, 1, :], W(name), winv[:, i:i + 1], -0.5, ALU.mult, ALU.is_lt))
                V.tensor_tensor(wq[:, i, :], wtmp[:, 0, :], wtmp[:, 1, :], ALU.subtract).then_inc(once("ternary"), 1)

            def save(L, p):
                g = PAIRS * L + p
                dve.wait_ge(pv_done, BCH * (g + 1))
                V.tensor_copy(outs[:, p, :], outb[p % 2][:, 0:128]).then_inc(o_saved, 1)

            def attention(L):
                if L == 1:
                    dve.wait_ge(m1_ready, 4)
                for p in range(PAIRS):
                    for a in range(ACH):
                        maxima(L, p, a)
                        if a == 5 and p >= 2:
                            save(L, p - 2)
                        if L == 1 and a == 8 and 1 <= p <= 3:
                            ternary(p - 1)
                    negate(L, p)
                save(L, PAIRS - 2)
                if L == 1:
                    step(V.tensor_scalar(stat[:, 12:13], pmax[0:N, 0:1], -0.5 * BIG, 3e38, ALU.is_lt, ALU.mult))
                    step(V.tensor_scalar(stat[:, 13:14], stat[:, 12:13], 10.0, None, ALU.mult))
                    step(V.tensor_tensor(stat[:, 14:15], stat[:, 13:14], stat[:, 13:14], ALU.subtract))
                save(L, PAIRS - 1)

            def output(L):
                dve.wait_ge(o_comb, L + 1)
                heads = outb[0][0:N, 0:9 * H].rearrange("p (h e) -> p h e", e=9)
                o3 = o[:, :].rearrange("p (h e) -> p h e", e=D)
                step(V.reciprocal(rsum[:, :], heads[:, :, 8]))
                step(V.tensor_tensor(o3, heads[:, :, 0:8], rsum[:, :].unsqueeze(2).broadcast_to([N, H, D]), ALU.mult))
                if L == 1:
                    last = V.scalar_tensor_tensor(out=o[:, :], in0=o[:, :], scalar=stat[:, 14:15], in1=row("bv1"),
                                                  op0=ALU.add, op1=ALU.add)
                else:
                    last = V.tensor_tensor(o[:, :], o[:, :], row("bv0"), ALU.add)
                last.then_inc(o_norm, 1)
                copy_oT(2 * L + 1)

            def copy_oT(turn):
                dve.wait_ge(o_T, turn)
                V.tensor_copy(oT[:, :], outb[1][:, 0:N]).then_inc(o_Tc, 1)

            def residual(k, biased=True):
                dve.wait_ge(y_proj, k)
                if biased:
                    dve.wait_ge(x_res, k)
                V.tensor_tensor(xs[:, k, :], outb[0][0:N, 256:384], xb[:, :] if biased else xs[:, k - 1, :],
                                ALU.add).then_inc(x_ready, 1)
                dve.wait_ge(x_ready, k)

            V.memset(keys[0][QK:QKM, :].bitcast(fp32), pair_of_ones)
            dve.wait_ge(ld_first, 64)
            norm(0)
            queries(0)
            cut_keys(range(0, 10))
            stack_queries(0)
            cut_keys(range(10, ACH))
            attention(0)
            output(0)
            residual(1)

            norm(1)
            dve.wait_ge(once("self_proj"), 1)
            proj = bank[0][:, 0:256].rearrange("p (a r n) -> p a r n", a=2, r=2)
            turn2 = lambda name: const(name).unsqueeze(1).broadcast_to([128, 2, N])
            V.tensor_tensor(v2, bank[1][:, 0:128], const("vmask"), ALU.mult)
            V.tensor_tensor(qkrot, proj[:, :, 0, :], turn2("cos"), ALU.mult)
            step(V.tensor_tensor(qksin, proj[:, :, 1, :], turn2("sin"), ALU.mult))
            step(V.tensor_tensor(qkrot, qkrot, qksin, ALU.add))
            V.tensor_tensor(kbd.rearrange("p (h n) -> p h n", h=H), qkrot[:, 1, :].unsqueeze(1).broadcast_to([128, H, N]),
                            const("head").unsqueeze(2).broadcast_to([128, H, N]), ALU.mult).then_inc(once("self_kbd"), 1)
            dve.wait_ge(once("self_scored"), 1)
            s3 = wide[0][:, 0:512].rearrange("p (h n) -> p h n", h=PAIRS)
            p3 = prob.rearrange("p (h n) -> p h n", h=PAIRS)
            over_keys = lambda x: x.unsqueeze(2).broadcast_to([128, PAIRS, N])
            step(V.reduce_max(smax, s3, AX.X))
            V.tensor_tensor(p3, s3, over_keys(smax), ALU.subtract).then_inc(once("self_shift"), 1)
            dve.wait_ge(once("self_exp0"), 1)
            step(V.reduce_sum(ssum, p3, AX.X))
            step(V.reciprocal(ssum, ssum))
            V.tensor_tensor(p3, p3, over_keys(ssum), ALU.mult).then_inc(once("self_exp"), 1)
            dve.wait_ge(once("self_T"), 1)
            V.tensor_copy(probT.rearrange("p j g n -> p (j g n)"), bank[0][:, :]).then_inc(once("self_Tc"), 1)
            dve.wait_ge(once("self_out"), 1)
            V.tensor_copy(o[:, :], bank[1][0:N, 128:256]).then_inc(o_norm, 1)
            copy_oT(2)
            residual(2)

            norm(2)
            dve.wait_ge(once("routed"), 1)
            mine = logit.unsqueeze(2).broadcast_to([N, H, H])
            other = logit.unsqueeze(1).broadcast_to([N, H, H])
            over3, even3 = (x.rearrange("p (i j) -> p i j", i=H) for x in (over, even))
            step(V.tensor_tensor(logit, bank[0][0:N, 0:H], row("router_b"), ALU.add))
            V.tensor_tensor(over3, other, mine, ALU.is_gt)
            step(V.tensor_tensor(even3, other, mine, ALU.is_equal))
            step(V.tensor_tensor(even, even, const("before", N), ALU.mult))
            step(V.tensor_tensor(over, over, even, ALU.add))
            step(V.reduce_sum(rank, over3, AX.X))
            V.tensor_scalar(fmask.rearrange("p (i b) -> p i b", i=H), rank.unsqueeze(2).broadcast_to([N, H, INNER // H]),
                            3.5, None, ALU.is_lt).then_inc(once("ff_mask"), 1)
            dve.wait_ge(once("ff_h"), 1)
            step(V.tensor_tensor(hpre.rearrange("p (f n) -> p f n", f=FT),
                                 bank[1][:, 0:256].rearrange("p (f n) -> p f n", f=FT),
                                 col("b1").unsqueeze(2).broadcast_to([128, FT, N]), ALU.add))
            dve.wait_ge(once("ff_maskT"), 1)
            V.scalar_tensor_tensor(out=hT_, in0=hpre, scalar=0.0, in1=outb[1][:, 0:256], op0=ALU.max,
                                   op1=ALU.mult).then_inc(once("ff_relu"), 1)
            residual(3)

            V.memset(ones, 1.0).then_inc(once("ones"), 1)
            norm(3)
            queries(1)
            cut_last()
            stack_queries(1)
            dve.wait_ge(once("w_mean"), 1)
            step(V.tensor_scalar(wmean, outb[1][:, 0:3], 1.0 / (INNER * C), 1e-5, ALU.mult, ALU.max))
            step(V.reciprocal(winv, wmean))
            attention(1)
            output(1)
            residual(4)

            norm(4)
            x = xnT[:, 0, :]
            V.tensor_scalar(nbias, cols[:, COLS["w_bias"].start:COLS["w_bias"].start + 2], -1.0, None, ALU.mult).then_inc(once("neg_bias"), 1)
            dve.wait_ge(ln_xT, 5)
            V.tensor_scalar(delta[:, 0:1], x[:, 0:1], -1.0, None, ALU.mult)
            step(V.tensor_tensor(delta[:, 1:N], x[:, 0:N - 1], x[:, 1:N], ALU.subtract))
            for i, name in enumerate(("x_r", "x_k", "x_v", "x_w", "x_a")):
                last = V.scalar_tensor_tensor(out=mix[:, i, :], in0=delta, scalar=col(name), in1=x, op0=ALU.mult, op1=ALU.add)
            last.then_inc(once("mixed"), 1)
            dve.wait_ge(once("rwkv_proj"), 1)
            V.tensor_copy(rkv, bank[0][:, 0:192].rearrange("p (m n) -> p m n", m=3)).then_inc(once("rkv_copied"), 1)
            dve.wait_ge(once("rkv_copied"), 1)
            r, k, v = (rkv[:, i, :] for i in range(3))
            step(V.tensor_scalar(kk, k, col("k_k"), None, ALU.mult))
            V.tensor_tensor(tmpA, kk, kk, ALU.mult).then_inc(once("kk_squared"), 1)

            def spread(i, name, vec):
                V.tensor_tensor(diag[:, i, :].rearrange("p (n j) -> p n j", j=D), vec.unsqueeze(2).broadcast_to([128, N, D]),
                                const("eye8").unsqueeze(1).broadcast_to([128, N, D]), ALU.mult).then_inc(once("spread_" + name), 1)

            def widen(event):
                dve.wait_ge(once(event + "_pow"), 1)
                V.tensor_copy(head_wide.rearrange("p (h e) -> p h e", e=D),
                              head_inv.unsqueeze(2).broadcast_to([N, H, D])).then_inc(once(event + "_spread"), 1)
                dve.wait_ge(once(event + "_inv"), 1)

            spread(0, "r", r)
            dve.wait_ge(once("kk_sum"), 1)
            V.tensor_scalar(head_sum, outb[0][0:N, 0:H], 1e-24, None, ALU.max).then_inc(once("kk_sq"), 1)
            dve.wait_ge(once("lora_exp"), 1)
            step(V.tensor_scalar(expo, expo, 1.0, None, ALU.add))
            step(V.reciprocal(sig, expo))
            step(V.tensor_scalar(sig[:, 0, :], sig[:, 0, :], float(np.exp(-0.5)), None, ALU.mult))
            spread(1, "w", sig[:, 0, :])
            a = sig[:, 1, :]
            step(V.tensor_scalar(kmix, a, -1.0, col("k_a"), ALU.add, ALU.mult))
            step(V.scalar_tensor_tensor(out=kmix, in0=kmix, scalar=1.0, in1=k, op0=ALU.add, op1=ALU.mult))
            spread(2, "k", kmix)
            widen("kk")
            step(V.scalar_tensor_tensor(out=nkk, in0=kk, scalar=-1.0, in1=outb[0][:, 64:128], op0=ALU.mult, op1=ALU.mult))
            spread(3, "a", nkk)
            step(V.scalar_tensor_tensor(out=bvec, in0=nkk, scalar=-1.0, in1=a, op0=ALU.mult, op1=ALU.mult))
            spread(4, "b", bvec)
            V.scalar_tensor_tensor(out=tmpB, in0=r, scalar=col("r_k"), in1=kmix, op0=ALU.mult, op1=ALU.mult).then_inc(once("rkk"), 1)
            dve.wait_ge(once("g_exp"), 1)
            step(V.tensor_scalar(gexp, gexp, 1.0, None, ALU.add))
            V.reciprocal(gsig, gexp).then_inc(once("g_sig"), 1)
            V.memset(first[:, :, 0, :], 0.0)
            step(V.tensor_copy(first[:, :, 1, :], const("eye8").unsqueeze(1).broadcast_to([128, SEGS, D])))
            dve.wait_ge(once("along"), ORDER.index("k") + 1)
            step(V.tensor_tensor(vk.rearrange("p (n j) -> p n j", j=D), v.unsqueeze(2).broadcast_to([128, N, D]),
                                 along[:, 2, :].rearrange("p (n j) -> p n j", j=D), ALU.mult))
            dve.wait_ge(once("along"), ORDER.index("b") + 1)

            def at(vec, s, y=True):
                u = vec.rearrange("p (c s j) -> p s c j", c=SEGS, s=STEPS)[:, s, :, :]
                return u.unsqueeze(2).broadcast_to([128, SEGS, 2, D]) if y else u

            by_a, decayed, summed = once("by_a"), once("decayed"), once("summed")
            before = first
            for s in range(STEPS):
                after = states[:, s, :, :, :]
                V.tensor_tensor(prod, before, at(along[:, 3, :], s), ALU.mult).then_inc(by_a, 1)
                V.tensor_tensor(prod2, before, at(along[:, 1, :], s), ALU.mult).then_inc(decayed, 1)
                dve.wait_ge(by_a, s + 1)
                V.reduce_sum(sa, prod, AX.X).then_inc(summed, 1)
                dve.wait_ge(decayed, 2 * s + 1)
                V.tensor_tensor(prod2[:, :, 0, :], prod2[:, :, 0, :], at(vk, s, False), ALU.add).then_inc(decayed, 1)
                dve.wait_ge(summed, s + 1)
                step(V.tensor_tensor(prod, sa.unsqueeze(3).broadcast_to([128, SEGS, 2, D]), at(along[:, 4, :], s), ALU.mult))
                dve.wait_ge(decayed, 2 * s + 2)
                step(V.tensor_tensor(after, prod, prod2, ALU.add))
                before = after
            for kind, dst, c0 in ((0, bdU, 0), (1, bdP, 1)):
                m = SEGS - 1 - c0
                last = V.tensor_tensor(dst.rearrange("p c (h j) -> p c h j", h=H),
                                       states[:, STEPS - 1, c0:SEGS - 1, kind, :].unsqueeze(2).broadcast_to([128, m, H, D]),
                                       const("head").unsqueeze(1).unsqueeze(3).broadcast_to([128, m, H, D]), ALU.mult)
            last.then_inc(once("seg_blocks"), 1)
            dve.wait_ge(once("along"), len(ORDER))
            for y in (1, 0):
                step(V.tensor_tensor(rd[:, y, :].rearrange("p (s c j) -> p s c j", s=STEPS, c=SEGS), states[:, :, :, y, :],
                                     along[:, 0, :].rearrange("p (c s j) -> p s c j", c=SEGS, s=STEPS), ALU.mult))
                V.reduce_sum(pread[:, y, :, :].rearrange("p s c -> p (s c)"), rd[:, y, :].rearrange("p (n j) -> p n j", j=D),
                             AX.X).then_inc(once("reads_done"), 1)
            for c in range(SEGS - 1):
                dve.wait_ge(once("carried"), c + 1)
                V.tensor_copy(carryT[:, c, :], bank[c % 2][:, 0:128]).then_inc(once("carry"), 1)
            dve.wait_ge(once("reads_done"), 2)
            dve.wait_ge(once("seg_out"), 1)
            V.tensor_copy(oseq[:, 0:8], pread[:, 0, :, 0])
            V.tensor_tensor(oseq[:, 8:64].rearrange("p (c s) -> p c s", s=STEPS),
                            outb[0][:, 72:128].rearrange("p (c s) -> p c s", s=STEPS),
                            pread[:, 0, :, 1:SEGS].rearrange("p s c -> p c s"), ALU.add).then_inc(once("o_seq"), 1)
            dve.wait_ge(once("gn_sum"), 1)
            step(V.scalar_tensor_tensor(out=oseq, in0=outb[1][:, 192:256], scalar=-1.0 / D, in1=oseq, op0=ALU.mult, op1=ALU.add))
            step(V.tensor_tensor(bonus, outb[1][:, 128:192], v, ALU.mult))
            V.tensor_tensor(tmpA, oseq, oseq, ALU.mult).then_inc(once("gn_sq"), 1)
            dve.wait_ge(once("gn_sqsum"), 1)
            V.tensor_scalar(head_sum, outb[0][0:N, 0:H], 1.0 / D, 1e-5, ALU.mult, ALU.add).then_inc(once("gn_var"), 1)
            widen("gn")
            step(V.tensor_tensor(onrm, oseq, outb[0][:, 64:128], ALU.mult))
            step(V.tensor_scalar(onrm, onrm, col("gn_w"), col("gn_b"), ALU.mult, ALU.add))
            step(V.tensor_tensor(onrm, onrm, bonus, ALU.add))
            V.scalar_tensor_tensor(out=gated, in0=outb[1][:, 64:128], scalar=col("g_bias"), in1=onrm, op0=ALU.add,
                                   op1=ALU.mult).then_inc(once("gated"), 1)
            residual(5, biased=False)

            MAGIC = 1.5 * 2.0 ** 23

            def magnify(src, dst, at0):
                step(V.reduce_max(am[:, at0:at0 + 1], src, AX.X, apply_absolute_value=True))
                step(V.tensor_scalar(am[:, at0:at0 + 1], am[:, at0:at0 + 1], 1e-5, None, ALU.max))
                V.tensor_scalar(am[:, at0 + 1:at0 + 2], am[:, at0:at0 + 1], 1.0 / 127.0, None, ALU.mult)
                step(V.reciprocal(am[:, at0 + 2:at0 + 3], am[:, at0:at0 + 1]))
                step(V.tensor_scalar(am[:, at0 + 2:at0 + 3], am[:, at0 + 2:at0 + 3], 127.0, None, ALU.mult))
                return V.tensor_scalar(dst, src, am[:, at0 + 2:at0 + 3], MAGIC, ALU.mult, ALU.add)

            def integers(src, tmp, dst):
                step(V.tensor_scalar(tmp, src, MAGIC, 127.0, ALU.subtract, ALU.min))
                return V.tensor_scalar(dst, tmp, -128.0, None, ALU.max)

            norm(5)
            magnify(xn[:, :], xint, 0).then_inc(once("x_int"), 1)
            V.tensor_scalar(am[:, 8:9], wmean[0:N, 0:1], am[:, 1:2], -1.0, ALU.mult, ALU.mult)
            V.tensor_scalar(am[:, 6:8], wmean[0:N, 0:2], am[:, 1:2], None, ALU.mult).then_inc(once("gate_scale"), 1)
            dve.wait_ge(once("gate_scale"), 1)
            dve.wait_ge(once("x_intT"), 1)
            integers(outb[0][:, 0:N], xclip, xiT).then_inc(once("x_intTc"), 1)
            dve.wait_ge(once("gate_up"), 1)
            step(V.tensor_scalar(up_, bank[1][0:N, :], am[:, 7:8], None, ALU.mult))
            dve.wait_ge(once("gate_exp"), 1)
            V.scalar_tensor_tensor(out=up_, in0=bank[0][0:N, :], scalar=am[:, 6:7], in1=up_, op0=ALU.mult, op1=ALU.mult)
            step(V.tensor_scalar(den_, den_, 1.0, None, ALU.add))
            step(V.reciprocal(den_, den_))
            step(V.tensor_tensor(up_, up_, den_, ALU.mult))
            magnify(up_, hint, 3).then_inc(once("h_int"), 1)
            step(V.tensor_scalar(am[:, 6:7], wmean[0:N, 2:3], am[:, 4:5], None, ALU.mult))
            dve.wait_ge(once("h_intT"), 1)
            integers(outb[1][:, 0:256].rearrange("p (f n) -> p f n", f=FT), hclip, hiT).then_inc(once("h_intTc"), 1)
            dve.wait_ge(y_proj, 6)
            V.scalar_tensor_tensor(out=xs[:, 6, :], in0=outb[0][0:N, 256:384], scalar=am[:, 6:7], in1=xs[:, 5, :],
                                   op0=ALU.mult, op1=ALU.add).then_inc(x_ready, 1)


def constants():
    f = np.zeros((128, N_CF), np.float32)
    p = np.arange(128)
    f[:, CF["ident"]] = np.eye(128)
    f[:, CF["group"]] = p[:, None] // D == p[None, :] // D
    r = np.arange(QK)
    f[:QK, CF["hmask"]] = (r[:, None] % 16) // D == p[None, :] // N
    for hh in range(2):
        for e in range(9):
            f[p % 32 == 9 * hh + e, CF["comb"].start + 9 * hh + e] = 1
    f[:, CF["head"]] = p[:, None] // D == np.arange(H)[None, :]
    f[:, CF["vmask"]] = p[:, None] // N == (p[None, :] // D) % 2
    theta = (1.0 / 10000.0 ** (np.arange(0, D, 2, dtype=np.float32) / D)).astype(np.float32)
    angle = np.outer(np.arange(N, dtype=np.float32), theta).astype(np.float32)
    angle = np.concatenate([angle, angle], axis=-1)
    f[:, CF["cos"]] = np.cos(angle).T[p % D]
    f[:, CF["sin"]] = np.sin(angle).T[p % D] * np.where(p % D < D // 2, -1, 1)[:, None]
    i = np.arange(H)
    f[:, CF["before"]] = (i[None, :] < i[:, None]).reshape(1, H * H)
    f[:, CF["eye8"]] = p[:, None] % D == np.arange(D)[None, :]
    b = np.zeros((128, N_CB), np.float32)
    b[:, CB["ident"]] = np.eye(128)
    b[:, CB["rep"]] = p[:, None] % N == p[None, :] % N
    b[:, CB["half"]] = 0.5 * (p[:, None] % N == p[None, :] % N)
    spread = np.zeros((128, 3, PAIRS, QK), np.float32)
    for j, part in enumerate(Q_PART):
        for h in range(PAIRS):
            for e in range(16):
                spread[16 * h + e, part, h, 16 * j + e] = 1
    b[:, CB["spread"]] = spread.reshape(128, -1)
    return f, b


def kernel(**inputs):
    import concourse.bacc as _bacc
    import ml_dtypes
    from concourse import mybir as _mybir
    from concourse.bass_utils import run_bass_kernel_spmd as _run

    v = {n: np.asarray(a) for n, a in inputs.items()}
    qkv = v["L0_attn_w_qkv"]
    turned = (np.arange(C) // D) * D + (np.arange(C) + D // 2) % D

    def pad(a):
        return np.concatenate([a, np.zeros((128 - a.shape[0], a.shape[1]), a.dtype)], axis=0)

    def by_rows(a):
        return a.reshape(FT, 128, C).transpose(1, 0, 2).reshape(128, FT * C)

    parts = {
        "aq": qkv[:, 0:C], "aqr": qkv[:, 0:C][:, turned], "ak": qkv[:, C:2 * C], "akr": qkv[:, C:2 * C][:, turned],
        "av": qkv[:, 2 * C:3 * C], "aout": v["L0_attn_w_out"], "router": v["L0_ffn_router_w"].T,
        "w1": v["L0_ffn_w1"].T, "w2": by_rows(v["L0_ffn_w2"].T), "W_r": v["L1_attn_W_r"], "W_k": v["L1_attn_W_k"],
        "W_v": v["L1_attn_W_v"], "W_o": v["L1_attn_W_o"], "wla": v["L1_attn_w_lora_a"], "wlb": pad(v["L1_attn_w_lora_b"]),
        "ala": v["L1_attn_a_lora_a"], "alb": pad(v["L1_attn_a_lora_b"]), "gla": v["L1_attn_g_lora_a"],
        "glb": v["L1_attn_g_lora_b"], "gate": v["L1_ffn_w_gate"].T, "up": v["L1_ffn_w_up"].T,
        "down": by_rows(v["L1_ffn_w_down"].T),
    }
    for L in range(2):
        for m in "qkvo":
            parts[f"W{m}{L}"] = v[f"L{L}_xattn_W{m}"].T
    columns = {
        "bk0": v["L0_xattn_bk"], "bq0": v["L0_xattn_bq"], "bk1": v["L1_xattn_bk"], "bq1": v["L1_xattn_bq"],
        "x_r": v["L1_attn_x_r"], "x_w": v["L1_attn_x_w"], "x_k": v["L1_attn_x_k"], "x_v": v["L1_attn_x_v"],
        "x_a": v["L1_attn_x_a"], "k_k": v["L1_attn_k_k"], "k_a": v["L1_attn_k_a"], "r_k": v["L1_attn_r_k"].reshape(C),
        "w_bias": v["L1_attn_w_lora_bias"], "a_bias": v["L1_attn_a_lora_bias"], "g_bias": v["L1_attn_g_lora_bias"],
        "gn_w": v["L1_attn_gn_weight"], "gn_b": v["L1_attn_gn_bias"],
    }
    columns = {n: a[:, None] for n, a in columns.items()}
    columns["b1"] = v["L0_ffn_b1"].reshape(FT, 128).T
    bias_rows = {"bv0": v["L0_xattn_bv"], "bo0": v["L0_xattn_bo"], "bv1": v["L1_xattn_bv"], "bo1": v["L1_xattn_bo"],
                 "b_out": v["L0_attn_b_out"], "b2": v["L0_ffn_b2"], "router_b": v["L0_ffn_router_b"]}
    cf, cb = constants()
    arrays = {
        "x": v["x"][0], "ctxT": v["ctx_1024"][0].T, "mask0": v["mask_BxSxS2_ff0"][0],
        "mask1": v["mask_SxS2_bk1"].view(np.int32),
        "weights": np.concatenate([parts[n] for n in WCOLS], axis=1),
        "columns": np.concatenate([columns[n] for n in COLS], axis=1),
        "rows": np.concatenate([bias_rows[n] for n in ROWS])[None, :],
        "tables": cf, "tables_bf16": cb.astype(ml_dtypes.bfloat16),
    }
    arrays = {n: np.ascontiguousarray(a) for n, a in arrays.items()}
    nc = _bacc.Bacc("TRN2", target_bir_lowering=False, num_devices=1)
    args = [nc.dram_tensor("in_" + n, a.shape, _mybir.dt.from_np(a.dtype), kind="ExternalInput").ap() for n, a in arrays.items()]
    out = nc.dram_tensor("out", (N, C), _mybir.dt.float32, kind="ExternalOutput").ap()
    program(nc, *args, out)
    r = _run(nc, [{"in_" + n: a for n, a in arrays.items()}], core_ids=[0])
    return r.results[0]["out"].reshape(1, N, C)
```
